# Optimizing a Trainium2 kernel written in Bass

```python
import numpy as np
import jax
import jax.numpy as jnp

def _softmax(x, axis=-1):
    return jax.nn.softmax(x, axis=axis)

def _gelu(x):
    return jax.nn.gelu(x, approximate=True)

def _silu(x):
    return jax.nn.silu(x)

def _sigmoid(x):
    return jax.nn.sigmoid(x)

def _layernorm(x, axis=-1, eps=1e-05):
    m = jnp.mean(x, axis=axis, keepdims=True)
    v = jnp.var(x, axis=axis, keepdims=True)
    return (x - m) / jnp.sqrt(v + eps)

def _scatter_add(tgt, idx, src, axis=0):
    return tgt.at[idx].add(src)

def _segment_sum(src, seg, n):
    return jax.ops.segment_sum(src, seg, n)
kernel_name = 'mk_prb_d2_jaxref_r8_8ee8a2'

def setup_inputs(seed: int=0):
    np.random.seed(seed)
    _w = jnp.asarray

    def _L0_attn_setup():
        import jax, jax.numpy as jnp
        import numpy as np
        EMB = 128
        HEADS = 16
        ATT = EMB // HEADS
        key = jax.random.key(seed)
        ks = jax.random.split(key, 5)
        s = 1.0 / np.sqrt(EMB)
        return {'x': jax.random.normal(ks[0], (4, 256, EMB), dtype=jnp.float32), 'Wq': jax.random.uniform(ks[1], (EMB, HEADS * ATT), jnp.float32, -s, s), 'Wk': jax.random.uniform(ks[2], (EMB, HEADS * ATT), jnp.float32, -s, s), 'Wv': jax.random.uniform(ks[3], (EMB, HEADS * ATT), jnp.float32, -s, s), 'Wo': jax.random.uniform(ks[4], (HEADS * ATT, EMB), jnp.float32, -s, s)}
    _L0_attn_in = _L0_attn_setup()

    def _L0_ffn_setup():
        import jax, jax.numpy as jnp
        import numpy as np
        B, S, H = (2, 128, 128)
        DFF = 256
        E = 8
        TOPK = 2

        def _expert_ffn(x, w1, b1, w2, b2, wg, bg, w3, b3):
            x1 = jnp.einsum('bsh,hf->bsf', x, w1) + b1
            x2 = jnp.einsum('bsh,hf->bsf', x, w2) + b2
            z = x1 * x2
            s = jax.nn.silu(jnp.einsum('bsf,fg->bsg', z, wg) + bg)
            return jnp.einsum('bsg,gh->bsh', s, w3) + b3
        key = jax.random.key(seed)
        ks = jax.random.split(key, 12)
        sc = 0.02
        return {'x': jax.random.normal(ks[0], (B, S, H), jnp.float32), 'gate_w': jax.random.normal(ks[1], (H, E), jnp.float32) * sc, 'gate_b': jnp.zeros((E,), jnp.float32), 'w1': jax.random.normal(ks[2], (E, H, DFF), jnp.float32) * sc, 'b1': jnp.zeros((E, DFF), jnp.float32), 'w2': jax.random.normal(ks[3], (E, H, DFF), jnp.float32) * sc, 'b2': jnp.zeros((E, DFF), jnp.float32), 'wg': jax.random.normal(ks[4], (E, DFF, DFF), jnp.float32) * sc, 'bg': jnp.zeros((E, DFF), jnp.float32), 'w3': jax.random.normal(ks[5], (E, DFF, H), jnp.float32) * sc, 'b3': jnp.zeros((E, H), jnp.float32)}
    _L0_ffn_in = _L0_ffn_setup()

    def _L1_attn_setup():
        import jax, jax.numpy as jnp
        import numpy as np
        SEQ_LEN = 256
        DIM_EMB = 128
        DIM_K = 128
        DIM_V = 128
        BATCH = 4
        key = jax.random.key(seed)
        kx, kq, kk, kv, ko = jax.random.split(key, 5)
        s = DIM_EMB ** (-0.5)
        return {'x': jax.random.normal(kx, (BATCH, SEQ_LEN, DIM_EMB), dtype=jnp.float32), 'Wq': jax.random.normal(kq, (DIM_EMB, DIM_K), dtype=jnp.float32) * s, 'Wk': jax.random.normal(kk, (DIM_EMB, DIM_K), dtype=jnp.float32) * s, 'Wv': jax.random.normal(kv, (DIM_EMB, DIM_V), dtype=jnp.float32) * s, 'Wo': jax.random.normal(ko, (DIM_V, DIM_V), dtype=jnp.float32) * DIM_V ** (-0.5)}
    _L1_attn_in = _L1_attn_setup()

    def _L1_ffn_setup():
        import jax, jax.numpy as jnp
        import numpy as np
        from jax.scipy.linalg import expm
        B, S, D, E, K, NROT = (2, 256, 128, 8, 2, 3)
        DF = 4 * D
        EPS = 1e-05
        key = jax.random.key(seed)
        ks = jax.random.split(key, 8)
        s = lambda d: 1.0 / np.sqrt(d)
        return {'x': jax.random.normal(ks[0], (B, S, D), jnp.float32), 'ln_g': jnp.ones((D,), jnp.float32), 'ln_b': jnp.zeros((D,), jnp.float32), 'abel_w': jax.random.normal(ks[1], (D, D), jnp.float32) * s(D), 'abel_b': jnp.zeros((D,), jnp.float32), 'gate_w_moe': jax.random.normal(ks[2], (D, E), jnp.float32) * s(D), 'gate_b_moe': jnp.zeros((E,), jnp.float32), 'w1': jax.random.normal(ks[3], (E, D, DF), jnp.float32) * s(D), 'b1': jnp.zeros((E, DF), jnp.float32), 'w2': jax.random.normal(ks[4], (E, DF, D), jnp.float32) * s(DF), 'b2': jnp.zeros((E, D), jnp.float32), 'gens': jax.random.normal(ks[5], (NROT, D, D), jnp.float32) * 0.02, 'mix_w': jax.random.normal(ks[6], (2 * D, 1), jnp.float32) * s(2 * D), 'mix_b': jnp.zeros((1,), jnp.float32)}
    _L1_ffn_in = _L1_ffn_setup()
    _d = {'L0_attn_x': _L0_attn_in['x'], 'L0_attn_Wq': _L0_attn_in['Wq'], 'L0_attn_Wk': _L0_attn_in['Wk'], 'L0_attn_Wv': _L0_attn_in['Wv'], 'L0_attn_Wo': _L0_attn_in['Wo'], 'L0_ffn_gate_w': _L0_ffn_in['gate_w'], 'L0_ffn_gate_b': _L0_ffn_in['gate_b'], 'L0_ffn_w1': _L0_ffn_in['w1'], 'L0_ffn_b1': _L0_ffn_in['b1'], 'L0_ffn_w2': _L0_ffn_in['w2'], 'L0_ffn_b2': _L0_ffn_in['b2'], 'L0_ffn_wg': _L0_ffn_in['wg'], 'L0_ffn_bg': _L0_ffn_in['bg'], 'L0_ffn_w3': _L0_ffn_in['w3'], 'L0_ffn_b3': _L0_ffn_in['b3'], 'L1_attn_Wq': _L1_attn_in['Wq'], 'L1_attn_Wk': _L1_attn_in['Wk'], 'L1_attn_Wv': _L1_attn_in['Wv'], 'L1_attn_Wo': _L1_attn_in['Wo'], 'L1_ffn_ln_g': _L1_ffn_in['ln_g'], 'L1_ffn_ln_b': _L1_ffn_in['ln_b'], 'L1_ffn_abel_w': _L1_ffn_in['abel_w'], 'L1_ffn_abel_b': _L1_ffn_in['abel_b'], 'L1_ffn_gate_w_moe': _L1_ffn_in['gate_w_moe'], 'L1_ffn_gate_b_moe': _L1_ffn_in['gate_b_moe'], 'L1_ffn_w1': _L1_ffn_in['w1'], 'L1_ffn_b1': _L1_ffn_in['b1'], 'L1_ffn_w2': _L1_ffn_in['w2'], 'L1_ffn_b2': _L1_ffn_in['b2'], 'L1_ffn_gens': _L1_ffn_in['gens'], 'L1_ffn_mix_w': _L1_ffn_in['mix_w'], 'L1_ffn_mix_b': _L1_ffn_in['mix_b']}
    _x0 = _d['L0_attn_x']
    _d['L0_attn_x'] = jax.random.normal(jax.random.fold_in(jax.random.key(seed), 1), (4, 1024, 128), dtype=_x0.dtype)
    del _x0
    return _d

def reference(L0_attn_x, L0_attn_Wq, L0_attn_Wk, L0_attn_Wv, L0_attn_Wo, L0_ffn_gate_w, L0_ffn_gate_b, L0_ffn_w1, L0_ffn_b1, L0_ffn_w2, L0_ffn_b2, L0_ffn_wg, L0_ffn_bg, L0_ffn_w3, L0_ffn_b3, L1_attn_Wq, L1_attn_Wk, L1_attn_Wv, L1_attn_Wo, L1_ffn_ln_g, L1_ffn_ln_b, L1_ffn_abel_w, L1_ffn_abel_b, L1_ffn_gate_w_moe, L1_ffn_gate_b_moe, L1_ffn_w1, L1_ffn_b1, L1_ffn_w2, L1_ffn_b2, L1_ffn_gens, L1_ffn_mix_w, L1_ffn_mix_b):

    def _L0_attn_ref(x, Wq, Wk, Wv, Wo):
        import jax, jax.numpy as jnp
        import numpy as np
        EMB = 128
        HEADS = 16
        ATT = EMB // HEADS
        b, t, _ = x.shape
        h, d = (HEADS, ATT)
        scale = d ** (-0.25)
        q = (x @ Wq).reshape(b, t, h, d) * scale
        k = (x @ Wk).reshape(b, t, h, d) * scale
        v = (x @ Wv).reshape(b, t, h, d)
        dot = jnp.einsum('bqhd,bkhd->bhqk', q, k)
        causal = jnp.tril(jnp.ones((t, t), dtype=bool))
        dot = jnp.where(causal[None, None], dot, -jnp.inf)
        attn = jax.nn.softmax(dot, axis=-1)
        out = jnp.einsum('bhqk,bkhd->bqhd', attn, v).reshape(b, t, h * d)
        return out @ Wo

    def _L0_ffn_ref(x, gate_w, gate_b, w1, b1, w2, b2, wg, bg, w3, b3):
        import jax, jax.numpy as jnp
        import numpy as np
        B, S, H = (2, 128, 128)
        DFF = 256
        E = 8
        TOPK = 2

        def _expert_ffn(x, w1, b1, w2, b2, wg, bg, w3, b3):
            x1 = jnp.einsum('bsh,hf->bsf', x, w1) + b1
            x2 = jnp.einsum('bsh,hf->bsf', x, w2) + b2
            z = x1 * x2
            s = jax.nn.silu(jnp.einsum('bsf,fg->bsg', z, wg) + bg)
            return jnp.einsum('bsg,gh->bsh', s, w3) + b3
        logits = jnp.einsum('bsh,he->bse', x, gate_w) + gate_b
        topv, topi = jax.lax.top_k(logits, TOPK)
        probs = jax.nn.softmax(topv, axis=-1)
        out = jnp.zeros_like(x)
        for e in range(E):
            we = jnp.sum(probs * (topi == e), axis=-1)
            y = _expert_ffn(x, w1[e], b1[e], w2[e], b2[e], wg[e], bg[e], w3[e], b3[e])
            out = out + we[..., None] * y
        return out

    def _L1_attn_ref(x, Wq, Wk, Wv, Wo):
        import jax, jax.numpy as jnp
        import numpy as np
        SEQ_LEN = 256
        DIM_EMB = 128
        DIM_K = 128
        DIM_V = 128
        BATCH = 4
        q = jnp.einsum('bse,ek->bsk', x, Wq)
        k = jnp.einsum('bse,ek->bsk', x, Wk)
        v = jnp.einsum('bse,ev->bsv', x, Wv)
        scores = jnp.einsum('bqk,bsk->bqs', q, k)
        S = scores.shape[-1]
        causal_mask = jnp.triu(jnp.ones((S, S), dtype=bool), k=1)
        scores = jnp.where(causal_mask[None], -jnp.inf, scores)
        attn = jax.nn.softmax(scores * Wq.shape[1] ** (-0.5), axis=-1)
        out = jnp.einsum('bqs,bsv->bqv', attn, v)
        return jnp.einsum('bqv,vo->bqo', out, Wo)

    def _L1_ffn_ref(x, ln_g, ln_b, abel_w, abel_b, gate_w_moe, gate_b_moe, w1, b1, w2, b2, gens, mix_w, mix_b):
        import jax, jax.numpy as jnp
        import numpy as np
        from jax.scipy.linalg import expm
        B, S, D, E, K, NROT = (2, 256, 128, 8, 2, 3)
        DF = 4 * D
        EPS = 1e-05
        residual = x
        mu = jnp.mean(x, axis=-1, keepdims=True)
        var = jnp.mean((x - mu) ** 2, axis=-1, keepdims=True)
        xn = (x - mu) * jax.lax.rsqrt(var + EPS) * ln_g + ln_b
        abel = jax.nn.gelu(xn @ abel_w + abel_b, approximate=False)
        logits = xn @ gate_w_moe + gate_b_moe
        tw, ti = jax.lax.top_k(logits, K)
        tw = jax.nn.softmax(tw, axis=-1)
        onehot = (ti[..., None] == jnp.arange(E)).astype(tw.dtype)
        wdense = jnp.sum(tw[..., None] * onehot, axis=2)
        h = jax.nn.gelu(jnp.einsum('bsd,edf->besf', xn, w1) + b1[None, :, None, :], approximate=False)
        eo = jnp.einsum('besf,efd->besd', h, w2) + b2[None, :, None, :]
        moe = jnp.einsum('besd,bse->bsd', eo, wdense)
        rot = expm(gens[0])
        for i in range(1, NROT):
            rot = rot @ expm(gens[i])
        nonabel = moe @ rot
        combined = jnp.concatenate([abel, nonabel], axis=-1)
        g = jax.nn.sigmoid(combined @ mix_w + mix_b)
        return residual + abel * (1.0 - g) + nonabel * g
    x = L0_attn_x
    xn = _layernorm(x, axis=-1)
    x = x + _L0_attn_ref(xn, L0_attn_Wq, L0_attn_Wk, L0_attn_Wv, L0_attn_Wo) + _L0_ffn_ref(xn, L0_ffn_gate_w, L0_ffn_gate_b, L0_ffn_w1, L0_ffn_b1, L0_ffn_w2, L0_ffn_b2, L0_ffn_wg, L0_ffn_bg, L0_ffn_w3, L0_ffn_b3)
    xn = _layernorm(x, axis=-1)
    x = x + _L1_attn_ref(xn, L1_attn_Wq, L1_attn_Wk, L1_attn_Wv, L1_attn_Wo) + _L1_ffn_ref(xn, L1_ffn_ln_g, L1_ffn_ln_b, L1_ffn_abel_w, L1_ffn_abel_b, L1_ffn_gate_w_moe, L1_ffn_gate_b_moe, L1_ffn_w1, L1_ffn_b1, L1_ffn_w2, L1_ffn_b2, L1_ffn_gens, L1_ffn_mix_w, L1_ffn_mix_b)
    return x

_drawn_inputs = setup_inputs


def setup_inputs(seed=0):
    import zlib

    import numpy as np

    out = dict(_drawn_inputs(seed))
    spreads = {'L0_ffn_gate_b': (0.0, 0.1),
     'L0_ffn_b1': (0.0, 0.8),
     'L0_ffn_b2': (0.0, 0.8),
     'L0_ffn_bg': (0.0, 0.424),
     'L0_ffn_b3': (0.0, 0.498),
     'L1_ffn_ln_g': (1.0, 0.2),
     'L1_ffn_ln_b': (0.0, 0.433),
     'L1_ffn_abel_b': (0.0, 1.807),
     'L1_ffn_gate_b_moe': (0.0, 0.45),
     'L1_ffn_b1': (0.0, 1.369),
     'L1_ffn_b2': (0.0, 0.927)}
    factors = {'L0_attn_Wq': 3.07,
     'L0_attn_Wk': 2.952,
     'L0_ffn_w1': 8.0,
     'L0_ffn_w2': 8.0,
     'L0_ffn_wg': 8.0,
     'L0_ffn_w3': 3.104}
    for name, (base, spread) in spreads.items():
        noise = np.random.default_rng([zlib.crc32(name.encode()), seed]).standard_normal(out[name].shape)
        drawn = base * np.exp(spread * noise) if base else spread * noise
        out[name] = jnp.asarray(drawn.astype(out[name].dtype))
    for name, factor in factors.items():
        out[name] = (out[name] * factor).astype(out[name].dtype)
    return out
```

```python
from contextlib import ExitStack

import concourse.bass as bass
from concourse import mybir

F32 = mybir.dt.float32
BF16 = mybir.dt.bfloat16
U32 = mybir.dt.uint32
ALU = mybir.AluOpType
ACT = mybir.ActivationFunctionType
AX = mybir.AxisListType

P = 128
NEG = -1.0e30
EPS = 1e-5
TILE = 512
SQUARINGS = 7
DEGREE = 8


class Count:

    def __init__(self, eng, sem, start=0):
        self.eng, self.sem, self.start, self.n = eng, sem, start, 0

    def mark(self, ins):
        self.n += 1
        ins.then_inc(self.sem, 1)

    def settle(self):
        self.eng.wait_ge(self.sem, self.start + self.n)


def moments_of(dve, cnt, src, stats, moments, blocks, stats_written):
    for j in range(blocks):
        cnt.mark(dve.bn_stats(stats[:, j, :], src(j)))
    cnt.settle()
    dve.sem_inc(stats_written, 1)
    for j in range(blocks):
        cnt.mark(dve.bn_aggr(moments[:, j, :], stats[:, j, :]))
    cnt.settle()


def deviation(act, moments, dev, eps):
    return act.activation(dev[:], moments[:, :, 1], ACT.Sqrt, bias=eps[:, 0:1])


def scale_rows(dve, cnt, src, dst, moments, dev, rstd, blocks):
    cnt.mark(dve.reciprocal(rstd[:], dev[:]))
    cnt.settle()
    for j in range(blocks):
        cnt.mark(dve.tensor_scalar(dst(j), src(j), moments[:, j, 0:1], rstd[:, j:j + 1],
                                   ALU.subtract, ALU.mult))


def top2_weights(dve, cnt, logits, weights, hot, score, best, rank, order, n, n_exp):
    wide = [P, n, n_exp]
    bc = lambda ap: ap.unsqueeze(2).to_broadcast(wide)
    ranks = order.unsqueeze(1).to_broadcast(wide)
    for k in range(2):
        src = logits if k == 0 else weights
        cnt.mark(dve.tensor_reduce(best[:, k, :], src, AX.X, ALU.max))
        cnt.settle()
        cnt.mark(dve.tensor_tensor(score, src, bc(best[:, k, :]), ALU.is_equal))
        cnt.settle()
        cnt.mark(dve.tensor_tensor(score, score, ranks, ALU.mult))
        cnt.settle()
        cnt.mark(dve.tensor_reduce(rank, score, AX.X, ALU.max))
        cnt.settle()
        cnt.mark(dve.tensor_tensor(hot[:, k], score, bc(rank), ALU.is_equal))
        cnt.settle()
        if k == 0:
            cnt.mark(dve.scalar_tensor_tensor(weights, hot[:, 0], -3.0e38, logits, ALU.mult, ALU.add))
            cnt.settle()
    cnt.mark(dve.tensor_tensor(rank, best[:, 1, :], best[:, 0, :], ALU.subtract))


def top2_mix(dve, cnt, weights, hot, best, rank, n, n_exp):
    bc = lambda ap: ap.unsqueeze(2).to_broadcast([P, n, n_exp])
    cnt.mark(dve.tensor_scalar(best[:, 0, :], rank, 1.0, None, ALU.add))
    cnt.settle()
    cnt.mark(dve.reciprocal(best[:, 1, :], best[:, 0, :]))
    cnt.settle()
    cnt.mark(dve.tensor_tensor(best[:, 0, :], best[:, 1, :], rank, ALU.mult))
    cnt.mark(dve.tensor_tensor(hot[:, 0], hot[:, 0], bc(best[:, 1, :]), ALU.mult))
    cnt.settle()
    cnt.mark(dve.tensor_tensor(hot[:, 1], hot[:, 1], bc(best[:, 0, :]), ALU.mult))
    cnt.settle()
    cnt.mark(dve.tensor_tensor(weights, hot[:, 0], hot[:, 1], ALU.add))


def two_layers(nc, x, a0_wq, a0_wk, a0_wv, a0_wo, f0_gw, f0_gb, f0_w1, f0_b1, f0_w2, f0_b2, f0_wg, f0_bg,
               f0_w3, f0_b3, a1_wq, a1_wk, a1_wv, a1_wo, ln_g, ln_b, abel_w, abel_b, f1_gw, f1_gb,
               f1_w1, f1_b1, f1_w2, f1_b2, gens, mix_w, mix_b, out):
    BATCH, T, D = x.shape
    N_EXP, _, F0 = f0_w1.shape
    F1 = f1_w1.shape[2]
    HD = 8
    HEADS = D // HD
    GH = 4
    GROUPS = HEADS // GH
    N = BATCH * T
    NBLK, BLK = N // P, T // P
    NTILE = N // TILE
    NROT = gens.shape[0]
    assert D == P and HD * 9 + 24 == 96 and GH * HD == 32 and T == 2 * TILE

    dram = lambda name, shape, dt: nc.dram_tensor(name, shape, dt, kind="Internal").ap()
    qk_parts = dram("qk_parts", [2, BATCH * GROUPS, 3, HD, GH, T], BF16)
    v_padded = dram("v_padded", [BATCH, BLK, P, HEADS * 32], F32)
    gate_rows = [dram(f"gate_rows{i}", [N_EXP, N], F32) for i in range(2)]

    ctx = ExitStack()
    with ctx:
        sb = lambda name, shape, dt, c=ctx: c.enter_context(nc.sbuf_tensor(name, shape, dt))
        sem = lambda name, c=ctx: c.enter_context(nc.semaphore(name))
        ps = ctx.enter_context(nc.psum_tensor("ps", [P, 8, TILE], F32))

        X = sb("X", [P, NBLK, D], F32)
        XNT = sb("XNT", [P, N], F32)
        ATT = sb("ATT", [P, NBLK, D], F32)
        ACC = sb("ACC", [P, N], F32)
        ident = sb("ident", [P, P], F32)
        identb = sb("identb", [P, P], BF16)
        mask_q = sb("mask_q", [P, P], BF16)
        mask_k = sb("mask_k", [P, P], BF16)
        order = sb("order", [P, N_EXP], F32)
        logits = sb("logits", [P, NBLK, N_EXP], F32)
        weights = sb("weights", [P, NBLK, N_EXP], F32)
        hot = sb("hot", [P, 2, NBLK, N_EXP], F32)
        score = sb("score", [P, NBLK, N_EXP], F32)
        best = sb("best", [P, 2, NBLK], F32)
        rank = sb("rank", [P, NBLK], F32)
        gate_t = sb("gate_t", [P, 2, P], F32)
        W_names = ["wq0", "wk0", "wv0", "wo0", "wq1", "wk1", "wv1", "wo1", "abw"]
        W_src = [a0_wq, a0_wk, a0_wv, a0_wo, a1_wq, a1_wk, a1_wv, a1_wo, abel_w]
        W = {n: sb(n, [P, D], F32) for n in W_names}
        gw = [sb(f"gw{i}", [P, N_EXP], F32) for i in range(2)]
        gb = [sb(f"gb{i}", [P, N_EXP], F32) for i in range(2)]
        FF0, FF1 = F0 // P, F1 // P
        PER0, PER1 = 3 * FF0 + 1, FF1 + 1
        FIRST1 = N_EXP * PER0
        OTHERS = {n: FIRST1 + N_EXP * PER1 + i for i, n in enumerate(("ln_g", "ln_b", "abel_b", "mix_a", "mix_b"))}
        NVEC = max(OTHERS.values()) + 1
        vecs = sb("vecs", [P, NVEC], F32)

        def vec(name):
            return vecs[:, OTHERS[name]:OTHERS[name] + 1]

        mixb = sb("mixb", [P, 1], F32)
        rot = sb("rot", [P, D], F32)
        eps = sb("eps", [P, 1], F32)
        x_in = sem("x_in")

        x_blocks = x.rearrange("b (j p) d -> b p j d", p=P)

        with ExitStack() as c:
            E = sb("E", [P, 2, NROT, D], F32, c)
            vec_rows = sb("vec_rows", [NVEC, P], F32, c)
            A = sb("A", [P, 2, NROT, D], F32, c)
            small_in, pool_steps, gens_in, pe_round, dve_round = (
                sem(n, c) for n in ("small_in", "pool_steps", "gens_in", "pe_round", "dve_round"))
            block = c.enter_context(nc.Block())

            small = [(W[n][:], s) for n, s in zip(W_names, W_src)]
            small += [(gw[0][:], f0_gw), (gw[1][:], f1_gw)]
            small += [(gb[0][:], f0_gb.partition_broadcast(P)), (gb[1][:], f1_gb.partition_broadcast(P))]
            small += [(mixb[:], mix_b.partition_broadcast(P))]
            for at, per, srcs in ((0, PER0, (f0_b1, f0_b2, f0_bg, f0_b3)), (FIRST1, PER1, (f1_b1, f1_b2))):
                for src in srcs:
                    for f in range(src.shape[1] // P):
                        small.append((vec_rows[bass.DynSlice(at, N_EXP, per), :], src[:, f * P:(f + 1) * P]))
                        at += 1
            for name, src in (("ln_g", ln_g), ("ln_b", ln_b), ("abel_b", abel_b)):
                small.append((vec_rows[OTHERS[name]:OTHERS[name] + 1, :], src.unsqueeze(0)))
            small.append((vec_rows[OTHERS["mix_a"]:OTHERS["mix_a"] + 2, :], mix_w.rearrange("(a p) o -> a (p o)", p=P)))

            @block.sync
            def _(sp):
                for b in range(BATCH):
                    sp.dma_start(X[:, b * BLK:(b + 1) * BLK, :], x_blocks[b]).then_inc(x_in, 16)
                for dst, src in small[0::2]:
                    sp.dma_start(dst, src).then_inc(small_in, 16)
                sp.wait_ge(small_in, 16 * len(small))

            @block.scalar
            def _(act):
                act.dma_start(E[:, 0], gens.rearrange("g p d -> p g d")).then_inc(gens_in, 16)
                for dst, src in small[1::2]:
                    act.dma_start(dst, src).then_inc(small_in, 16)

            @block.gpsimd
            def _(pool):
                cnt = Count(pool, pool_steps)
                cnt.mark(pool.memset(ident[:], 1.0))
                cnt.mark(pool.memset(mask_q[:], 0.0))
                cnt.mark(pool.memset(mask_k[:], 0.0))
                cnt.mark(pool.memset(eps[:], EPS))
                for e in range(N_EXP):
                    cnt.mark(pool.memset(order[:, e:e + 1], float(N_EXP - e)))
                cnt.settle()
                cnt.mark(pool.affine_select(ident[:], ident[:], [[-1, P]], ALU.is_equal, 0.0, 0, 1))
                cnt.mark(pool.affine_select(mask_q[:], mask_q[:], [[-1, P]], ALU.is_ge, NEG, 0, 1))
                cnt.mark(pool.affine_select(mask_k[:], mask_k[:], [[1, P]], ALU.is_ge, NEG, 0, -1))
                cnt.settle()
                cnt.mark(pool.tensor_copy(identb[:], ident[:]))
                cnt.settle()

            POOL_READY = 4 + N_EXP + 3

            @block.tensor
            def _(pe):
                pe.wait_ge(pool_steps, POOL_READY)
                pe.wait_ge(dve_round, 1)
                for i in range(NROT):
                    m = pe.transpose(ps[:, 0, i * D:(i + 1) * D], A[:, 0, i, :], ident[:])
                m.then_inc(pe_round, 1)
                for k in range(DEGREE - 1):
                    pe.wait_ge(dve_round, 2 + k)
                    for i in range(NROT):
                        m = pe.matmul(ps[:, 0, i * D:(i + 1) * D], A[:, 1, i, :], E[:, 0, i, :],
                                      start=True, stop=True)
                    m.then_inc(pe_round, 1)
                pe.wait_ge(dve_round, DEGREE + 1)
                for i in range(NROT):
                    m = pe.transpose(ps[:, 1, i * D:(i + 1) * D], E[:, 0, i, :], ident[:])
                m.then_inc(pe_round, 1)
                for k in range(SQUARINGS):
                    pe.wait_ge(dve_round, DEGREE + 2 + k)
                    for i in range(NROT):
                        pe.matmul(ps[:, 0, i * D:(i + 1) * D], E[:, 1, i, :], E[:, 0, i, :],
                                  start=True, stop=True)
                    for i in range(NROT):
                        m = pe.matmul(ps[:, 1, i * D:(i + 1) * D], E[:, 0, i, :], E[:, 1, i, :],
                                      start=True, stop=True)
                    m.then_inc(pe_round, 1)
                for i in range(1, NROT):
                    pe.wait_ge(dve_round, DEGREE + 3 + SQUARINGS + i - 1)
                    pe.matmul(ps[:, 0, 0:D], E[:, 1, 0, :], E[:, 0, i, :], start=True, stop=True)
                    m = pe.matmul(ps[:, 1, 0:D], E[:, 0, i, :], E[:, 1, 0, :], start=True, stop=True)
                    m.then_inc(pe_round, 1)
                pe.wait_ge(small_in, 16 * len(small))
                pe.transpose(ps[:, 2, 0:NVEC], vec_rows[:], ident[0:NVEC, 0:NVEC]).then_inc(pe_round, 1)

            @block.vector
            def _(dve):
                pair = lambda k: ps[:, k, 0:NROT * D].rearrange("p (g d) -> p g d", g=NROT)
                idents = ident[:].unsqueeze(1).to_broadcast([P, NROT, D])
                cnt = Count(dve, dve_round)
                rounds = 0

                def pe_done():
                    dve.wait_ge(pe_round, rounds)

                dve.wait_ge(gens_in, 16)
                cnt.mark(dve.tensor_scalar(A[:, 0], E[:, 0], 2.0 ** -SQUARINGS, None, ALU.mult))
                dve.wait_ge(pool_steps, POOL_READY)
                cnt.settle()
                rounds += 1
                pe_done()
                dve.tensor_copy(A[:, 1], pair(0))
                cnt.mark(dve.scalar_tensor_tensor(E[:, 0], A[:, 0], 1.0 / DEGREE, idents, ALU.mult, ALU.add))
                for k in range(DEGREE - 1, 0, -1):
                    rounds += 1
                    pe_done()
                    if k > 1:
                        cnt.mark(dve.scalar_tensor_tensor(E[:, 0], pair(0), 1.0 / k, idents, ALU.mult, ALU.add))
                    else:
                        cnt.mark(dve.tensor_copy(E[:, 0], pair(0)))
                rounds += 1
                pe_done()
                cnt.mark(dve.tensor_copy(E[:, 1], pair(1)))
                cnt.settle()
                for k in range(SQUARINGS):
                    rounds += 1
                    pe_done()
                    dve.scalar_tensor_tensor(E[:, 0], E[:, 0], 2.0, pair(0), ALU.mult, ALU.add)
                    cnt.mark(dve.scalar_tensor_tensor(E[:, 1], E[:, 1], 2.0, pair(1), ALU.mult, ALU.add))
                    cnt.settle()
                dve.tensor_tensor(E[:, 0], E[:, 0], idents, ALU.add)
                cnt.mark(dve.tensor_tensor(E[:, 1], E[:, 1], idents, ALU.add))
                cnt.settle()
                for i in range(1, NROT):
                    rounds += 1
                    pe_done()
                    dve.tensor_copy(E[:, 0, 0, :], ps[:, 0, 0:D])
                    cnt.mark(dve.tensor_copy(E[:, 1, 0, :], ps[:, 1, 0:D]))
                    cnt.settle()
                dve.tensor_copy(rot[:], E[:, 0, 0, :])
                rounds += 1
                pe_done()
                dve.tensor_copy(vecs[:], ps[:, 2, 0:NVEC])

        with ExitStack() as c:
            xn = sb("xn", [P, BLK, D], F32, c)
            xnt = sb("xnt", [P, T], F32, c)
            qkf = sb("qkf", [P, 2, T], F32, c)
            rest = sb("rest", [P, 2, T], F32, c)
            parts = sb("parts", [P, 3, 2, T], BF16, c)
            vpad = sb("vpad", [P, BLK, HEADS, 32], F32, c)
            stats = sb("stats", [P, BLK, 6], F32, c)
            moments = sb("moments", [P, BLK, 2], F32, c)
            rstd = sb("rstd", [P, BLK], F32, c)
            dev = sb("dev", [P, BLK], F32, c)
            (dve_steps, xn_ready, xt_banks, xnt_ready, xnt_copied, v_ready, qk_banks, qk_ready, qkf_free, v_banks,
             g_bank, v_evac, parts_ready, parts_stored, v_stored, vpad_set, g_ready, moments_ready, dev_ready) = (sem(n, c) for n in (
                 "dve_steps", "xn_ready", "xt_banks", "xnt_ready", "xnt_copied", "v_ready", "qk_banks", "qk_ready",
                 "qkf_free", "v_banks", "g_bank", "v_evac", "parts_ready", "parts_stored", "v_stored",
                 "vpad_set", "g_ready", "moments_ready", "dev_ready"))
            stats_written = sem("stats_written", c)
            block = c.enter_context(nc.Block())
            HALF = BLK // 2
            STORES = 2 * 3 * GROUPS
            DVE_STEPS = 3 * BLK + 2 + 3

            @block.sync
            def _(sp):
                with sp.Fori(0, BATCH) as b:
                    sp.wait_ge(parts_ready, b + 1)
                    for qk in range(2):
                        for part in range(3):
                            for g in range(GROUPS):
                                dst = qk_parts[qk, bass.ds(b * GROUPS + g, 1), part].squeeze(0)
                                sp.dma_start(dst.rearrange("d h t -> h d t"),
                                             parts[g * 32:(g + 1) * 32, part, qk, :]).then_inc(parts_stored, 16)
                    sp.wait_ge(v_evac, b * 2 + 2)
                    sp.dma_start(v_padded[bass.ds(b, 1)].squeeze(0).rearrange("j p c -> p j c"),
                                 vpad[:].rearrange("p j h c -> p j (h c)")).then_inc(v_stored, 16)
                sp.wait_ge(parts_stored, 16 * STORES * BATCH)
                sp.wait_ge(v_stored, 16 * BATCH)

            @block.gpsimd
            def _(pool):
                pool.memset(vpad[:], 0.0).then_inc(vpad_set, 1)
                pool.wait_ge(vpad_set, 1)
                pool.memset(vpad[:, :, :, HD:HD + 1], 1.0).then_inc(vpad_set, 1)
                with pool.Fori(0, BATCH) as b:
                    for h in range(2):
                        pool.wait_ge(xnt_ready, b * 2 + h + 1)
                        pool.tensor_copy(XNT[:, bass.ds(b * T + h * TILE, TILE)],
                                         xnt[:, h * TILE:(h + 1) * TILE]).then_inc(xnt_copied, 1)

            @block.tensor
            def _(pe):
                with pe.Fori(0, BATCH) as b:
                    for h in range(2):
                        pe.wait_ge(xn_ready, b + 1)
                        pe.wait_ge(v_banks, b * 2 + h + 1)
                        for j in range(HALF):
                            m = pe.transpose(ps[:, h, j * P:(j + 1) * P], xn[:, h * HALF + j, :], ident[:])
                        m.then_inc(xt_banks, 1)
                    pe.wait_ge(xnt_ready, b * 2 + 2)
                    pe.wait_ge(g_bank, b + 1)
                    for j in range(BLK):
                        m = pe.matmul(ps[:, 6, j * N_EXP:(j + 1) * N_EXP], xnt[:, j * P:(j + 1) * P], gw[0][:],
                                      start=True, stop=True)
                    m.then_inc(g_ready, 1)
                    for qk, w in enumerate((W["wq0"], W["wk0"])):
                        for h in range(2):
                            pe.wait_ge(qk_banks, b * 4 + qk * 2 + h + 1)
                            pe.matmul(ps[:, 2 + qk * 2 + h, :], w[:], xnt[:, h * TILE:(h + 1) * TILE],
                                      start=True, stop=True).then_inc(qk_ready, 1)
                    for h in range(2):
                        for j in range(HALF):
                            m = pe.matmul(ps[:, h, j * P:(j + 1) * P],
                                          xnt[:, (h * HALF + j) * P:(h * HALF + j + 1) * P], W["wv0"][:],
                                          start=True, stop=True)
                        m.then_inc(v_ready, 1)

            @block.scalar
            def _(act):
                act.sem_inc(qk_banks, 4)
                with act.Fori(0, BATCH) as b:
                    act.wait_ge(moments_ready, b + 1)
                    deviation(act, moments, dev, eps).then_inc(dev_ready, 1)
                    for h in range(2):
                        act.wait_ge(xt_banks, b * 2 + h + 1)
                        act.wait_ge(v_banks, b * 2 + 2)
                        act.activation(xnt[:, h * TILE:(h + 1) * TILE], ps[:, h, :], ACT.Copy).then_inc(xnt_ready, 1)
                    for i in range(4):
                        act.wait_ge(qk_ready, b * 4 + i + 1)
                        act.wait_ge(qkf_free, b + 1)
                        act.activation(qkf[:, i // 2, (i % 2) * TILE:(i % 2 + 1) * TILE], ps[:, 2 + i, :],
                                       ACT.Copy, scale=float(HD) ** -0.25).then_inc(qk_banks, 1)

            @block.vector
            def _(dve):
                dve.sem_inc(v_banks, 2)
                dve.sem_inc(g_bank, 1)
                dve.sem_inc(qkf_free, 1)
                dve.wait_ge(x_in, 16 * BATCH)
                dve.wait_ge(vpad_set, 2)
                with dve.Fori(0, BATCH) as b:
                    cnt = Count(dve, dve_steps, b * DVE_STEPS)
                    rows = lambda j: X[:, bass.ds(b * BLK + j, 1), :].squeeze(1)
                    moments_of(dve, cnt, rows, stats, moments, BLK, stats_written)
                    dve.sem_inc(moments_ready, 1)
                    dve.wait_ge(dev_ready, b + 1)
                    scale_rows(dve, cnt, rows, lambda j: xn[:, j, :], moments, dev, rstd, BLK)
                    cnt.settle()
                    dve.sem_inc(xn_ready, 1)
                    dve.wait_ge(g_ready, b + 1)
                    cnt.mark(dve.tensor_tensor(
                        logits[:, bass.ds(b * BLK, BLK), :],
                        ps[:, 6, 0:BLK * N_EXP].rearrange("p (j e) -> p j e", j=BLK),
                        gb[0][:].unsqueeze(1).to_broadcast([P, BLK, N_EXP]), ALU.add))
                    cnt.settle()
                    dve.sem_inc(g_bank, 1)
                    dve.wait_ge(qk_banks, b * 4 + 8)
                    cnt.mark(dve.tensor_copy(parts[:, 0], qkf[:]))
                    cnt.settle()
                    cnt.mark(dve.tensor_tensor(rest[:], qkf[:], parts[:, 0], ALU.subtract))
                    cnt.settle()
                    cnt.mark(dve.tensor_copy(parts[:, 1], rest[:]))
                    cnt.settle()
                    dve.tensor_tensor(parts[:, 2], rest[:], parts[:, 1], ALU.subtract).then_inc(parts_ready, 1)
                    dve.wait_ge(parts_ready, b + 1)
                    dve.sem_inc(qkf_free, 1)
                    for h in range(2):
                        dve.wait_ge(v_ready, b * 2 + h + 1)
                        dve.tensor_copy(vpad[:, h * HALF:(h + 1) * HALF, :, 0:HD],
                                        ps[:, h, :].rearrange("p (j h d) -> p j h d", j=HALF, h=HEADS))\
                            .then_inc(v_evac, 1)
                        dve.wait_ge(v_evac, b * 2 + h + 1)
                        dve.sem_inc(v_banks, 1)
                    dve.wait_ge(parts_stored, b * (16 * STORES) + 16 * STORES)
                    dve.wait_ge(v_stored, b * 16 + 16)
                    dve.wait_ge(xnt_copied, b * 2 + 2)

        def route(layer):
            with ExitStack() as c:
                dve_steps, gap_ready, exp_ready, w_ready, turned, gate_ready, rows_stored = (
                    sem(f"{n}{layer}", c) for n in ("dve_steps_r", "gap_ready", "exp_ready", "w_ready", "turned",
                                                    "gate_ready", "rows_stored"))
                block = c.enter_context(nc.Block())
                PARTS = NBLK * N_EXP // P

                @block.vector
                def _(dve):
                    cnt = Count(dve, dve_steps)
                    top2_weights(dve, cnt, logits[:], weights[:], hot[:], score[:], best[:], rank[:], order[:],
                                 NBLK, N_EXP)
                    cnt.settle()
                    dve.sem_inc(gap_ready, 1)
                    dve.wait_ge(exp_ready, 1)
                    top2_mix(dve, cnt, weights[:], hot[:], best[:], rank[:], NBLK, N_EXP)
                    cnt.settle()
                    dve.sem_inc(w_ready, 1)
                    dve.wait_ge(turned, 1)
                    dve.tensor_copy(gate_t[:], ps[:, 0, 0:PARTS * P].rearrange("p (k q) -> p k q", k=PARTS))\
                        .then_inc(gate_ready, 1)

                @block.scalar
                def _(act):
                    act.wait_ge(gap_ready, 1)
                    act.activation(rank[:], rank[:], ACT.Exp).then_inc(exp_ready, 1)

                @block.tensor
                def _(pe):
                    pe.wait_ge(w_ready, 1)
                    flat = weights[:].rearrange("p n e -> p (n e)")
                    for k in range(PARTS):
                        m = pe.transpose(ps[:, 0, k * P:(k + 1) * P], flat[:, k * P:(k + 1) * P], ident[:])
                    m.then_inc(turned, 1)

                @block.sync
                def _(sp):
                    sp.wait_ge(gate_ready, 1)
                    rows = gate_rows[layer].rearrange("e (k n q) -> k n e q", k=PARTS, q=P)
                    for k in range(PARTS):
                        sp.dma_start(rows[k], gate_t[:, k, :]).then_inc(rows_stored, 16)
                    sp.wait_ge(rows_stored, 16 * PARTS)

        route(0)

        with ExitStack() as c:
            NU = BATCH * GROUPS
            qs = [sb(f"qs{g}", [P, GH, T], BF16, c) for g in range(GROUPS)]
            ks = [sb(f"ks{g}", [P, GH, T], BF16, c) for g in range(GROUPS)]
            vs = [sb(f"vs{g}", [P, BLK, GH * 32], F32, c) for g in range(GROUPS)]
            probs = sb("probs", [P, 2, GH, TILE], F32, c)
            o_sb = sb("o_sb", [P, TILE], F32, c)
            maxima = sb("maxima", [P, 2, GH, BLK + BLK // 2], F32, c)
            shift = sb("shift", [P, 3, GH, BLK], BF16, c)
            shift_rest = sb("shift_rest", [P, GH, BLK], F32, c)
            shift_t = sb("shift_t", [3 * GH * BLK, P], BF16, c)
            sums = sb("sums", [P, 4, GH], F32, c)
            unit_in = [sem(f"unit_in{g}", c) for g in range(GROUPS)]
            (rows_set, rows_steps, rows_clear, score_ready, exp_done, max_ready, max_done, pv_done, o_out, o_turned,
             misc_free, shift_ready, shift_turned, shift_out, shift_in, dve_steps) = (
                sem(n, c) for n in (
                    "rows_set", "rows_steps", "rows_clear", "score_ready", "exp_done", "max_ready", "max_done",
                    "pv_done", "o_out", "o_turned", "misc_free", "shift_ready", "shift_turned", "shift_out",
                    "shift_in", "dve_steps_b"))
            rows_used = sem("rows_used", c)
            block = c.enter_context(nc.Block())

            CHUNKS = [(h, qb, kt, min(TILE, (qb + 1) * P - kt * TILE))
                      for h in range(GH) for qb in range(BLK) for kt in range(1 + (qb * P) // TILE)]
            NC = len(CHUNKS)
            HALFC = NC // 2
            STEPS = [(qt, kb) for qt in range(2) for kb in range(4 * (qt + 1))]
            NS = len(STEPS)
            work = [4 - max(0, kb - 4 * qt) for qt, kb in STEPS]
            cuts = []
            for first in (0, NS // 2):
                total = sum(work[first:first + NS // 2])
                edges = [HALFC * sum(work[first:first + i]) // total for i in range(NS // 2 + 1)]
                cuts += list(zip(edges, edges[1:]))
            UNIT_LOADS = 16 * 7
            RETURN_STEP, SHIFT_STEP = 5, 7
            DVE_STEPS = 6

            def after(b, g, k):
                return b + (g + k) // GROUPS, (g + k) % GROUPS

            def ahead_of(s, b, g):
                return (*after(b, g, 1), HALFC) if s < NS // 2 else (*after(b, g, 2), 0)

            @block.sync
            def _(sp):
                def load(b, g):
                    u = b * GROUPS + g
                    q_src = qk_parts[0, bass.ds(u, 1)].squeeze(0).rearrange("c d h t -> c d (h t)")
                    k_src = qk_parts[1, bass.ds(u, 1)].squeeze(0).rearrange("c d h t -> (c d) (h t)")
                    for i in range(3):
                        rows = slice(24 * i, 24 * (i + 1))
                        sp.dma_start(qs[g][rows].rearrange("r h t -> r (h t)"),
                                     q_src[i].unsqueeze(0).to_broadcast([3, HD, GH * T])).then_inc(unit_in[g], 16)
                        sp.dma_start(ks[g][rows].rearrange("r h t -> r (h t)"), k_src).then_inc(unit_in[g], 16)
                    v_src = v_padded[bass.ds(b, 1)].squeeze(0).rearrange("j p c -> p j c")
                    sp.dma_start(vs[g][:], v_src[:, :, g * P:(g + 1) * P]).then_inc(unit_in[g], 16)

                def store_shift(b, g):
                    sp.wait_ge(shift_out, b * GROUPS + g + 1)
                    sp.dma_start(qs[g][96:99].rearrange("r h t -> r (h t)"), shift_t[:]).then_inc(shift_in, 16)

                sp.wait_ge(rows_set, 1)
                for g in range(GROUPS):
                    load(0, g)
                store_shift(0, 0)
                with sp.Fori(0, BATCH - 1) as b:
                    for g in range(GROUPS):
                        store_shift(*after(b, g, 1))
                        sp.wait_ge(pv_done, b * (GROUPS * NS) + (g + 1) * NS + 2)
                        load(b + 1, g)
                for g in range(GROUPS - 1):
                    store_shift(BATCH - 1, g + 1)
                sp.wait_ge(shift_in, 16 * NU)

            @block.gpsimd
            def _(pool):
                cnt = Count(pool, rows_steps)
                for g in range(GROUPS):
                    cnt.mark(pool.memset(qs[g][:].bitcast(U32), 0))
                    cnt.mark(pool.memset(ks[g][:].bitcast(U32), 0))
                cnt.settle()
                for g in range(GROUPS):
                    cnt.mark(pool.memset(ks[g][96:99], 1.0))
                cnt.settle()
                pool.sem_inc(rows_set, 1)
                pool.sem_inc(rows_clear, GROUPS)
                with pool.Fori(0, BATCH - 1) as b:
                    for g in range(GROUPS):
                        pool.wait_ge(pv_done, b * (GROUPS * NS) + (g + 1) * NS + 2)
                        pool.sem_inc(rows_used, 1)
                        pool.memset(qs[g][96:99].bitcast(U32), 0).then_inc(rows_clear, 1)

            @block.tensor
            def _(pe):
                def loaded(b, g):
                    pe.wait_ge(unit_in[g], b * UNIT_LOADS + UNIT_LOADS)
                    pe.wait_ge(rows_clear, b * GROUPS + g + 1)

                def first_pass(b, g, lo, hi):
                    for i in range(lo, hi):
                        h, qb, kt, w = CHUNKS[i]
                        pe.wait_ge(max_done, b * (GROUPS * NC) + g * NC + i + 1)
                        diagonal = qb * P // TILE == kt
                        dst = ps[:, i % 2, :]
                        m = pe.matmul(dst[:, 0:w], qs[g][:, h, qb * P:(qb + 1) * P],
                                      ks[g][:, h, kt * TILE:kt * TILE + w], start=True, stop=not diagonal)
                        if diagonal:
                            m = pe.matmul(dst[:, w - P:w], identb[:], mask_q[:], start=False, stop=True)
                        m.then_inc(max_ready, 1)

                def turn_shift(b, g, misc_uses):
                    pe.wait_ge(shift_ready, b * GROUPS + g + 1)
                    pe.wait_ge(misc_free, misc_uses)
                    pe.transpose(ps[0:3 * GH * BLK, 7, :].bitcast(BF16)[:, 0:P],
                                 shift[:].rearrange("p c h q -> p (c h q)"), identb[:]).then_inc(shift_turned, 1)

                def turn_output(b, g, qt, misc_uses):
                    pe.wait_ge(o_out, b * (2 * GROUPS) + 2 * g + qt + 2)
                    pe.wait_ge(misc_free, misc_uses)
                    for j in range(4):
                        m = pe.transpose(ps[:, 7, j * P:(j + 1) * P], o_sb[:, j * P:(j + 1) * P], ident[:])
                    m.then_inc(o_turned, 1)

                def scores(b, g, s, pair):
                    qt, kb = STEPS[s]
                    k = 2 * s + pair
                    skip = max(0, kb - 4 * qt) * P
                    pe.wait_ge(exp_done, b * (2 * GROUPS * NS) + 2 * g * NS + k + 1)
                    for i in range(2):
                        h = 2 * pair + i
                        dst = ps[:, 2 + 2 * (k % 2) + i, :]
                        m = pe.matmul(dst[:, 0:TILE - skip], ks[g][:, h, kb * P:(kb + 1) * P],
                                      qs[g][:, h, qt * TILE + skip:(qt + 1) * TILE],
                                      start=True, stop=kb < 4 * qt)
                        if kb >= 4 * qt:
                            m = pe.matmul(dst[:, 0:P], identb[:], mask_k[:], start=False, stop=True)
                    m.then_inc(score_ready, 1)

                def values(b, g, s):
                    qt, kb = STEPS[s]
                    skip = max(0, kb - 4 * qt) * P
                    pe.wait_ge(exp_done, b * (2 * GROUPS * NS) + 2 * g * NS + 2 * s + 4)
                    if kb == 0:
                        pe.wait_ge(o_out, b * (2 * GROUPS) + 2 * g + qt + 1)
                    for h in range(GH):
                        m = pe.matmul(ps[32 * h:32 * (h + 1), 6, skip:TILE], vs[g][:, kb, 32 * h:32 * (h + 1)],
                                      probs[:, s % 2, h, 0:TILE - skip], start=(kb == 0),
                                      stop=(kb == 4 * qt + 3))
                    m.then_inc(pv_done, 1)

                def unit(b, g, has_next=True, has_after=True):
                    u = b * GROUPS + g
                    pe.wait_ge(shift_in, u * 16 + 16)
                    for s in range(NS):
                        lo, hi = cuts[s]
                        mid = (lo + hi) // 2
                        ahead = has_next if s < NS // 2 else has_after
                        bn, gn, off = ahead_of(s, b, g)
                        if s == NS // 2 and ahead:
                            loaded(bn, gn)
                        scores(b, g, s, 0)
                        if ahead:
                            first_pass(bn, gn, off + lo, off + mid)
                        scores(b, g, s, 1)
                        if ahead:
                            first_pass(bn, gn, off + mid, off + hi)
                        if s > 0:
                            values(b, g, s - 1)
                        if s == RETURN_STEP:
                            turn_output(b, g, 0, u * 3 + 2)
                        if s == SHIFT_STEP and has_next:
                            turn_shift(*after(b, g, 1), u * 3 + 3)
                    values(b, g, NS - 1)
                    turn_output(b, g, 1, u * 3 + 3 + has_next)

                pe.sem_inc(pv_done, 2)
                pe.sem_inc(o_turned, 1)
                loaded(0, 0)
                first_pass(0, 0, 0, NC)
                turn_shift(0, 0, 1)
                loaded(0, 1)
                first_pass(0, 1, 0, HALFC)
                with pe.Fori(0, BATCH - 1) as b:
                    for g in range(GROUPS):
                        unit(b, g)
                for g in range(GROUPS):
                    unit(BATCH - 1, g, g + 1 < GROUPS, g + 2 < GROUPS)

            @block.scalar
            def _(act):
                def unit(b, g):
                    u = b * GROUPS + g
                    for s, (qt, kb) in enumerate(STEPS):
                        w = TILE - max(0, kb - 4 * qt) * P
                        act.wait_ge(pv_done, u * NS + s + 1)
                        for pair in range(2):
                            k = 2 * s + pair
                            act.wait_ge(score_ready, u * (2 * NS) + k + 1)
                            act.activation(probs[:, s % 2, 2 * pair:2 * pair + 2, 0:w],
                                           ps[:, 2 + 2 * (k % 2):4 + 2 * (k % 2), 0:w], ACT.Exp)\
                                .then_inc(exp_done, 1)
                        if s in (4, NS - 1):
                            q = 0 if s == 4 else 1
                            act.wait_ge(pv_done, u * NS + (4 if q == 0 else NS) + 2)
                            act.wait_ge(o_turned, u * 2 + q + 1)
                            act.activation(o_sb[:], ps[:, 6, :], ACT.Copy).then_inc(o_out, 1)

                act.sem_inc(exp_done, 2)
                act.sem_inc(o_out, 1)
                with act.Fori(0, BATCH) as b:
                    for g in range(GROUPS):
                        unit(b, g)

            @block.vector
            def _(dve):
                def reduce(b, g, lo, hi):
                    for i in range(lo, hi):
                        h, qb, kt, w = CHUNKS[i]
                        dve.wait_ge(max_ready, b * (GROUPS * NC) + g * NC + i + 1)
                        col = qb if kt == 0 else BLK + qb - 4
                        dve.tensor_reduce(maxima[:, g % 2, h, col:col + 1], ps[:, i % 2, 0:w], AX.X, ALU.max)\
                            .then_inc(max_done, 1)

                def take_output(cnt, b, g, qt):
                    dve.wait_ge(o_turned, b * (2 * GROUPS) + 2 * g + qt + 2)
                    o = ps[:, 7, :].rearrange("p (q h c) -> p q h c", q=4, h=GH)
                    cnt.mark(dve.reciprocal(sums[:], o[:, :, :, HD]))
                    cnt.settle()
                    blk = b * BLK + 4 * qt
                    dst = ATT[:, bass.ds(blk, 4), g * 32:(g + 1) * 32].rearrange("p q (h d) -> p q h d", h=GH)
                    dve.tensor_tensor(dst, o[:, :, :, 0:HD], sums[:].unsqueeze(3).to_broadcast([P, 4, GH, HD]),
                                      ALU.mult).then_inc(misc_free, 1)

                def make_shift(cnt, b, g):
                    m = maxima[:, g % 2]
                    dve.wait_ge(max_done, b * (GROUPS * NC) + (g + 1) * NC + 2)
                    cnt.mark(dve.tensor_tensor(m[:, :, 4:BLK], m[:, :, 4:BLK], m[:, :, BLK:], ALU.max))
                    cnt.settle()
                    cnt.mark(dve.tensor_scalar(shift[:, 0], m[:, :, 0:BLK], -1.0, None, ALU.mult))
                    cnt.settle()
                    cnt.mark(dve.scalar_tensor_tensor(shift_rest[:], m[:, :, 0:BLK], -1.0, shift[:, 0],
                                                      ALU.mult, ALU.subtract))
                    cnt.settle()
                    cnt.mark(dve.tensor_copy(shift[:, 1], shift_rest[:]))
                    cnt.settle()
                    dve.tensor_tensor(shift[:, 2], shift_rest[:], shift[:, 1], ALU.subtract).then_inc(shift_ready, 1)

                def take_shift(b, g, first=False):
                    u = b * GROUPS + g
                    dve.wait_ge(shift_turned, u + 1)
                    if not first:
                        dve.wait_ge(shift_in, u * 16)
                    dve.tensor_copy(shift_t[:], ps[0:3 * GH * BLK, 7, :].bitcast(BF16)[:, 0:P]).then_inc(shift_out, 1)
                    dve.wait_ge(shift_out, u + 1)
                    dve.sem_inc(misc_free, 1)

                def unit(b, g, has_next=True, has_after=True):
                    cnt = Count(dve, dve_steps, b * (GROUPS * DVE_STEPS) + (g + 1) * DVE_STEPS)
                    for s in range(NS):
                        lo, hi = cuts[s]
                        bn, gn, off = ahead_of(s, b, g)
                        if has_next if s < NS // 2 else has_after:
                            reduce(bn, gn, off + lo, off + hi)
                        if s == RETURN_STEP:
                            take_output(cnt, b, g, 0)
                            if has_next:
                                make_shift(cnt, *after(b, g, 1))
                        if s == SHIFT_STEP and has_next:
                            take_shift(*after(b, g, 1))
                    take_output(cnt, b, g, 1)
                    assert cnt.n == (DVE_STEPS if has_next else 2)

                dve.sem_inc(max_done, 2)
                dve.sem_inc(misc_free, 1)
                dve.sem_inc(dve_steps, DVE_STEPS - 4)
                reduce(0, 0, 0, NC)
                make_shift(Count(dve, dve_steps, DVE_STEPS - 4), 0, 0)
                take_shift(0, 0, first=True)
                reduce(0, 1, 0, HALFC)
                with dve.Fori(0, BATCH - 1) as b:
                    for g in range(GROUPS):
                        unit(b, g)
                for g in range(GROUPS):
                    unit(BATCH - 1, g, g + 1 < GROUPS, g + 2 < GROUPS)

        with ExitStack() as c:
            w12 = sb("w12", [P, 2, 2, F0], F32, c)
            wg = sb("wg", [P, 2, FF0, F0], F32, c)
            w3 = sb("w3", [P, 2, FF0, D], F32, c)
            vec0 = sb("vec0", [P, 2, PER0], F32, c)
            gate = sb("gate", [P, 2, N], F32, c)
            x1 = sb("x1", [P, 2, FF0, TILE], F32, c)
            z = sb("z", [P, 2, FF0, TILE], F32, c)
            act_out = sb("act_out", [P, 2, FF0, TILE], F32, c)
            y = sb("y", [P, 2, TILE], F32, c)
            weights_in = [sem(f"weights_in{i}", c) for i in range(2)]
            (x12_ready, x1_ready, z_ready, g_ready, silu_ready, y_ready, y_out, added) = (
                sem(f"{n}_c", c) for n in ("x12_ready", "x1_ready", "z_ready", "g_ready", "silu_ready", "y_ready",
                                           "y_out", "added"))
            block = c.enter_context(nc.Block())
            NSTEP = N_EXP * NTILE
            PER = 2 * NTILE
            TURNS = N_EXP // 2 - 1
            EXPERT_LOADS = 16 * 6

            @block.sync
            def _(sp):
                def load(e, slot):
                    one = lambda ap: ap[bass.ds(e, 1)].squeeze(0)
                    for dst, src in ((vec0[:, slot], vecs[:, bass.ds(e * PER0, PER0)]), (w12[:, slot, 0], one(f0_w1)), (w12[:, slot, 1], one(f0_w2)),
                                     (wg[:, slot], one(f0_wg).rearrange("(f p) g -> p f g", p=P)),
                                     (w3[:, slot], one(f0_w3).rearrange("(f p) g -> p f g", p=P)),
                                     (gate[:, slot], gate_rows[0][bass.ds(e, 1)].squeeze(0).partition_broadcast(P))):
                        sp.dma_start(dst, src).then_inc(weights_in[slot], 16)

                load(0, 0)
                load(1, 1)
                with sp.Fori(0, TURNS) as i:
                    for slot in range(2):
                        sp.wait_ge(y_out, i * PER + (slot + 1) * NTILE + 2)
                        load(i * 2 + 2 + slot, slot)

            @block.tensor
            def _(pe):
                def up(i, j):
                    slot, t = j // NTILE % 2, j % NTILE
                    if j % NTILE == 0:
                        pe.wait_ge(weights_in[slot], (i + j // PER) * EXPERT_LOADS + EXPERT_LOADS)
                    s = i * PER + j
                    for f in range(FF0):
                        pe.wait_ge(z_ready, s * FF0 + f + 1)
                        for k in range(2):
                            m = pe.matmul(ps[:, 2 * k + f, :], w12[:, slot, k, f * P:(f + 1) * P],
                                          XNT[:, t * TILE:(t + 1) * TILE], start=True, stop=True)
                        m.then_inc(x12_ready, 1)

                def gated(i, j):
                    slot, s = j // NTILE % 2, i * PER + j
                    pe.wait_ge(z_ready, s * FF0 + 2 * FF0)
                    for go in range(FF0):
                        pe.wait_ge(silu_ready, s * FF0 + go + 1)
                        for f in range(FF0):
                            m = pe.matmul(ps[:, 4 + go, :], wg[:, slot, f, go * P:(go + 1) * P],
                                          z[:, j % 2, f, :], start=(f == 0), stop=(f == FF0 - 1))
                        m.then_inc(g_ready, 1)

                def down(i, j):
                    slot, s = j // NTILE % 2, i * PER + j
                    pe.wait_ge(silu_ready, s * FF0 + 2 * FF0)
                    pe.wait_ge(y_out, s + 1)
                    for f in range(FF0):
                        m = pe.matmul(ps[:, 6 + j % 2, :], w3[:, slot, f, :], act_out[:, j % 2, f, :],
                                      start=(f == 0), stop=(f == FF0 - 1))
                    m.then_inc(y_ready, 1)

                pe.sem_inc(g_ready, 2 * FF0)
                pe.sem_inc(y_ready, 2)
                up(0, 0)
                up(0, 1)
                gated(0, 0)
                with pe.Fori(0, TURNS) as i:
                    for j in range(1, PER + 1):
                        up(i, j + 1)
                        down(i, j - 1)
                        gated(i, j)
                for j in range(1, PER):
                    if j + 1 < PER:
                        up(TURNS, j + 1)
                    down(TURNS, j - 1)
                    gated(TURNS, j)
                down(TURNS, PER - 1)

            @block.scalar
            def _(act):
                def first(i, j):
                    slot, s = j // NTILE % 2, i * PER + j
                    for f in range(FF0):
                        act.wait_ge(x12_ready, s * FF0 + f + 1)
                        bias = vec0[:, slot, f:f + 1]
                        act.activation(x1[:, j % 2, f, :], ps[:, f, :], ACT.Identity, bias=bias).then_inc(x1_ready, 1)

                def silu(i, j):
                    slot, s = j // NTILE % 2, i * PER + j
                    act.wait_ge(y_ready, s + 1)
                    for go in range(FF0):
                        act.wait_ge(g_ready, (s + 2) * FF0 + go + 1)
                        bias = vec0[:, slot, 2 * FF0 + go:2 * FF0 + go + 1]
                        act.activation(act_out[:, j % 2, go, :], ps[:, 4 + go, :], ACT.Silu, bias=bias)\
                            .then_inc(silu_ready, 1)

                act.sem_inc(silu_ready, FF0)
                first(0, 0)
                with act.Fori(0, TURNS) as i:
                    for j in range(PER):
                        first(i, j + 1)
                        silu(i, j)
                for j in range(PER):
                    if j + 1 < PER:
                        first(TURNS, j + 1)
                    silu(TURNS, j)

            @block.vector
            def _(dve):
                def product(i, j):
                    slot, s = j // NTILE % 2, i * PER + j
                    dve.wait_ge(g_ready, s * FF0 + FF0)
                    for f in range(FF0):
                        dve.wait_ge(x1_ready, s * FF0 + f + 1)
                        bias = vec0[:, slot, FF0 + f:FF0 + f + 1]
                        dve.scalar_tensor_tensor(z[:, j % 2, f, :], ps[:, 2 + f, :], bias, x1[:, j % 2, f, :],
                                                 ALU.add, ALU.mult).then_inc(z_ready, 1)

                def weigh(i, j):
                    slot, t, s = j // NTILE % 2, j % NTILE, i * PER + j
                    dve.wait_ge(y_ready, s + 3)
                    dve.wait_ge(added, s + 1)
                    bias = vec0[:, slot, 3 * FF0:PER0]
                    dve.scalar_tensor_tensor(y[:, j % 2, :], ps[:, 6 + j % 2, :], bias,
                                             gate[:, slot, t * TILE:(t + 1) * TILE], ALU.add, ALU.mult)\
                        .then_inc(y_out, 1)

                dve.sem_inc(z_ready, FF0)
                dve.sem_inc(y_out, 2)
                product(0, 0)
                product(0, 1)
                with dve.Fori(0, TURNS) as i:
                    for j in range(1, PER + 1):
                        product(i, j + 1)
                        weigh(i, j - 1)
                for j in range(1, PER):
                    if j + 1 < PER:
                        product(TURNS, j + 1)
                    weigh(TURNS, j - 1)
                weigh(TURNS, PER - 1)

            @block.gpsimd
            def _(pool):
                def add(s, j):
                    t = j % NTILE
                    pool.wait_ge(y_out, s + 3)
                    pool.wait_ge(added, s + 2)
                    tile = ACC[:, t * TILE:(t + 1) * TILE]
                    pool.tensor_tensor(tile, tile, y[:, j % 2, :], ALU.add).then_inc(added, 1)

                pool.memset(ACC[:], 0.0).then_inc(added, 2)
                with pool.Fori(0, N_EXP // 2) as i:
                    for j in range(PER):
                        add(i * PER + j, j)

        with ExitStack() as c:
            att_b = sb("att_b", [P, BLK, D], F32, c)
            acc_b = sb("acc_b", [P, T], F32, c)
            att_t = sb("att_t", [P, T], F32, c)
            x1b = sb("x1b", [P, BLK, D], F32, c)
            xnb = sb("xnb", [P, BLK, D], F32, c)
            xmb = sb("xmb", [P, BLK, D], F32, c)
            xn_t = sb("xn_t", [P, T], F32, c)
            xm_t = sb("xm_t", [P, T], F32, c)
            q_t = sb("q_t", [P, T], F32, c)
            k_t = sb("k_t", [P, T], F32, c)
            v = sb("v", [P, BLK, D], F32, c)
            p_sb = sb("p_sb", [P, 2, T], F32, c)
            p_t = sb("p_t", [P, 2, BLK, P], F32, c)
            o_t = sb("o_t", [P, P], F32, c)
            top = sb("top", [P, BLK], F32, c)
            bias = sb("bias", [P, BLK], F32, c)
            den = sb("den", [P, BLK], F32, c)
            rden = sb("rden", [P, BLK], F32, c)
            stats = sb("stats1", [P, BLK, 6], F32, c)
            moments = sb("moments1", [P, BLK, 2], F32, c)
            dev = sb("dev1", [P, BLK], F32, c)
            rstd = sb("rstd1", [P, BLK], F32, c)
            (slices_in, t_ready, t_out, x1_ready, x1_out, dve_steps, moments_ready, dev_ready, norm_ready, g_ready,
             g_out, qk_ready, qk_out, v_ready, v_out, s_ready, bias_ready, p_ready, o_ready, o_out, y_ready, y_out,
             xm_copied) = (sem(f"{n}_d", c) for n in (
                 "slices_in", "t_ready", "t_out", "x1_ready", "x1_out", "dve_steps", "moments_ready", "dev_ready",
                 "norm_ready", "g_ready", "g_out", "qk_ready", "qk_out", "v_ready", "v_out", "s_ready", "bias_ready",
                 "p_ready", "o_ready", "o_out", "y_ready", "y_out", "xm_copied"))
            stats_written = sem("stats_written_d", c)
            block = c.enter_context(nc.Block())
            SC = float(D) ** -0.5
            HALF = BLK // 2
            T_ATT, T_XN, T_XM = 0, 2, 4
            T_P = [6 + sum(1 + k // HALF for k in range(qb)) for qb in range(BLK + 1)]
            T_USES = T_P[BLK]
            DVE_STEPS = 2 + 2 * (3 * BLK + 1) + 2 + 2 * BLK

            @block.gpsimd
            def _(pool):
                with pool.Fori(0, BATCH) as b:
                    pool.wait_ge(x1_ready, b * 2 + 2)
                    pool.tensor_copy(att_b[:], ATT[:, bass.ds(b * BLK, BLK), :]).then_inc(slices_in, 1)
                    pool.tensor_copy(acc_b[:], ACC[:, bass.ds(b * T, T)]).then_inc(slices_in, 1)
                    pool.wait_ge(t_out, b * T_USES + T_XN + 2 + 2 + 2)
                    pool.tensor_copy(XNT[:, bass.ds(b * T, T)], xm_t[:]).then_inc(xm_copied, 1)

            @block.tensor
            def _(pe):
                pe.sem_inc(x1_ready, 2)
                with pe.Fori(0, BATCH) as b:
                    def turn(n, blocks):
                        pe.wait_ge(t_out, b * T_USES + n + 1)
                        for j, src in enumerate(blocks):
                            m = pe.transpose(ps[:, n % 2, j * P:(j + 1) * P], src, ident[:])
                        m.then_inc(t_ready, 1)

                    pe.wait_ge(slices_in, b * 2 + 1)
                    for h in range(2):
                        turn(T_ATT + h, [att_b[:, h * HALF + j, :] for j in range(HALF)])
                    pe.wait_ge(slices_in, b * 2 + 2)
                    pe.wait_ge(o_out, b * BLK + 1)
                    pe.wait_ge(y_out, b * BLK + 1)
                    for h in range(2):
                        pe.wait_ge(t_out, b * T_USES + T_ATT + h + 3)
                        for j in range(HALF):
                            blk = slice((h * HALF + j) * P, (h * HALF + j + 1) * P)
                            pe.matmul(ps[:, 2 + h, j * P:(j + 1) * P], att_t[:, blk], W["wo0"][:],
                                      start=True, stop=False)
                            m = pe.matmul(ps[:, 2 + h, j * P:(j + 1) * P], acc_b[:, blk], ident[:],
                                          start=False, stop=True)
                        m.then_inc(x1_ready, 1)
                    pe.wait_ge(norm_ready, b * 2 + 1)
                    for h in range(2):
                        turn(T_XN + h, [xnb[:, h * HALF + j, :] for j in range(HALF)])
                    pe.wait_ge(t_out, b * T_USES + T_XN + 2 + 2)
                    for i in range(4):
                        pe.wait_ge(p_ready, b * BLK + 2)
                        pe.matmul(ps[:, 4 + i, :], W["wq1" if i < 2 else "wk1"][:],
                                  xn_t[:, (i % 2) * TILE:(i % 2 + 1) * TILE], start=True, stop=True)\
                            .then_inc(qk_ready, 1)
                    for h in range(2):
                        pe.wait_ge(x1_out, b * 2 + h + 1)
                        for j in range(HALF):
                            blk = slice((h * HALF + j) * P, (h * HALF + j + 1) * P)
                            m = pe.matmul(ps[:, 2 + h, j * P:(j + 1) * P], xn_t[:, blk], W["wv1"][:],
                                          start=True, stop=True)
                        m.then_inc(v_ready, 1)
                    pe.wait_ge(norm_ready, b * 2 + 2)
                    for h in range(2):
                        turn(T_XM + h, [xmb[:, h * HALF + j, :] for j in range(HALF)])
                    pe.wait_ge(t_out, b * T_USES + T_XM + 2 + 2)
                    pe.wait_ge(qk_out, b * 4 + 4)
                    for j in range(BLK):
                        m = pe.matmul(ps[:, 7, j * N_EXP:(j + 1) * N_EXP], xm_t[:, j * P:(j + 1) * P], gw[1][:],
                                      start=True, stop=True)
                    m.then_inc(g_ready, 1)

                    def scores(qb):
                        bank = 4 + 2 * (qb % 2)
                        if qb >= 2:
                            pe.wait_ge(p_ready, b * BLK + qb + 1)
                        if qb == 1:
                            pe.wait_ge(g_out, b + 1)
                        n_keys = (qb + 1) * P
                        for kt in range(1 + qb // 4):
                            w = min(TILE, n_keys - kt * TILE)
                            last = (kt == qb // 4)
                            m = pe.matmul(ps[:, bank + kt, 0:w], q_t[:, qb * P:(qb + 1) * P],
                                          k_t[:, kt * TILE:kt * TILE + w], start=True, stop=not last)
                            if last:
                                m = pe.matmul(ps[:, bank + kt, w - P:w], identb[:], mask_q[:],
                                              start=False, stop=True)
                        m.then_inc(s_ready, 1)

                    def project(qb):
                        pe.wait_ge(o_out, b * BLK + qb + 2)
                        pe.wait_ge(y_out, b * BLK + qb + 1)
                        pe.matmul(ps[:, 3, 0:D], o_t[:], W["wo1"][:], start=True, stop=True).then_inc(y_ready, 1)

                    scores(0)
                    scores(1)
                    pe.wait_ge(v_out, b * 2 + 2)
                    for qb in range(BLK):
                        pe.wait_ge(p_ready, b * BLK + qb + 3)
                        for h in range(1 + qb // HALF):
                            turn(T_P[qb] + h, [p_sb[:, qb % 2, kb * P:(kb + 1) * P]
                                               for kb in range(h * HALF, min((h + 1) * HALF, qb + 1))])
                        if qb + 2 < BLK:
                            scores(qb + 2)
                        pe.wait_ge(t_out, b * T_USES + T_P[qb + 1] + 2)
                        pe.wait_ge(o_out, b * BLK + qb + 1)
                        for kb in range(qb + 1):
                            m = pe.matmul(ps[:, 2, 0:P], v[:, kb, :], p_t[:, qb % 2, kb, :],
                                          start=(kb == 0), stop=(kb == qb))
                        m.then_inc(o_ready, 1)
                        if qb > 0:
                            project(qb - 1)
                    project(BLK - 1)

            @block.scalar
            def _(act):
                act.sem_inc(t_out, 2)
                act.sem_inc(o_out, 1)
                act.sem_inc(p_ready, 2)
                with act.Fori(0, BATCH) as b:
                    def take(n, dst, src, **affine):
                        act.wait_ge(t_ready, b * T_USES + n + 1)
                        act.activation(dst, src, ACT.Identity, **affine).then_inc(t_out, 1)

                    def half(t, h):
                        return t[:, h * TILE:(h + 1) * TILE]

                    for h in range(2):
                        take(T_ATT + h, half(att_t, h), ps[:, h, :])
                    act.wait_ge(moments_ready, b * 2 + 1)
                    deviation(act, moments, dev, eps).then_inc(dev_ready, 1)
                    for h in range(2):
                        take(T_XN + h, half(xn_t, h), ps[:, h, :])
                    act.wait_ge(moments_ready, b * 2 + 2)
                    deviation(act, moments, dev, eps).then_inc(dev_ready, 1)
                    for i in range(4):
                        act.wait_ge(qk_ready, b * 4 + i + 1)
                        act.activation(half(q_t if i < 2 else k_t, i % 2), ps[:, 4 + i, :], ACT.Copy)\
                            .then_inc(qk_out, 1)
                    act.wait_ge(xm_copied, b + 1)
                    for h in range(2):
                        take(T_XM + h, half(xm_t, h), ps[:, h, :], scale=vec("ln_g"), bias=vec("ln_b"))

                    def exponentials(qb):
                        w = (qb + 1) * P
                        act.wait_ge(bias_ready, b * BLK + qb + 1)
                        src = ps[:, 4 + 2 * (qb % 2):6 + 2 * (qb % 2), :].rearrange("p k c -> p (k c)")[:, 0:w]
                        act.activation(p_sb[:, qb % 2, 0:w], src, ACT.Exp, bias=bias[:, qb:qb + 1], scale=SC,
                                       accum_out=den[:, qb:qb + 1]).then_inc(p_ready, 1)

                    exponentials(0)
                    for qb in range(BLK):
                        if qb + 1 < BLK:
                            exponentials(qb + 1)
                        for h in range(1 + qb // HALF):
                            n = min((h + 1) * HALF, qb + 1) - h * HALF
                            use = T_P[qb] + h
                            take(use, p_t[:, qb % 2, h * HALF:h * HALF + n, :],
                                 ps[:, use % 2, 0:n * P].rearrange("p (k q) -> p k q", k=n))
                        act.wait_ge(o_ready, b * BLK + qb + 1)
                        if qb > 0:
                            act.wait_ge(y_ready, b * BLK + qb)
                        act.activation(o_t[:], ps[:, 2, 0:P], ACT.Copy).then_inc(o_out, 1)

            @block.vector
            def _(dve):
                dve.sem_inc(y_out, 1)
                dve.sem_inc(xm_copied, 1)
                with dve.Fori(0, BATCH) as b:
                    cnt = Count(dve, dve_steps, b * DVE_STEPS)
                    for h in range(2):
                        dve.wait_ge(x1_ready, b * 2 + h + 3)
                        cnt.mark(dve.tensor_tensor(
                            x1b[:, h * HALF:(h + 1) * HALF, :],
                            ps[:, 2 + h, :].rearrange("p (j d) -> p j d", j=HALF),
                            X[:, bass.ds(b * BLK + h * HALF, HALF), :], ALU.add))
                        cnt.settle()
                        dve.sem_inc(x1_out, 1)
                    moments_of(dve, cnt, lambda j: x1b[:, j, :], stats, moments, BLK, stats_written)
                    dve.sem_inc(moments_ready, 1)
                    dve.wait_ge(dev_ready, b * 2 + 1)
                    scale_rows(dve, cnt, lambda j: x1b[:, j, :], lambda j: xnb[:, j, :], moments, dev, rstd, BLK)
                    cnt.settle()
                    dve.sem_inc(norm_ready, 1)
                    moments_of(dve, cnt, lambda j: xnb[:, j, :], stats, moments, BLK, stats_written)
                    dve.sem_inc(moments_ready, 1)
                    dve.wait_ge(dev_ready, b * 2 + 2)
                    scale_rows(dve, cnt, lambda j: xnb[:, j, :], lambda j: xmb[:, j, :], moments, dev, rstd, BLK)
                    cnt.settle()
                    dve.sem_inc(norm_ready, 1)
                    cnt.mark(dve.tensor_tensor(x1b[:], x1b[:], xnb[:], ALU.add))
                    for h in range(2):
                        dve.wait_ge(v_ready, b * 2 + h + 1)
                        dve.tensor_copy(v[:, h * HALF:(h + 1) * HALF, :],
                                        ps[:, 2 + h, :].rearrange("p (j d) -> p j d", j=HALF)).then_inc(v_out, 1)
                    dve.wait_ge(g_ready, b + 1)
                    cnt.mark(dve.tensor_tensor(
                        logits[:, bass.ds(b * BLK, BLK), :],
                        ps[:, 7, 0:BLK * N_EXP].rearrange("p (j e) -> p j e", j=BLK),
                        gb[1][:].unsqueeze(1).to_broadcast([P, BLK, N_EXP]), ALU.add))
                    cnt.settle()
                    dve.sem_inc(g_out, 1)

                    def maximum(qb):
                        w = (qb + 1) * P
                        dve.wait_ge(s_ready, b * BLK + qb + 1)
                        src = ps[:, 4 + 2 * (qb % 2):6 + 2 * (qb % 2), :].rearrange("p k c -> p (k c)")[:, 0:w]
                        cnt.mark(dve.tensor_reduce(top[:, qb:qb + 1], src, AX.X, ALU.max))
                        cnt.settle()
                        dve.tensor_scalar(bias[:, qb:qb + 1], top[:, qb:qb + 1], -SC, None, ALU.mult)\
                            .then_inc(bias_ready, 1)

                    def finish(qb):
                        dve.wait_ge(y_ready, b * BLK + qb + 1)
                        dve.scalar_tensor_tensor(X[:, bass.ds(b * BLK + qb, 1), :].squeeze(1), ps[:, 3, 0:D],
                                                 rden[:, qb:qb + 1], x1b[:, qb, :], ALU.mult, ALU.add)\
                            .then_inc(y_out, 1)

                    maximum(0)
                    maximum(1)
                    for qb in range(BLK):
                        dve.wait_ge(p_ready, b * BLK + qb + 3)
                        cnt.mark(dve.reciprocal(rden[:, qb:qb + 1], den[:, qb:qb + 1]))
                        cnt.settle()
                        if qb + 2 < BLK:
                            maximum(qb + 2)
                        if qb > 0:
                            finish(qb - 1)
                    finish(BLK - 1)
                    assert cnt.n == DVE_STEPS

        route(1)

        with ExitStack() as c:
            u1 = sb("u1", [P, 2, F1], F32, c)
            u2 = sb("u2", [P, 2, FF1, D], F32, c)
            vec1 = sb("vec1", [P, 2, PER1], F32, c)
            gate = sb("gate1", [P, 2, N], F32, c)
            hid = sb("hid", [P, 2, FF1, TILE], F32, c)
            y = sb("y1", [P, 2, TILE], F32, c)
            weights_in = [sem(f"weights1_in{i}", c) for i in range(2)]
            (h_ready, gelu_ready, y_ready, y_out, added) = (
                sem(f"{n}_e", c) for n in ("h_ready", "gelu_ready", "y_ready", "y_out", "added"))
            block = c.enter_context(nc.Block())
            PER = 2 * NTILE
            TURNS = N_EXP // 2 - 1
            EXPERT_LOADS = 16 * 4

            @block.sync
            def _(sp):
                def load(e, slot):
                    one = lambda ap: ap[bass.ds(e, 1)].squeeze(0)
                    for dst, src in ((vec1[:, slot], vecs[:, bass.ds(e * PER1 + FIRST1, PER1)]), (u1[:, slot], one(f1_w1)),
                                     (u2[:, slot], one(f1_w2).rearrange("(f p) g -> p f g", p=P)),
                                     (gate[:, slot], gate_rows[1][bass.ds(e, 1)].squeeze(0).partition_broadcast(P))):
                        sp.dma_start(dst, src).then_inc(weights_in[slot], 16)

                load(0, 0)
                load(1, 1)
                with sp.Fori(0, TURNS) as i:
                    for slot in range(2):
                        sp.wait_ge(y_out, i * PER + (slot + 1) * NTILE + 2)
                        load(i * 2 + 2 + slot, slot)

            @block.tensor
            def _(pe):
                def up(i, j):
                    slot, t, s = j // NTILE % 2, j % NTILE, i * PER + j
                    if j % NTILE == 0:
                        pe.wait_ge(weights_in[slot], (i + j // PER) * EXPERT_LOADS + EXPERT_LOADS)
                    for f in range(FF1):
                        pe.wait_ge(gelu_ready, s * FF1 + f + 1)
                        pe.matmul(ps[:, f, :], u1[:, slot, f * P:(f + 1) * P], XNT[:, t * TILE:(t + 1) * TILE],
                                  start=True, stop=True).then_inc(h_ready, 1)

                def down(i, j):
                    slot, s = j // NTILE % 2, i * PER + j
                    pe.wait_ge(y_out, s + 1)
                    for f in range(FF1):
                        pe.wait_ge(gelu_ready, s * FF1 + f + 1 + FF1)
                        m = pe.matmul(ps[:, 4 + j % 2, :], u2[:, slot, f, :], hid[:, j % 2, f, :],
                                      start=(f == 0), stop=(f == FF1 - 1))
                    m.then_inc(y_ready, 1)

                pe.sem_inc(y_ready, 2)
                up(0, 0)
                with pe.Fori(0, TURNS) as i:
                    for j in range(PER):
                        up(i, j + 1)
                        down(i, j)
                for j in range(PER):
                    if j + 1 < PER:
                        up(TURNS, j + 1)
                    down(TURNS, j)

            @block.scalar
            def _(act):
                act.sem_inc(gelu_ready, FF1)
                with act.Fori(0, N_EXP // 2) as i:
                    for j in range(PER):
                        slot, s = j // NTILE, i * PER + j
                        act.wait_ge(y_ready, s + 1)
                        for f in range(FF1):
                            act.wait_ge(h_ready, s * FF1 + f + 1)
                            bias = vec1[:, slot, f:f + 1]
                            act.activation(hid[:, j % 2, f, :], ps[:, f, :], ACT.Gelu, bias=bias)\
                                .then_inc(gelu_ready, 1)

            @block.vector
            def _(dve):
                dve.sem_inc(y_out, 2)
                with dve.Fori(0, N_EXP // 2) as i:
                    for j in range(PER):
                        s, slot, t = i * PER + j, j // NTILE, j % NTILE
                        dve.wait_ge(y_ready, s + 3)
                        dve.wait_ge(added, s + 1)
                        bias = vec1[:, slot, FF1:PER1]
                        dve.scalar_tensor_tensor(y[:, j % 2, :], ps[:, 4 + j % 2, :], bias,
                                                 gate[:, slot, t * TILE:(t + 1) * TILE], ALU.add, ALU.mult)\
                            .then_inc(y_out, 1)

            @block.gpsimd
            def _(pool):
                pool.memset(ACC[:], 0.0).then_inc(added, 2)
                with pool.Fori(0, N_EXP // 2) as i:
                    for j in range(PER):
                        s, t = i * PER + j, j % NTILE
                        pool.wait_ge(y_out, s + 3)
                        pool.wait_ge(added, s + 2)
                        tile = ACC[:, t * TILE:(t + 1) * TILE]
                        pool.tensor_tensor(tile, tile, y[:, j % 2, :], ALU.add).then_inc(added, 1)

        with ExitStack() as c:
            abel = sb("abel", [P, N], F32, c)
            non = sb("non", [P, 2, TILE], F32, c)
            g_sb = sb("g_sb", [P, 2, TILE], F32, c)
            mixed = sb("mixed", [P, 2, TILE], F32, c)
            mix = sb("mix", [P, 2, D], F32, c)
            out_sb = sb("out_sb", [P, 2, TILE // P, D], F32, c)
            (mix_set, a_ready, abel_ready, n_ready, non_ready, z_ready, g_ready, dve_steps, mixed_ready, t_ready,
             out_ready) = (sem(f"{n}_f", c) for n in (
                 "mix_set", "a_ready", "abel_ready", "n_ready", "non_ready", "z_ready", "g_ready", "dve_steps",
                 "mixed_ready", "t_ready", "out_ready"))
            stored = [sem(f"stored{i}", c) for i in range(2)]
            block = c.enter_context(nc.Block())
            out_tiles = out.rearrange("b (k j p) d -> (b k) p j d", p=P, j=TILE // P)

            @block.sync
            def _(sp):
                for t in range(NTILE):
                    sp.wait_ge(out_ready, t + 3)
                    sp.dma_start(out_tiles[t], out_sb[:, t % 2]).then_inc(stored[t % 2], 16)
                for i in range(2):
                    sp.wait_ge(stored[i], 16 * NTILE // 2)

            @block.tensor
            def _(pe):
                pe.sem_inc(t_ready, 2)
                pe.sem_inc(z_ready, 2)
                for t in range(NTILE):
                    pe.wait_ge(abel_ready, t + 1)
                    pe.matmul(ps[:, t % 2, :], W["abw"][:], XNT[:, t * TILE:(t + 1) * TILE],
                              start=True, stop=True).then_inc(a_ready, 1)

                def turned(t):
                    pe.wait_ge(mixed_ready, t + 1)
                    pe.wait_ge(out_ready, t + 1)
                    for j in range(TILE // P):
                        m = pe.transpose(ps[:, 6 + t % 2, j * P:(j + 1) * P],
                                         mixed[:, t % 2, j * P:(j + 1) * P], ident[:])
                    m.then_inc(t_ready, 1)

                pe.wait_ge(mix_set, 2)
                for t in range(NTILE):
                    cols = slice(t * TILE, (t + 1) * TILE)
                    pe.wait_ge(non_ready, t + 1)
                    pe.matmul(ps[:, 2 + t % 2, :], rot[:], ACC[:, cols], start=True, stop=True).then_inc(n_ready, 1)
                    pe.wait_ge(g_ready, t + 1)
                    pe.wait_ge(abel_ready, t + 3)
                    pe.matmul(ps[:, 4 + t % 2, :], mix[:, 0, :], abel[:, cols], start=True, stop=False)
                    pe.wait_ge(non_ready, t + 3)
                    pe.matmul(ps[:, 4 + t % 2, :], mix[:, 1, :], non[:, t % 2, :], start=False, stop=True)\
                        .then_inc(z_ready, 1)
                    if t > 0:
                        turned(t - 1)
                turned(NTILE - 1)

            @block.scalar
            def _(act):
                act.sem_inc(abel_ready, 2)
                act.sem_inc(g_ready, 2)
                for t in range(NTILE):
                    act.wait_ge(a_ready, t + 1)
                    act.activation(abel[:, t * TILE:(t + 1) * TILE], ps[:, t % 2, :], ACT.Gelu,
                                   bias=vec("abel_b")).then_inc(abel_ready, 1)
                for t in range(NTILE):
                    act.wait_ge(z_ready, t + 3)
                    if t >= 2:
                        act.wait_ge(mixed_ready, t - 1)
                    act.activation(g_sb[:, t % 2, :], ps[:, 4 + t % 2, :], ACT.Sigmoid, bias=mixb[:])\
                        .then_inc(g_ready, 1)

            @block.vector
            def _(dve):
                dve.sem_inc(non_ready, 2)
                dve.sem_inc(out_ready, 2)
                for k in range(2):
                    dve.tensor_copy(mix[:, k, :], vec(("mix_a", "mix_b")[k]).to_broadcast([P, D])).then_inc(mix_set, 1)
                cnt = Count(dve, dve_steps)

                def output(t):
                    dve.wait_ge(t_ready, t + 3)
                    if t >= 2:
                        dve.wait_ge(stored[t % 2], 16 * (t // 2))
                    dve.tensor_tensor(out_sb[:, t % 2], ps[:, 6 + t % 2, :].rearrange("p (j d) -> p j d", d=D),
                                      X[:, t * (TILE // P):(t + 1) * (TILE // P), :], ALU.add).then_inc(out_ready, 1)

                def take(t):
                    dve.wait_ge(n_ready, t + 1)
                    dve.wait_ge(z_ready, t + 1)
                    dve.tensor_copy(non[:, t % 2, :], ps[:, 2 + t % 2, :]).then_inc(non_ready, 1)

                take(0)
                for t in range(NTILE):
                    ab = abel[:, t * TILE:(t + 1) * TILE]
                    dve.wait_ge(t_ready, t + 1)
                    dve.wait_ge(non_ready, t + 3)
                    dve.wait_ge(abel_ready, t + 3)
                    cnt.mark(dve.tensor_tensor(mixed[:, t % 2, :], non[:, t % 2, :], ab, ALU.subtract))
                    cnt.settle()
                    if t + 1 < NTILE:
                        take(t + 1)
                    dve.wait_ge(g_ready, t + 3)
                    cnt.mark(dve.tensor_tensor(mixed[:, t % 2, :], mixed[:, t % 2, :], g_sb[:, t % 2, :], ALU.mult))
                    cnt.settle()
                    dve.tensor_tensor(mixed[:, t % 2, :], mixed[:, t % 2, :], ab, ALU.add).then_inc(mixed_ready, 1)
                    if t > 0:
                        output(t - 1)
                output(NTILE - 1)


_INS = ['L0_attn_x', 'L0_attn_Wq', 'L0_attn_Wk', 'L0_attn_Wv', 'L0_attn_Wo', 'L0_ffn_gate_w', 'L0_ffn_gate_b',
        'L0_ffn_w1', 'L0_ffn_b1', 'L0_ffn_w2', 'L0_ffn_b2', 'L0_ffn_wg', 'L0_ffn_bg', 'L0_ffn_w3', 'L0_ffn_b3',
        'L1_attn_Wq', 'L1_attn_Wk', 'L1_attn_Wv', 'L1_attn_Wo', 'L1_ffn_ln_g', 'L1_ffn_ln_b', 'L1_ffn_abel_w',
        'L1_ffn_abel_b', 'L1_ffn_gate_w_moe', 'L1_ffn_gate_b_moe', 'L1_ffn_w1', 'L1_ffn_b1', 'L1_ffn_w2',
        'L1_ffn_b2', 'L1_ffn_gens', 'L1_ffn_mix_w', 'L1_ffn_mix_b']
_OUTS = [((4, 1024, 128), 'float32')]


def kernel(**inputs):
    import numpy as _np
    import concourse.bacc as _bacc
    from concourse import mybir as _mybir
    from concourse.bass_utils import run_bass_kernel_spmd as _run

    nc = _bacc.Bacc("TRN2", target_bir_lowering=False, num_devices=1)
    arrays, args = {}, []
    for name in _INS:
        a = _np.ascontiguousarray(inputs[name])
        arrays[f"in_{name}_dram"] = a
        args.append(nc.dram_tensor(f"in_{name}_dram", a.shape, _mybir.dt.from_np(a.dtype), kind="ExternalInput").ap())
    for i, (shape, dtype) in enumerate(_OUTS):
        dt = _mybir.dt.from_np(_np.dtype(dtype))
        args.append(nc.dram_tensor(f"out_{i}_dram", shape, dt, kind="ExternalOutput").ap())
    two_layers(nc, *args)
    r = _run(nc, [arrays], core_ids=[0])
    got = tuple(r.results[0][f"out_{i}_dram"] for i in range(len(_OUTS)))
    return got[0]
```

```python
from contextlib import ExitStack, contextmanager

import concourse.bass as bass
from concourse import mybir

F32 = mybir.dt.float32
BF16 = mybir.dt.bfloat16
U32 = mybir.dt.uint32
ALU = mybir.AluOpType
ACT = mybir.ActivationFunctionType
AX = mybir.AxisListType

P = 128
NEG = -1.0e30
EPS = 1e-5
TILE = 512
SQUARINGS = 7
DEGREE = 8


class Count:

    def __init__(self, eng, sem, start=0):
        self.eng, self.sem, self.start, self.n = eng, sem, start, 0

    def mark(self, ins):
        self.n += 1
        ins.then_inc(self.sem, 1)

    def settle(self):
        self.eng.wait_ge(self.sem, self.start + self.n)


def moments_of(dve, cnt, src, stats, moments, blocks, stats_written):
    for j in range(blocks):
        cnt.mark(dve.bn_stats(stats[:, j, :], src(j)))
    cnt.settle()
    dve.sem_inc(stats_written, 1)
    for j in range(blocks):
        cnt.mark(dve.bn_aggr(moments[:, j, :], stats[:, j, :]))
    cnt.settle()


def deviation(act, moments, dev, eps):
    return act.activation(dev[:], moments[:, :, 1], ACT.Sqrt, bias=eps[:, 0:1])


def scale_rows(dve, cnt, src, dst, moments, dev, rstd, blocks):
    cnt.mark(dve.reciprocal(rstd[:], dev[:]))
    cnt.settle()
    for j in range(blocks):
        cnt.mark(dve.tensor_scalar(dst(j), src(j), moments[:, j, 0:1], rstd[:, j:j + 1],
                                   ALU.subtract, ALU.mult))


def top2_choices(dve, cnt, logits, lower, hot, score, best, rank, order, n, n_exp):
    wide = [P, n, n_exp]
    bc = lambda ap: ap.unsqueeze(2).to_broadcast(wide)
    ranks = order.unsqueeze(1).to_broadcast(wide)
    for k in range(2):
        src = logits if k == 0 else lower
        cnt.mark(dve.tensor_reduce(best[:, k, :], src, AX.X, ALU.max))
        cnt.settle()
        cnt.mark(dve.tensor_tensor(score, src, bc(best[:, k, :]), ALU.is_equal))
        cnt.settle()
        cnt.mark(dve.tensor_tensor(score, score, ranks, ALU.mult))
        cnt.settle()
        cnt.mark(dve.tensor_reduce(rank, score, AX.X, ALU.max))
        cnt.settle()
        cnt.mark(dve.tensor_tensor(hot[:, k], score, bc(rank), ALU.is_equal))
        cnt.settle()
        if k == 0:
            cnt.mark(dve.scalar_tensor_tensor(lower, hot[:, 0], -3.0e38, logits, ALU.mult, ALU.add))
            cnt.settle()
    cnt.mark(dve.tensor_tensor(rank, best[:, 1, :], best[:, 0, :], ALU.subtract))


def two_layers(nc, x, a0_wq, a0_wk, a0_wv, a0_wo, f0_gw, f0_gb, f0_w1, f0_b1, f0_w2, f0_b2, f0_wg, f0_bg,
               f0_w3, f0_b3, a1_wq, a1_wk, a1_wv, a1_wo, ln_g, ln_b, abel_w, abel_b, f1_gw, f1_gb,
               f1_w1, f1_b1, f1_w2, f1_b2, gens, mix_w, mix_b, out):
    BATCH, T, D = x.shape
    N_EXP, _, F0 = f0_w1.shape
    F1 = f1_w1.shape[2]
    HD = 8
    HEADS = D // HD
    GH = 4
    GROUPS = HEADS // GH
    N = BATCH * T
    NBLK, BLK = N // P, T // P
    NTILE = N // TILE
    NROT = gens.shape[0]
    assert D == P and HD * 9 + 24 == 96 and GH * HD == 32 and T == 2 * TILE

    dram = lambda name, shape, dt: nc.dram_tensor(name, shape, dt, kind="Internal").ap()
    qk_parts = dram("qk_parts", [2, BATCH * GROUPS, 3, HD, GH, T], BF16)
    v_padded = dram("v_padded", [BATCH, BLK, P, HEADS * 32], F32)
    TILES = (2 * N + N_EXP * (TILE - 1)) // TILE
    x_slots = [dram(f"x_slots{i}", [TILES * TILE, D], F32) for i in range(2)]
    y_slots = [dram(f"y_slots{i}", [TILES * TILE, D], F32) for i in range(2)]

    ctx = ExitStack()
    with ctx:
        sb = lambda name, shape, dt, c=ctx: c.enter_context(nc.sbuf_tensor(name, shape, dt))
        sem = lambda name, c=None: nc.alloc_semaphore(name=name)
        ps = ctx.enter_context(nc.psum_tensor("ps", [P, 8, TILE], F32))

        X = sb("X", [P, NBLK, D], F32)
        XN = sb("XN", [P, NBLK, D], F32)
        ATT = sb("ATT", [P, NBLK, D], F32)
        ident = sb("ident", [P, P], F32)
        identb = sb("identb", [P, P], BF16)
        mask_q = sb("mask_q", [P, P], BF16)
        mask_k = sb("mask_k", [P, P], BF16)
        order = sb("order", [P, N_EXP], F32)
        logits = sb("logits", [P, NBLK, N_EXP], F32)
        share = sb("share", [P, 2, NBLK], F32)
        slot_of = sb("slot_of", [P, 2, NBLK], U32)
        tile_expert = sb("tile_expert", [P, TILES], U32)
        before = sb("before", [P, P], F32)
        ones = sb("ones", [P, P], F32)
        zeros = sb("zeros", [P, D], F32)
        steps_of = sb("steps_of", [P, NTILE], F32)
        tile_index = sb("tile_index", [P, TILES], F32)
        W_names = ["wq0", "wk0", "wv0", "wo0", "wq1", "wk1", "wv1", "wo1", "abw"]
        W_src = [a0_wq, a0_wk, a0_wv, a0_wo, a1_wq, a1_wk, a1_wv, a1_wo, abel_w]
        W = {n: sb(n, [P, D], F32) for n in W_names}
        gw = [sb(f"gw{i}", [P, N_EXP], F32) for i in range(2)]
        gb = [sb(f"gb{i}", [P, N_EXP], F32) for i in range(2)]
        FF0, FF1 = F0 // P, F1 // P
        PER0, PER1 = 3 * FF0 + 1, FF1 + 1
        FIRST1 = N_EXP * PER0
        OTHERS = {n: FIRST1 + N_EXP * PER1 + i for i, n in enumerate(("ln_g", "ln_b", "abel_b", "mix_a", "mix_b"))}
        NVEC = max(OTHERS.values()) + 1
        vecs = sb("vecs", [P, NVEC], F32)

        def vec(name):
            return vecs[:, OTHERS[name]:OTHERS[name] + 1]

        mixb = sb("mixb", [P, 1], F32)
        rot = sb("rot", [P, D], F32)
        eps = sb("eps", [P, 1], F32)
        x_in = sem("x_in")
        zeroed = sem("zeroed")

        x_blocks = x.rearrange("b (j p) d -> b p j d", p=P)

        @contextmanager
        def phase():
            known = nc.snapshot_sems()
            with ExitStack() as c:
                yield c
            nc.clear_and_free_semaphores(nc.allocated_since(known))
            nc.all_engine_barrier()

        with phase() as c:
            E = sb("E", [P, 2, NROT, D], F32, c)
            vec_rows = sb("vec_rows", [NVEC, P], F32, c)
            A = sb("A", [P, 2, NROT, D], F32, c)
            small_in, pool_steps, gens_in, pe_round, dve_round = (
                sem(n, c) for n in ("small_in", "pool_steps", "gens_in", "pe_round", "dve_round"))
            block = c.enter_context(nc.Block())

            small = [(W[n][:], s) for n, s in zip(W_names, W_src)]
            small += [(gw[0][:], f0_gw), (gw[1][:], f1_gw)]
            small += [(gb[0][:], f0_gb.partition_broadcast(P)), (gb[1][:], f1_gb.partition_broadcast(P))]
            small += [(mixb[:], mix_b.partition_broadcast(P))]
            for at, per, srcs in ((0, PER0, (f0_b1, f0_b2, f0_bg, f0_b3)), (FIRST1, PER1, (f1_b1, f1_b2))):
                for src in srcs:
                    for f in range(src.shape[1] // P):
                        small.append((vec_rows[bass.DynSlice(at, N_EXP, per), :], src[:, f * P:(f + 1) * P]))
                        at += 1
            for name, src in (("ln_g", ln_g), ("ln_b", ln_b), ("abel_b", abel_b)):
                small.append((vec_rows[OTHERS[name]:OTHERS[name] + 1, :], src.unsqueeze(0)))
            small.append((vec_rows[OTHERS["mix_a"]:OTHERS["mix_a"] + 2, :], mix_w.rearrange("(a p) o -> a (p o)", p=P)))

            @block.sync
            def _(sp):
                for b in range(BATCH):
                    sp.dma_start(X[:, b * BLK:(b + 1) * BLK, :], x_blocks[b]).then_inc(x_in, 16)
                for dst, src in small[0::2]:
                    sp.dma_start(dst, src).then_inc(small_in, 16)
                sp.wait_ge(small_in, 16 * len(small))

            @block.scalar
            def _(act):
                act.dma_start(E[:, 0], gens.rearrange("g p d -> p g d")).then_inc(gens_in, 16)
                for dst, src in small[1::2]:
                    act.dma_start(dst, src).then_inc(small_in, 16)

            @block.gpsimd
            def _(pool):
                cnt = Count(pool, pool_steps)
                cnt.mark(pool.memset(ident[:], 1.0))
                cnt.mark(pool.memset(mask_q[:], 0.0))
                cnt.mark(pool.memset(mask_k[:], 0.0))
                cnt.mark(pool.memset(eps[:], EPS))
                cnt.mark(pool.memset(ones[:], 1.0))
                cnt.mark(pool.memset(before[:], 1.0))
                cnt.mark(pool.memset(zeros[:], 0.0))
                for e in range(N_EXP):
                    cnt.mark(pool.memset(order[:, e:e + 1], float(N_EXP - e)))
                cnt.settle()
                cnt.mark(pool.affine_select(ident[:], ident[:], [[-1, P]], ALU.is_equal, 0.0, 0, 1))
                cnt.mark(pool.affine_select(mask_q[:], mask_q[:], [[-1, P]], ALU.is_ge, NEG, 0, 1))
                cnt.mark(pool.affine_select(mask_k[:], mask_k[:], [[1, P]], ALU.is_ge, NEG, 0, -1))
                cnt.settle()
                cnt.mark(pool.tensor_copy(identb[:], ident[:]))
                cnt.mark(pool.affine_select(before[:], before[:], [[1, P]], ALU.is_gt, 0.0, 0, -1))
                for k in range(NTILE):
                    cnt.mark(pool.memset(steps_of[:, k:k + 1], float(k * TILE)))
                for k in range(TILES):
                    cnt.mark(pool.memset(tile_index[:, k:k + 1], float(k)))
                for i in range(2):
                    pool.dma_start(x_slots[i].rearrange("(p r) d -> p r d", p=P),
                                   zeros[:].unsqueeze(1).to_broadcast([P, TILES * TILE // P, D])).then_inc(zeroed, 16)
                cnt.settle()

            POOL_READY = 7 + N_EXP + 3

            @block.tensor
            def _(pe):
                pe.wait_ge(pool_steps, POOL_READY)
                pe.wait_ge(dve_round, 1)
                for i in range(NROT):
                    m = pe.transpose(ps[:, 0, i * D:(i + 1) * D], A[:, 0, i, :], ident[:])
                m.then_inc(pe_round, 1)
                for k in range(DEGREE - 1):
                    pe.wait_ge(dve_round, 2 + k)
                    for i in range(NROT):
                        m = pe.matmul(ps[:, 0, i * D:(i + 1) * D], A[:, 1, i, :], E[:, 0, i, :],
                                      start=True, stop=True)
                    m.then_inc(pe_round, 1)
                pe.wait_ge(dve_round, DEGREE + 1)
                for i in range(NROT):
                    m = pe.transpose(ps[:, 1, i * D:(i + 1) * D], E[:, 0, i, :], ident[:])
                m.then_inc(pe_round, 1)
                for k in range(SQUARINGS):
                    pe.wait_ge(dve_round, DEGREE + 2 + k)
                    for i in range(NROT):
                        pe.matmul(ps[:, 0, i * D:(i + 1) * D], E[:, 1, i, :], E[:, 0, i, :],
                                  start=True, stop=True)
                    for i in range(NROT):
                        m = pe.matmul(ps[:, 1, i * D:(i + 1) * D], E[:, 0, i, :], E[:, 1, i, :],
                                      start=True, stop=True)
                    m.then_inc(pe_round, 1)
                for i in range(1, NROT):
                    pe.wait_ge(dve_round, DEGREE + 3 + SQUARINGS + i - 1)
                    pe.matmul(ps[:, 0, 0:D], E[:, 1, 0, :], E[:, 0, i, :], start=True, stop=True)
                    m = pe.matmul(ps[:, 1, 0:D], E[:, 0, i, :], E[:, 1, 0, :], start=True, stop=True)
                    m.then_inc(pe_round, 1)
                pe.wait_ge(small_in, 16 * len(small))
                pe.transpose(ps[:, 2, 0:NVEC], vec_rows[:], ident[0:NVEC, 0:NVEC]).then_inc(pe_round, 1)

            @block.vector
            def _(dve):
                pair = lambda k: ps[:, k, 0:NROT * D].rearrange("p (g d) -> p g d", g=NROT)
                idents = ident[:].unsqueeze(1).to_broadcast([P, NROT, D])
                cnt = Count(dve, dve_round)
                rounds = 0

                def pe_done():
                    dve.wait_ge(pe_round, rounds)

                dve.wait_ge(gens_in, 16)
                cnt.mark(dve.tensor_scalar(A[:, 0], E[:, 0], 2.0 ** -SQUARINGS, None, ALU.mult))
                dve.wait_ge(pool_steps, POOL_READY)
                cnt.settle()
                rounds += 1
                pe_done()
                dve.tensor_copy(A[:, 1], pair(0))
                cnt.mark(dve.scalar_tensor_tensor(E[:, 0], A[:, 0], 1.0 / DEGREE, idents, ALU.mult, ALU.add))
                for k in range(DEGREE - 1, 0, -1):
                    rounds += 1
                    pe_done()
                    if k > 1:
                        cnt.mark(dve.scalar_tensor_tensor(E[:, 0], pair(0), 1.0 / k, idents, ALU.mult, ALU.add))
                    else:
                        cnt.mark(dve.tensor_copy(E[:, 0], pair(0)))
                rounds += 1
                pe_done()
                cnt.mark(dve.tensor_copy(E[:, 1], pair(1)))
                cnt.settle()
                for k in range(SQUARINGS):
                    rounds += 1
                    pe_done()
                    dve.scalar_tensor_tensor(E[:, 0], E[:, 0], 2.0, pair(0), ALU.mult, ALU.add)
                    cnt.mark(dve.scalar_tensor_tensor(E[:, 1], E[:, 1], 2.0, pair(1), ALU.mult, ALU.add))
                    cnt.settle()
                dve.tensor_tensor(E[:, 0], E[:, 0], idents, ALU.add)
                cnt.mark(dve.tensor_tensor(E[:, 1], E[:, 1], idents, ALU.add))
                cnt.settle()
                for i in range(1, NROT):
                    rounds += 1
                    pe_done()
                    dve.tensor_copy(E[:, 0, 0, :], ps[:, 0, 0:D])
                    cnt.mark(dve.tensor_copy(E[:, 1, 0, :], ps[:, 1, 0:D]))
                    cnt.settle()
                dve.tensor_copy(rot[:], E[:, 0, 0, :])
                rounds += 1
                pe_done()
                dve.tensor_copy(vecs[:], ps[:, 2, 0:NVEC])

        with phase() as c:
            xn = sb("xn", [P, BLK, D], F32, c)
            xnt = sb("xnt", [P, T], F32, c)
            qkf = sb("qkf", [P, 2, T], F32, c)
            rest = sb("rest", [P, 2, T], F32, c)
            parts = sb("parts", [P, 3, 2, T], BF16, c)
            vpad = sb("vpad", [P, BLK, HEADS, 32], F32, c)
            stats = sb("stats", [P, BLK, 6], F32, c)
            moments = sb("moments", [P, BLK, 2], F32, c)
            rstd = sb("rstd", [P, BLK], F32, c)
            dev = sb("dev", [P, BLK], F32, c)
            (dve_steps, xn_ready, xt_banks, xnt_ready, xn_copied, v_ready, qk_banks, qk_ready, qkf_free, v_banks,
             g_bank, v_evac, parts_ready, parts_stored, v_stored, vpad_set, g_ready, moments_ready, dev_ready) = (sem(n, c) for n in (
                 "dve_steps", "xn_ready", "xt_banks", "xnt_ready", "xn_copied", "v_ready", "qk_banks", "qk_ready",
                 "qkf_free", "v_banks", "g_bank", "v_evac", "parts_ready", "parts_stored", "v_stored",
                 "vpad_set", "g_ready", "moments_ready", "dev_ready"))
            stats_written = sem("stats_written", c)
            block = c.enter_context(nc.Block())
            HALF = BLK // 2
            STORES = 2 * 3 * GROUPS
            DVE_STEPS = 3 * BLK + 2 + 3

            @block.sync
            def _(sp):
                with sp.Fori(0, BATCH) as b:
                    sp.wait_ge(parts_ready, b + 1)
                    for qk in range(2):
                        for part in range(3):
                            for g in range(GROUPS):
                                dst = qk_parts[qk, bass.ds(b * GROUPS + g, 1), part].squeeze(0)
                                sp.dma_start(dst.rearrange("d h t -> h d t"),
                                             parts[g * 32:(g + 1) * 32, part, qk, :]).then_inc(parts_stored, 16)
                    sp.wait_ge(v_evac, b * 2 + 2)
                    sp.dma_start(v_padded[bass.ds(b, 1)].squeeze(0).rearrange("j p c -> p j c"),
                                 vpad[:].rearrange("p j h c -> p j (h c)")).then_inc(v_stored, 16)
                sp.wait_ge(parts_stored, 16 * STORES * BATCH)
                sp.wait_ge(v_stored, 16 * BATCH)

            @block.gpsimd
            def _(pool):
                pool.memset(vpad[:], 0.0).then_inc(vpad_set, 1)
                pool.wait_ge(vpad_set, 1)
                pool.memset(vpad[:, :, :, HD:HD + 1], 1.0).then_inc(vpad_set, 1)
                with pool.Fori(0, BATCH) as b:
                    pool.wait_ge(xn_ready, b + 1)
                    pool.tensor_copy(XN[:, bass.ds(b * BLK, BLK), :], xn[:]).then_inc(xn_copied, 1)

            @block.tensor
            def _(pe):
                with pe.Fori(0, BATCH) as b:
                    for h in range(2):
                        pe.wait_ge(xn_ready, b + 1)
                        pe.wait_ge(v_banks, b * 2 + h + 1)
                        for j in range(HALF):
                            m = pe.transpose(ps[:, h, j * P:(j + 1) * P], xn[:, h * HALF + j, :], ident[:])
                        m.then_inc(xt_banks, 1)
                    pe.wait_ge(xnt_ready, b * 2 + 2)
                    pe.wait_ge(g_bank, b + 1)
                    for j in range(BLK):
                        m = pe.matmul(ps[:, 6, j * N_EXP:(j + 1) * N_EXP], xnt[:, j * P:(j + 1) * P], gw[0][:],
                                      start=True, stop=True)
                    m.then_inc(g_ready, 1)
                    for qk, w in enumerate((W["wq0"], W["wk0"])):
                        for h in range(2):
                            pe.wait_ge(qk_banks, b * 4 + qk * 2 + h + 1)
                            pe.matmul(ps[:, 2 + qk * 2 + h, :], w[:], xnt[:, h * TILE:(h + 1) * TILE],
                                      start=True, stop=True).then_inc(qk_ready, 1)
                    for h in range(2):
                        for j in range(HALF):
                            m = pe.matmul(ps[:, h, j * P:(j + 1) * P],
                                          xnt[:, (h * HALF + j) * P:(h * HALF + j + 1) * P], W["wv0"][:],
                                          start=True, stop=True)
                        m.then_inc(v_ready, 1)

            @block.scalar
            def _(act):
                act.sem_inc(qk_banks, 4)
                with act.Fori(0, BATCH) as b:
                    act.wait_ge(moments_ready, b + 1)
                    deviation(act, moments, dev, eps).then_inc(dev_ready, 1)
                    for h in range(2):
                        act.wait_ge(xt_banks, b * 2 + h + 1)
                        act.wait_ge(v_banks, b * 2 + 2)
                        act.activation(xnt[:, h * TILE:(h + 1) * TILE], ps[:, h, :], ACT.Copy).then_inc(xnt_ready, 1)
                    for i in range(4):
                        act.wait_ge(qk_ready, b * 4 + i + 1)
                        act.wait_ge(qkf_free, b + 1)
                        act.activation(qkf[:, i // 2, (i % 2) * TILE:(i % 2 + 1) * TILE], ps[:, 2 + i, :],
                                       ACT.Copy, scale=float(HD) ** -0.25).then_inc(qk_banks, 1)

            @block.vector
            def _(dve):
                dve.sem_inc(v_banks, 2)
                dve.sem_inc(g_bank, 1)
                dve.sem_inc(qkf_free, 1)
                dve.wait_ge(x_in, 16 * BATCH)
                dve.wait_ge(vpad_set, 2)
                with dve.Fori(0, BATCH) as b:
                    cnt = Count(dve, dve_steps, b * DVE_STEPS)
                    rows = lambda j: X[:, bass.ds(b * BLK + j, 1), :].squeeze(1)
                    moments_of(dve, cnt, rows, stats, moments, BLK, stats_written)
                    dve.sem_inc(moments_ready, 1)
                    dve.wait_ge(dev_ready, b + 1)
                    scale_rows(dve, cnt, rows, lambda j: xn[:, j, :], moments, dev, rstd, BLK)
                    cnt.settle()
                    dve.sem_inc(xn_ready, 1)
                    dve.wait_ge(g_ready, b + 1)
                    cnt.mark(dve.tensor_tensor(
                        logits[:, bass.ds(b * BLK, BLK), :],
                        ps[:, 6, 0:BLK * N_EXP].rearrange("p (j e) -> p j e", j=BLK),
                        gb[0][:].unsqueeze(1).to_broadcast([P, BLK, N_EXP]), ALU.add))
                    cnt.settle()
                    dve.sem_inc(g_bank, 1)
                    dve.wait_ge(qk_banks, b * 4 + 8)
                    cnt.mark(dve.tensor_copy(parts[:, 0], qkf[:]))
                    cnt.settle()
                    cnt.mark(dve.tensor_tensor(rest[:], qkf[:], parts[:, 0], ALU.subtract))
                    cnt.settle()
                    cnt.mark(dve.tensor_copy(parts[:, 1], rest[:]))
                    cnt.settle()
                    dve.tensor_tensor(parts[:, 2], rest[:], parts[:, 1], ALU.subtract).then_inc(parts_ready, 1)
                    dve.wait_ge(parts_ready, b + 1)
                    dve.sem_inc(qkf_free, 1)
                    for h in range(2):
                        dve.wait_ge(v_ready, b * 2 + h + 1)
                        dve.tensor_copy(vpad[:, h * HALF:(h + 1) * HALF, :, 0:HD],
                                        ps[:, h, :].rearrange("p (j h d) -> p j h d", j=HALF, h=HEADS))\
                            .then_inc(v_evac, 1)
                        dve.wait_ge(v_evac, b * 2 + h + 1)
                        dve.sem_inc(v_banks, 1)
                    dve.wait_ge(parts_stored, b * (16 * STORES) + 16 * STORES)
                    dve.wait_ge(v_stored, b * 16 + 16)
                    dve.wait_ge(xn_copied, b + 1)

        def route(layer):
            with phase() as c:
                one = lambda n, shape, dt=F32: sb(f"{n}{layer}", shape, dt, c)
                grid = [P, NBLK, N_EXP]
                lower, score, member, pos = (one(n, grid) for n in ("lower", "score", "member", "pos"))
                hot = one("hot", [P, 2, NBLK, N_EXP])
                best, rank = one("best", [P, 2, NBLK]), one("rank", [P, NBLK])
                upto = one("upto", [P, N_EXP, NBLK])
                over = one("over", [P, N_EXP, NTILE])
                used, ends, starts = (one(n, [P, N_EXP]) for n in ("used", "ends", "starts"))
                slot_f = one("slot_f", [P, 2, NBLK])
                passed, owner = one("passed", [P, TILES, N_EXP]), one("owner", [P, TILES])
                dve_steps, gap_ready, exp_ready, member_ready, counted = (
                    sem(f"{n}{layer}", c) for n in ("dve_steps_r", "gap_ready", "exp_ready", "member_ready",
                                                    "counted"))
                block = c.enter_context(nc.Block())
                CELLS = NBLK * N_EXP

                @block.scalar
                def _(act):
                    act.wait_ge(gap_ready, 1)
                    act.activation(rank[:], rank[:], ACT.Exp).then_inc(exp_ready, 1)

                @block.tensor
                def _(pe):
                    pe.wait_ge(member_ready, 1)
                    rows = member[:].rearrange("p n e -> p (n e)")
                    pe.matmul(ps[:, 0, 0:CELLS], before[:], rows, start=True, stop=True)
                    pe.matmul(ps[:, 0, CELLS:2 * CELLS], ones[:], rows, start=True, stop=True).then_inc(counted, 1)

                @block.vector
                def _(dve):
                    cnt = Count(dve, dve_steps)

                    def step(ins):
                        cnt.mark(ins)
                        cnt.settle()

                    def spread(ap, axis, shape):
                        return ap.unsqueeze(axis).to_broadcast(shape)

                    top2_choices(dve, cnt, logits[:], lower[:], hot[:], score[:], best[:], rank[:], order[:],
                                 NBLK, N_EXP)
                    cnt.settle()
                    dve.sem_inc(gap_ready, 1)
                    dve.tensor_tensor(member[:], hot[:, 0], hot[:, 1], ALU.add).then_inc(member_ready, 1)
                    dve.wait_ge(exp_ready, 1)
                    step(dve.tensor_scalar(best[:, 0, :], rank[:], 1.0, None, ALU.add))
                    step(dve.reciprocal(share[:, 0, :], best[:, 0, :]))
                    cnt.mark(dve.tensor_tensor(share[:, 1, :], share[:, 0, :], rank[:], ALU.mult))

                    dve.wait_ge(counted, 1)
                    within = ps[:, 0, 0:CELLS].rearrange("p (n e) -> p n e", n=NBLK)
                    total = ps[:, 0, CELLS:2 * CELLS].rearrange("p (n e) -> p n e", n=NBLK)
                    for e in range(N_EXP):
                        cnt.mark(dve.tensor_tensor_scan(upto[:, e, :], ones[:, 0:NBLK], total[:, :, e], 0.0,
                                                        ALU.mult, ALU.add))
                    cnt.settle()
                    cnt.mark(dve.tensor_tensor(pos[:], upto[:].rearrange("p e n -> p n e"), total, ALU.subtract))
                    shape = [P, N_EXP, NTILE]
                    step(dve.tensor_tensor(over[:], spread(upto[:, :, NBLK - 1], 2, shape),
                                           spread(steps_of[:], 1, shape), ALU.is_gt))
                    cnt.mark(dve.tensor_tensor(pos[:], pos[:], within, ALU.add))
                    step(dve.tensor_reduce(used[:], over[:], AX.X, ALU.add))
                    step(dve.tensor_tensor_scan(ends[:], ones[:, 0:N_EXP], used[:], 0.0, ALU.mult, ALU.add))
                    step(dve.tensor_tensor(starts[:], ends[:], used[:], ALU.subtract))
                    step(dve.scalar_tensor_tensor(pos[:], spread(starts[:], 1, grid), float(TILE), pos[:],
                                                  ALU.mult, ALU.add))
                    for k in range(2):
                        step(dve.tensor_tensor(score[:], hot[:, k], pos[:], ALU.mult))
                        step(dve.tensor_reduce(slot_f[:, k, :], score[:], AX.X, ALU.add))
                    cnt.mark(dve.tensor_copy(slot_of[:], slot_f[:]))
                    shape = [P, TILES, N_EXP]
                    step(dve.tensor_tensor(passed[:], spread(ends[:], 1, shape), spread(tile_index[:], 2, shape),
                                           ALU.is_le))
                    step(dve.tensor_reduce(owner[:], passed[:], AX.X, ALU.add))
                    step(dve.tensor_scalar(tile_expert[:], owner[:], float(N_EXP - 1), None, ALU.min))

        def scatter_rows(pool, layer, scattered):
            pool.wait_ge(zeroed, 32)
            for k in range(2):
                for n in range(NBLK):
                    pool.indirect_dma_start(
                        x_slots[layer], bass.IndirectOffsetOnAxis(ap=slot_of[:, k, n:n + 1], axis=0),
                        XN[:, n, :], None, bounds_check=TILES * TILE - 1).then_inc(scattered, 16)

        def gather_rows(pool, layer, dst, gathered, picked):
            per = 2 * TILE // P
            for t in range(NTILE + 1):
                if t < NTILE:
                    for k in range(2):
                        for n in range(t * TILE // P, (t + 1) * TILE // P):
                            pool.indirect_dma_start(
                                dst[:, k, n, :], None, y_slots[layer],
                                bass.IndirectOffsetOnAxis(ap=slot_of[:, k, n:n + 1], axis=0),
                                bounds_check=TILES * TILE - 1).then_inc(gathered[t % 2], 16)
                if t > 0:
                    pool.wait_ge(gathered[(t - 1) % 2], ((t - 1) // 2 + 1) * 16 * per)
                    pool.sem_inc(picked, 1)

        route(0)

        with phase() as c:
            NU = BATCH * GROUPS
            qs = [sb(f"qs{g}", [P, GH, T], BF16, c) for g in range(GROUPS)]
            ks = [sb(f"ks{g}", [P, GH, T], BF16, c) for g in range(GROUPS)]
            vs = [sb(f"vs{g}", [P, BLK, GH * 32], F32, c) for g in range(GROUPS)]
            probs = sb("probs", [P, 2, GH, TILE], F32, c)
            o_sb = sb("o_sb", [P, TILE], F32, c)
            maxima = sb("maxima", [P, 2, GH, BLK + BLK // 2], F32, c)
            shift = sb("shift", [P, 3, GH, BLK], BF16, c)
            shift_rest = sb("shift_rest", [P, GH, BLK], F32, c)
            shift_t = sb("shift_t", [3 * GH * BLK, P], BF16, c)
            sums = sb("sums", [P, 4, GH], F32, c)
            unit_in = [sem(f"unit_in{g}", c) for g in range(GROUPS)]
            (rows_set, rows_steps, rows_clear, score_ready, exp_done, max_ready, max_done, pv_done, o_out, o_turned,
             misc_free, shift_ready, shift_turned, shift_out, shift_in, dve_steps) = (
                sem(n, c) for n in (
                    "rows_set", "rows_steps", "rows_clear", "score_ready", "exp_done", "max_ready", "max_done",
                    "pv_done", "o_out", "o_turned", "misc_free", "shift_ready", "shift_turned", "shift_out",
                    "shift_in", "dve_steps_b"))
            rows_used, scattered = sem("rows_used", c), sem("scattered", c)
            block = c.enter_context(nc.Block())

            CHUNKS = [(h, qb, kt, min(TILE, (qb + 1) * P - kt * TILE))
                      for h in range(GH) for qb in range(BLK) for kt in range(1 + (qb * P) // TILE)]
            NC = len(CHUNKS)
            HALFC = NC // 2
            STEPS = [(qt, kb) for qt in range(2) for kb in range(4 * (qt + 1))]
            NS = len(STEPS)
            work = [4 - max(0, kb - 4 * qt) for qt, kb in STEPS]
            cuts = []
            for first in (0, NS // 2):
                total = sum(work[first:first + NS // 2])
                edges = [HALFC * sum(work[first:first + i]) // total for i in range(NS // 2 + 1)]
                cuts += list(zip(edges, edges[1:]))
            UNIT_LOADS = 16 * 7
            RETURN_STEP, SHIFT_STEP = 5, 7
            DVE_STEPS = 6

            def after(b, g, k):
                return b + (g + k) // GROUPS, (g + k) % GROUPS

            def ahead_of(s, b, g):
                return (*after(b, g, 1), HALFC) if s < NS // 2 else (*after(b, g, 2), 0)

            @block.sync
            def _(sp):
                def load(b, g):
                    u = b * GROUPS + g
                    q_src = qk_parts[0, bass.ds(u, 1)].squeeze(0).rearrange("c d h t -> c d (h t)")
                    k_src = qk_parts[1, bass.ds(u, 1)].squeeze(0).rearrange("c d h t -> (c d) (h t)")
                    for i in range(3):
                        rows = slice(24 * i, 24 * (i + 1))
                        sp.dma_start(qs[g][rows].rearrange("r h t -> r (h t)"),
                                     q_src[i].unsqueeze(0).to_broadcast([3, HD, GH * T])).then_inc(unit_in[g], 16)
                        sp.dma_start(ks[g][rows].rearrange("r h t -> r (h t)"), k_src).then_inc(unit_in[g], 16)
                    v_src = v_padded[bass.ds(b, 1)].squeeze(0).rearrange("j p c -> p j c")
                    sp.dma_start(vs[g][:], v_src[:, :, g * P:(g + 1) * P]).then_inc(unit_in[g], 16)

                def store_shift(b, g):
                    sp.wait_ge(shift_out, b * GROUPS + g + 1)
                    sp.dma_start(qs[g][96:99].rearrange("r h t -> r (h t)"), shift_t[:]).then_inc(shift_in, 16)

                sp.wait_ge(rows_set, 1)
                for g in range(GROUPS):
                    load(0, g)
                store_shift(0, 0)
                with sp.Fori(0, BATCH - 1) as b:
                    for g in range(GROUPS):
                        store_shift(*after(b, g, 1))
                        sp.wait_ge(pv_done, b * (GROUPS * NS) + (g + 1) * NS + 2)
                        load(b + 1, g)
                for g in range(GROUPS - 1):
                    store_shift(BATCH - 1, g + 1)
                sp.wait_ge(shift_in, 16 * NU)

            @block.gpsimd
            def _(pool):
                cnt = Count(pool, rows_steps)
                for g in range(GROUPS):
                    cnt.mark(pool.memset(qs[g][:].bitcast(U32), 0))
                    cnt.mark(pool.memset(ks[g][:].bitcast(U32), 0))
                cnt.settle()
                for g in range(GROUPS):
                    cnt.mark(pool.memset(ks[g][96:99], 1.0))
                cnt.settle()
                pool.sem_inc(rows_set, 1)
                pool.sem_inc(rows_clear, GROUPS)
                scatter_rows(pool, 0, scattered)
                with pool.Fori(0, BATCH - 1) as b:
                    for g in range(GROUPS):
                        pool.wait_ge(pv_done, b * (GROUPS * NS) + (g + 1) * NS + 2)
                        pool.sem_inc(rows_used, 1)
                        pool.memset(qs[g][96:99].bitcast(U32), 0).then_inc(rows_clear, 1)
                pool.wait_ge(scattered, 16 * 2 * NBLK)

            @block.tensor
            def _(pe):
                def loaded(b, g):
                    pe.wait_ge(unit_in[g], b * UNIT_LOADS + UNIT_LOADS)
                    pe.wait_ge(rows_clear, b * GROUPS + g + 1)

                def first_pass(b, g, lo, hi):
                    for i in range(lo, hi):
                        h, qb, kt, w = CHUNKS[i]
                        pe.wait_ge(max_done, b * (GROUPS * NC) + g * NC + i + 1)
                        diagonal = qb * P // TILE == kt
                        dst = ps[:, i % 2, :]
                        m = pe.matmul(dst[:, 0:w], qs[g][:, h, qb * P:(qb + 1) * P],
                                      ks[g][:, h, kt * TILE:kt * TILE + w], start=True, stop=not diagonal)
                        if diagonal:
                            m = pe.matmul(dst[:, w - P:w], identb[:], mask_q[:], start=False, stop=True)
                        m.then_inc(max_ready, 1)

                def turn_shift(b, g, misc_uses):
                    pe.wait_ge(shift_ready, b * GROUPS + g + 1)
                    pe.wait_ge(misc_free, misc_uses)
                    pe.transpose(ps[0:3 * GH * BLK, 7, :].bitcast(BF16)[:, 0:P],
                                 shift[:].rearrange("p c h q -> p (c h q)"), identb[:]).then_inc(shift_turned, 1)

                def turn_output(b, g, qt, misc_uses):
                    pe.wait_ge(o_out, b * (2 * GROUPS) + 2 * g + qt + 2)
                    pe.wait_ge(misc_free, misc_uses)
                    for j in range(4):
                        m = pe.transpose(ps[:, 7, j * P:(j + 1) * P], o_sb[:, j * P:(j + 1) * P], ident[:])
                    m.then_inc(o_turned, 1)

                def scores(b, g, s, pair):
                    qt, kb = STEPS[s]
                    k = 2 * s + pair
                    skip = max(0, kb - 4 * qt) * P
                    pe.wait_ge(exp_done, b * (2 * GROUPS * NS) + 2 * g * NS + k + 1)
                    for i in range(2):
                        h = 2 * pair + i
                        dst = ps[:, 2 + 2 * (k % 2) + i, :]
                        m = pe.matmul(dst[:, 0:TILE - skip], ks[g][:, h, kb * P:(kb + 1) * P],
                                      qs[g][:, h, qt * TILE + skip:(qt + 1) * TILE],
                                      start=True, stop=kb < 4 * qt)
                        if kb >= 4 * qt:
                            m = pe.matmul(dst[:, 0:P], identb[:], mask_k[:], start=False, stop=True)
                    m.then_inc(score_ready, 1)

                def values(b, g, s):
                    qt, kb = STEPS[s]
                    skip = max(0, kb - 4 * qt) * P
                    pe.wait_ge(exp_done, b * (2 * GROUPS * NS) + 2 * g * NS + 2 * s + 4)
                    if kb == 0:
                        pe.wait_ge(o_out, b * (2 * GROUPS) + 2 * g + qt + 1)
                    for h in range(GH):
                        m = pe.matmul(ps[32 * h:32 * (h + 1), 6, skip:TILE], vs[g][:, kb, 32 * h:32 * (h + 1)],
                                      probs[:, s % 2, h, 0:TILE - skip], start=(kb == 0),
                                      stop=(kb == 4 * qt + 3))
                    m.then_inc(pv_done, 1)

                def unit(b, g, has_next=True, has_after=True):
                    u = b * GROUPS + g
                    pe.wait_ge(shift_in, u * 16 + 16)
                    for s in range(NS):
                        lo, hi = cuts[s]
                        mid = (lo + hi) // 2
                        ahead = has_next if s < NS // 2 else has_after
                        bn, gn, off = ahead_of(s, b, g)
                        if s == NS // 2 and ahead:
                            loaded(bn, gn)
                        scores(b, g, s, 0)
                        if ahead:
                            first_pass(bn, gn, off + lo, off + mid)
                        scores(b, g, s, 1)
                        if ahead:
                            first_pass(bn, gn, off + mid, off + hi)
                        if s > 0:
                            values(b, g, s - 1)
                        if s == RETURN_STEP:
                            turn_output(b, g, 0, u * 3 + 2)
                        if s == SHIFT_STEP and has_next:
                            turn_shift(*after(b, g, 1), u * 3 + 3)
                    values(b, g, NS - 1)
                    turn_output(b, g, 1, u * 3 + 3 + has_next)

                pe.sem_inc(pv_done, 2)
                pe.sem_inc(o_turned, 1)
                loaded(0, 0)
                first_pass(0, 0, 0, NC)
                turn_shift(0, 0, 1)
                loaded(0, 1)
                first_pass(0, 1, 0, HALFC)
                with pe.Fori(0, BATCH - 1) as b:
                    for g in range(GROUPS):
                        unit(b, g)
                for g in range(GROUPS):
                    unit(BATCH - 1, g, g + 1 < GROUPS, g + 2 < GROUPS)

            @block.scalar
            def _(act):
                def unit(b, g):
                    u = b * GROUPS + g
                    for s, (qt, kb) in enumerate(STEPS):
                        w = TILE - max(0, kb - 4 * qt) * P
                        act.wait_ge(pv_done, u * NS + s + 1)
                        for pair in range(2):
                            k = 2 * s + pair
                            act.wait_ge(score_ready, u * (2 * NS) + k + 1)
                            act.activation(probs[:, s % 2, 2 * pair:2 * pair + 2, 0:w],
                                           ps[:, 2 + 2 * (k % 2):4 + 2 * (k % 2), 0:w], ACT.Exp)\
                                .then_inc(exp_done, 1)
                        if s in (4, NS - 1):
                            q = 0 if s == 4 else 1
                            act.wait_ge(pv_done, u * NS + (4 if q == 0 else NS) + 2)
                            act.wait_ge(o_turned, u * 2 + q + 1)
                            act.activation(o_sb[:], ps[:, 6, :], ACT.Copy).then_inc(o_out, 1)

                act.sem_inc(exp_done, 2)
                act.sem_inc(o_out, 1)
                with act.Fori(0, BATCH) as b:
                    for g in range(GROUPS):
                        unit(b, g)

            @block.vector
            def _(dve):
                def reduce(b, g, lo, hi):
                    for i in range(lo, hi):
                        h, qb, kt, w = CHUNKS[i]
                        dve.wait_ge(max_ready, b * (GROUPS * NC) + g * NC + i + 1)
                        col = qb if kt == 0 else BLK + qb - 4
                        dve.tensor_reduce(maxima[:, g % 2, h, col:col + 1], ps[:, i % 2, 0:w], AX.X, ALU.max)\
                            .then_inc(max_done, 1)

                def take_output(cnt, b, g, qt):
                    dve.wait_ge(o_turned, b * (2 * GROUPS) + 2 * g + qt + 2)
                    o = ps[:, 7, :].rearrange("p (q h c) -> p q h c", q=4, h=GH)
                    cnt.mark(dve.reciprocal(sums[:], o[:, :, :, HD]))
                    cnt.settle()
                    blk = b * BLK + 4 * qt
                    dst = ATT[:, bass.ds(blk, 4), g * 32:(g + 1) * 32].rearrange("p q (h d) -> p q h d", h=GH)
                    dve.tensor_tensor(dst, o[:, :, :, 0:HD], sums[:].unsqueeze(3).to_broadcast([P, 4, GH, HD]),
                                      ALU.mult).then_inc(misc_free, 1)

                def make_shift(cnt, b, g):
                    m = maxima[:, g % 2]
                    dve.wait_ge(max_done, b * (GROUPS * NC) + (g + 1) * NC + 2)
                    cnt.mark(dve.tensor_tensor(m[:, :, 4:BLK], m[:, :, 4:BLK], m[:, :, BLK:], ALU.max))
                    cnt.settle()
                    cnt.mark(dve.tensor_scalar(shift[:, 0], m[:, :, 0:BLK], -1.0, None, ALU.mult))
                    cnt.settle()
                    cnt.mark(dve.scalar_tensor_tensor(shift_rest[:], m[:, :, 0:BLK], -1.0, shift[:, 0],
                                                      ALU.mult, ALU.subtract))
                    cnt.settle()
                    cnt.mark(dve.tensor_copy(shift[:, 1], shift_rest[:]))
                    cnt.settle()
                    dve.tensor_tensor(shift[:, 2], shift_rest[:], shift[:, 1], ALU.subtract).then_inc(shift_ready, 1)

                def take_shift(b, g, first=False):
                    u = b * GROUPS + g
                    dve.wait_ge(shift_turned, u + 1)
                    if not first:
                        dve.wait_ge(shift_in, u * 16)
                    dve.tensor_copy(shift_t[:], ps[0:3 * GH * BLK, 7, :].bitcast(BF16)[:, 0:P]).then_inc(shift_out, 1)
                    dve.wait_ge(shift_out, u + 1)
                    dve.sem_inc(misc_free, 1)

                def unit(b, g, has_next=True, has_after=True):
                    cnt = Count(dve, dve_steps, b * (GROUPS * DVE_STEPS) + (g + 1) * DVE_STEPS)
                    for s in range(NS):
                        lo, hi = cuts[s]
                        bn, gn, off = ahead_of(s, b, g)
                        if has_next if s < NS // 2 else has_after:
                            reduce(bn, gn, off + lo, off + hi)
                        if s == RETURN_STEP:
                            take_output(cnt, b, g, 0)
                            if has_next:
                                make_shift(cnt, *after(b, g, 1))
                        if s == SHIFT_STEP and has_next:
                            take_shift(*after(b, g, 1))
                    take_output(cnt, b, g, 1)
                    assert cnt.n == (DVE_STEPS if has_next else 2)

                dve.sem_inc(max_done, 2)
                dve.sem_inc(misc_free, 1)
                dve.sem_inc(dve_steps, DVE_STEPS - 4)
                reduce(0, 0, 0, NC)
                make_shift(Count(dve, dve_steps, DVE_STEPS - 4), 0, 0)
                take_shift(0, 0, first=True)
                reduce(0, 1, 0, HALFC)
                with dve.Fori(0, BATCH - 1) as b:
                    for g in range(GROUPS):
                        unit(b, g)
                for g in range(GROUPS):
                    unit(BATCH - 1, g, g + 1 < GROUPS, g + 2 < GROUPS)

        QT = TILE // P

        def tile_traffic(sp, layer, loads, used, y_out, y_sb, y_stored, sp_steps):
            early, middle, late = loads
            turns = (TILES - 2) // 2

            def wait(sem, count):
                sp.wait_ge(sem, count)
                sp.sem_inc(sp_steps, 1)

            def load(group, s, slot, wait=lambda: None):
                e = sp.value_load(tile_expert[0:1, bass.ds(s, 1)], min_val=0, max_val=N_EXP - 1)
                wait()
                rows = x_slots[layer][bass.ds(s * TILE, TILE), :].rearrange("(j p) d -> p j d", p=P)
                tensors, loaded = group
                for dst, src in tensors(e, slot, rows):
                    sp.dma_start(dst, src).then_inc(loaded[slot], 16)

            def store(s, slot):
                wait(y_out, s + 2)
                sp.dma_start(y_slots[layer][bass.ds(s * TILE, TILE), :].rearrange("(j p) d -> p j d", p=P),
                             y_sb[:, slot]).then_inc(y_stored[slot], 16)

            def step(s, slot, has_last=True, more=True):
                if more:
                    load(early, s + 2, slot, lambda: wait(*used[0](s)))
                if has_last:
                    store(s - 1, 1 - slot)
                    if more or s + 1 < TILES:
                        load(late, s + 1, 1 - slot)
                if more:
                    load(middle, s + 2, slot, lambda: wait(*used[1](s)))

            for slot in range(2):
                sp.sem_inc(y_stored[slot], 16)
                for group in loads:
                    load(group, slot, slot)
            step(0, 0, has_last=False)
            with sp.Fori(0, turns) as i:
                for j in (1, 2):
                    step(i * 2 + j, j % 2)
            for s in range(2 * turns + 1, TILES):
                step(s, s % 2, more=False)
            store(TILES - 1, (TILES - 1) % 2)
            for slot in range(2):
                sp.wait_ge(y_stored[slot], 16 * ((TILES + 1 - slot) // 2) + 16)

        def pipeline(eng, count, ahead, now, behind=None, first=None):
            def step(s, slot, has_last=True, has_next=True):
                if first and has_next:
                    first(s + 1, 1 - slot)
                if behind and has_last:
                    behind(s - 1, 1 - slot)
                if has_next:
                    ahead(s + 1, 1 - slot)
                now(s, slot)

            if first:
                first(0, 0)
            ahead(0, 0)
            step(0, 0, has_last=False)
            turns = (count - 2) // 2
            with eng.Fori(0, turns) as i:
                for j in (1, 2):
                    step(i * 2 + j, j % 2)
            for s in range(2 * turns + 1, count):
                step(s, s % 2, has_next=s + 1 < count)
            if behind:
                behind(count - 1, (count - 1) % 2)

        with phase() as c:
            w12 = sb("w12", [P, 2, 2, F0], F32, c)
            wg = sb("wg", [P, 2, FF0, F0], F32, c)
            w3 = sb("w3", [P, 2, FF0, D], F32, c)
            vec0 = sb("vec0", [P, 2, PER0], F32, c)
            b3 = sb("b3", [P, 2, D], F32, c)
            xs = sb("xs", [P, 2, QT, D], F32, c)
            xt = sb("xt", [P, 2, TILE], F32, c)
            x1 = sb("x1", [P, 2, FF0, TILE], F32, c)
            z = sb("z", [P, 2, FF0, TILE], F32, c)
            act_out = sb("act_out", [P, 2, FF0, TILE], F32, c)
            y = sb("y", [P, 2, QT, D], F32, c)
            rows_in, gate_in, down_in = ([sem(f"{n}{i}_c", c) for i in range(2)]
                                         for n in ("rows_in", "gate_in", "down_in"))
            y_stored = [sem(f"y_stored{i}", c) for i in range(2)]
            (t_ready, xt_ready, x12_ready, x1_ready, z_ready, g_ready, silu_ready, y_ready, y_out) = (
                sem(f"{n}_c", c) for n in ("t_ready", "xt_ready", "x12_ready", "x1_ready", "z_ready", "g_ready",
                                           "silu_ready", "y_ready", "y_out"))
            sp_steps = sem("sp_steps_c", c)
            block = c.enter_context(nc.Block())

            @block.sync
            def _(sp):
                one = lambda ap, e: ap[bass.ds(e, 1)].squeeze(0)
                early = lambda e, slot, rows: (
                    (xs[:, slot], rows), (w12[:, slot, 0], one(f0_w1, e)), (w12[:, slot, 1], one(f0_w2, e)))
                middle = lambda e, slot, rows: (
                    (vec0[:, slot], vecs[:, bass.ds(e * PER0, PER0)]),
                    (wg[:, slot], one(f0_wg, e).rearrange("(f p) g -> p f g", p=P)))
                late = lambda e, slot, rows: (
                    (w3[:, slot], one(f0_w3, e).rearrange("(f p) g -> p f g", p=P)),
                    (b3[:, slot], one(f0_b3, e).partition_broadcast(P)))
                used = (lambda s: (x12_ready, s * FF0 + FF0), lambda s: (silu_ready, s * FF0 + 2 * FF0))
                tile_traffic(sp, 0, ((early, rows_in), (middle, gate_in), (late, down_in)), used, y_out, y, y_stored,
                             sp_steps)

            @block.tensor
            def _(pe):
                def turn(s, slot):
                    pe.wait_ge(rows_in[slot], (s - slot) * 24 + 48)
                    pe.wait_ge(xt_ready, s + 1)
                    for j in range(QT):
                        m = pe.transpose(ps[:, 7, j * P:(j + 1) * P], xs[:, slot, j, :], ident[:])
                    m.then_inc(t_ready, 1)

                def up(s, slot):
                    pe.wait_ge(xt_ready, s + 2)
                    for f in range(FF0):
                        pe.wait_ge(z_ready, s * FF0 + f + 1)
                        for k in range(2):
                            m = pe.matmul(ps[:, 2 * k + f, :], w12[:, slot, k, f * P:(f + 1) * P],
                                          xt[:, slot, :], start=True, stop=True)
                        m.then_inc(x12_ready, 1)

                def gated(s, slot):
                    pe.wait_ge(gate_in[slot], (s - slot) * 16 + 32)
                    pe.wait_ge(z_ready, s * FF0 + 2 * FF0)
                    for go in range(FF0):
                        pe.wait_ge(silu_ready, s * FF0 + go + 1)
                        for f in range(FF0):
                            m = pe.matmul(ps[:, 4 + go, :], wg[:, slot, f, go * P:(go + 1) * P],
                                          z[:, slot, f, :], start=(f == 0), stop=(f == FF0 - 1))
                        m.then_inc(g_ready, 1)

                def down(s, slot):
                    pe.wait_ge(down_in[slot], (s - slot) * 16 + 32)
                    pe.wait_ge(silu_ready, s * FF0 + 2 * FF0)
                    pe.wait_ge(y_out, s + 1)
                    for j in range(QT):
                        for f in range(FF0):
                            m = pe.matmul(ps[:, 6, j * P:(j + 1) * P], act_out[:, slot, f, j * P:(j + 1) * P],
                                          w3[:, slot, f, :], start=(f == 0), stop=(f == FF0 - 1))
                    m.then_inc(y_ready, 1)

                pipeline(pe, TILES, up, gated, behind=down, first=turn)

            @block.scalar
            def _(act):
                def take_rows(s, slot):
                    act.wait_ge(t_ready, s + 1)
                    act.activation(xt[:, slot, :], ps[:, 7, :], ACT.Copy).then_inc(xt_ready, 1)

                def first(s, slot):
                    act.wait_ge(gate_in[slot], (s - slot) * 16 + 32)
                    for f in range(FF0):
                        act.wait_ge(x12_ready, s * FF0 + f + 1)
                        act.activation(x1[:, slot, f, :], ps[:, f, :], ACT.Identity, bias=vec0[:, slot, f:f + 1])\
                            .then_inc(x1_ready, 1)

                def silu(s, slot):
                    for go in range(FF0):
                        act.wait_ge(g_ready, s * FF0 + go + 1)
                        act.activation(act_out[:, slot, go, :], ps[:, 4 + go, :], ACT.Silu,
                                       bias=vec0[:, slot, 2 * FF0 + go:2 * FF0 + go + 1]).then_inc(silu_ready, 1)

                act.sem_inc(xt_ready, 1)
                act.sem_inc(silu_ready, FF0)
                pipeline(act, TILES, first, silu, first=take_rows)

            @block.vector
            def _(dve):
                def product(s, slot):
                    for f in range(FF0):
                        dve.wait_ge(x1_ready, s * FF0 + f + 1)
                        dve.scalar_tensor_tensor(z[:, slot, f, :], ps[:, 2 + f, :],
                                                 vec0[:, slot, FF0 + f:FF0 + f + 1], x1[:, slot, f, :],
                                                 ALU.add, ALU.mult).then_inc(z_ready, 1)

                def result(s, slot):
                    dve.wait_ge(y_ready, s + 1)
                    dve.wait_ge(y_stored[slot], (s - slot) * 8 + 16)
                    dve.tensor_tensor(y[:, slot], ps[:, 6, :].rearrange("p (j d) -> p j d", j=QT),
                                      b3[:, slot].unsqueeze(1).to_broadcast([P, QT, D]), ALU.add).then_inc(y_out, 1)

                dve.sem_inc(z_ready, FF0)
                dve.sem_inc(y_out, 1)
                pipeline(dve, TILES, product, lambda s, slot: None, behind=result)

        XNT = sb("XNT", [P, N], F32)
        XMT = sb("XMT", [P, N], F32)
        picked = sb("picked", [P, 2, NBLK, D], F32)
        with phase() as c:
            att = sb("att", [P, 2, QT, D], F32, c)
            att_t = sb("att_t", [P, TILE], F32, c)
            x1 = sb("x1b", [P, 2, QT, D], F32, c)
            xn = sb("xnb", [P, 2, QT, D], F32, c)
            xm = sb("xmb", [P, 2, QT, D], F32, c)
            xn_t = sb("xn_t", [P, 2, TILE], F32, c)
            xm_t = sb("xm_t", [P, 2, TILE], F32, c)
            stats = sb("stats1", [P, QT, 6], F32, c)
            moments = sb("moments1", [P, QT, 2], F32, c)
            dev = sb("dev1", [P, QT], F32, c)
            rstd = sb("rstd1", [P, QT], F32, c)
            att_in, xn_kept, xm_kept, rows_kept, gathered = (
                [sem(f"{n}{i}_d", c) for i in range(2)]
                for n in ("att_in", "xn_kept", "xm_kept", "rows_kept", "gathered"))
            (rows_picked, att_turned, att_out, wo_ready, x1_out, sum_steps, norm_steps, stats_written, moments_ready,
             dev_ready, xn_ready, xn_turned, xn_out, xm_ready, xm_turned, xm_out, g_ready, g_out) = (
                sem(f"{n}_d", c) for n in (
                    "rows_picked", "att_turned", "att_out", "wo_ready", "x1_out", "sum_steps", "norm_steps",
                    "stats_written", "moments_ready", "dev_ready", "xn_ready", "xn_turned", "xn_out", "xm_ready",
                    "xm_turned", "xm_out", "g_ready", "g_out"))
            sp_steps = sem("sp_steps_d", c)
            block = c.enter_context(nc.Block())
            SUM_STEPS, NORM_STEPS = 1 + 2 * QT, 2 * (3 * QT + 1) + 1

            def tile_blocks(t):
                return bass.ds(t * QT, QT)

            @block.sync
            def _(sp):
                def load(t, slot):
                    sp.dma_start(att[:, slot], ATT[:, tile_blocks(t), :]).then_inc(att_in[slot], 16)

                def keep(t, slot):
                    sp.wait_ge(xn_out, t + 2)
                    sp.dma_start(XNT[:, bass.ds(t * TILE, TILE)], xn_t[:, slot]).then_inc(xn_kept[slot], 16)
                    sp.wait_ge(xm_ready, t + 1)
                    sp.dma_start(XN[:, tile_blocks(t), :], xm[:, slot]).then_inc(rows_kept[slot], 16)
                    sp.wait_ge(xm_out, t + 2)
                    sp.sem_inc(sp_steps, 1)
                    sp.dma_start(XMT[:, bass.ds(t * TILE, TILE)], xm_t[:, slot]).then_inc(xm_kept[slot], 16)

                for slot in range(2):
                    for kept in (xn_kept, xm_kept, rows_kept):
                        sp.sem_inc(kept[slot], 16)
                load(0, 0)
                load(1, 1)
                with sp.Fori(0, NTILE // 2 - 1) as i:
                    for slot in range(2):
                        sp.wait_ge(att_turned, i * 2 + slot + 1)
                        load(i * 2 + slot + 2, slot)
                        keep(i * 2 + slot, slot)
                for t in range(NTILE - 2, NTILE):
                    keep(t, t % 2)
                for slot in range(2):
                    for kept in (xn_kept, xm_kept, rows_kept):
                        sp.wait_ge(kept[slot], 16 * NTILE // 2 + 16)

            @block.gpsimd
            def _(pool):
                gather_rows(pool, 0, picked, gathered, rows_picked)

            @block.tensor
            def _(pe):
                def attention_out(t, slot):
                    pe.wait_ge(att_in[slot], (t - slot) * 8 + 16)
                    pe.wait_ge(att_out, t + 1)
                    for j in range(QT):
                        m = pe.transpose(ps[:, 0, j * P:(j + 1) * P], att[:, slot, j, :], ident[:])
                    m.then_inc(att_turned, 1)
                    pe.wait_ge(att_out, t + 2)
                    pe.wait_ge(x1_out, t + 1)
                    for j in range(QT):
                        m = pe.matmul(ps[:, 1, j * P:(j + 1) * P], att_t[:, j * P:(j + 1) * P], W["wo0"][:],
                                      start=True, stop=True)
                    m.then_inc(wo_ready, 1)

                def norms_turned(t, slot):
                    for src, bank, ready, out_of, turned in ((xn, 2, xn_ready, xn_out, xn_turned),
                                                             (xm, 3, xm_ready, xm_out, xm_turned)):
                        pe.wait_ge(ready, t + 1)
                        pe.wait_ge(out_of, t + 1)
                        for j in range(QT):
                            m = pe.transpose(ps[:, bank, j * P:(j + 1) * P], src[:, slot, j, :], ident[:])
                        m.then_inc(turned, 1)
                    pe.wait_ge(xm_out, t + 2)
                    pe.wait_ge(g_out, t + 1)
                    for j in range(QT):
                        m = pe.matmul(ps[:, 4, j * N_EXP:(j + 1) * N_EXP], xm_t[:, slot, j * P:(j + 1) * P],
                                      gw[1][:], start=True, stop=True)
                    m.then_inc(g_ready, 1)

                pipeline(pe, NTILE, attention_out, norms_turned)

            @block.scalar
            def _(act):
                def take_attention(t, slot):
                    act.wait_ge(att_turned, t + 1)
                    act.activation(att_t[:], ps[:, 0, :], ACT.Copy).then_inc(att_out, 1)

                def norms(t, slot):
                    act.wait_ge(moments_ready, t * 2 + 1)
                    deviation(act, moments, dev, eps).then_inc(dev_ready, 1)
                    act.wait_ge(moments_ready, t * 2 + 2)
                    deviation(act, moments, dev, eps).then_inc(dev_ready, 1)
                    act.wait_ge(xn_turned, t + 1)
                    act.wait_ge(xn_kept[slot], (t - slot) * 8 + 16)
                    act.activation(xn_t[:, slot], ps[:, 2, :], ACT.Copy).then_inc(xn_out, 1)
                    act.wait_ge(xm_turned, t + 1)
                    act.wait_ge(xm_kept[slot], (t - slot) * 8 + 16)
                    act.activation(xm_t[:, slot], ps[:, 3, :], ACT.Identity, scale=vec("ln_g"), bias=vec("ln_b"))\
                        .then_inc(xm_out, 1)

                act.sem_inc(att_out, 1)
                act.sem_inc(xn_out, 1)
                act.sem_inc(xm_out, 1)
                pipeline(act, NTILE, take_attention, norms)

            @block.vector
            def _(dve):
                def first_sum(t, slot):
                    cnt = Count(dve, sum_steps, t * SUM_STEPS)
                    dve.wait_ge(wo_ready, t + 1)
                    cnt.mark(dve.tensor_tensor(x1[:, slot], ps[:, 1, :].rearrange("p (j d) -> p j d", j=QT),
                                               X[:, tile_blocks(t), :], ALU.add))
                    cnt.settle()
                    dve.sem_inc(x1_out, 1)
                    dve.wait_ge(rows_picked, t + 1)
                    for k in range(2):
                        for j in range(QT):
                            n = bass.ds(t * QT + j, 1)
                            cnt.mark(dve.scalar_tensor_tensor(
                                x1[:, slot, j, :], picked[:, k, n, :].squeeze(1), share[:, k, n], x1[:, slot, j, :],
                                ALU.mult, ALU.add))
                        cnt.settle()

                def norms(t, slot):
                    cnt = Count(dve, norm_steps, t * NORM_STEPS)
                    moments_of(dve, cnt, lambda j: x1[:, slot, j, :], stats, moments, QT, stats_written)
                    dve.sem_inc(moments_ready, 1)
                    dve.wait_ge(dev_ready, t * 2 + 1)
                    scale_rows(dve, cnt, lambda j: x1[:, slot, j, :], lambda j: xn[:, slot, j, :], moments, dev,
                               rstd, QT)
                    cnt.settle()
                    dve.sem_inc(xn_ready, 1)
                    moments_of(dve, cnt, lambda j: xn[:, slot, j, :], stats, moments, QT, stats_written)
                    dve.sem_inc(moments_ready, 1)
                    cnt.mark(dve.tensor_tensor(X[:, tile_blocks(t), :], x1[:, slot], xn[:, slot], ALU.add))
                    dve.wait_ge(dev_ready, t * 2 + 2)
                    dve.wait_ge(rows_kept[slot], (t - slot) * 8 + 16)
                    scale_rows(dve, cnt, lambda j: xn[:, slot, j, :], lambda j: xm[:, slot, j, :], moments, dev,
                               rstd, QT)
                    cnt.settle()
                    dve.sem_inc(xm_ready, 1)
                    assert cnt.n == NORM_STEPS

                def gate_logits(t, slot):
                    dve.wait_ge(g_ready, t + 1)
                    dve.tensor_tensor(
                        logits[:, tile_blocks(t), :], ps[:, 4, 0:QT * N_EXP].rearrange("p (j e) -> p j e", j=QT),
                        gb[1][:].unsqueeze(1).to_broadcast([P, QT, N_EXP]), ALU.add).then_inc(g_out, 1)

                dve.sem_inc(x1_out, 1)
                dve.sem_inc(g_out, 1)
                pipeline(dve, NTILE, first_sum, norms, behind=gate_logits)

        route(1)

        with phase() as c:
            xn_b = sb("xn_b", [P, T], F32, c)
            q_t = sb("q_t", [P, T], F32, c)
            k_t = sb("k_t", [P, T], F32, c)
            v = sb("v", [P, BLK, D], F32, c)
            p_sb = sb("p_sb", [P, 2, T], F32, c)
            p_t = sb("p_t", [P, 2, BLK, P], F32, c)
            o_t = sb("o_t", [P, P], F32, c)
            top = sb("top", [P, BLK], F32, c)
            bias = sb("bias", [P, BLK], F32, c)
            den = sb("den", [P, BLK], F32, c)
            rden = sb("rden", [P, BLK], F32, c)
            (slice_in, t_ready, t_out, dve_steps, qk_ready, qk_out, v_ready, v_out, s_ready, bias_ready, p_ready,
             o_ready, o_out, y_ready, y_out, scattered) = (sem(f"{n}_a", c) for n in (
                 "slice_in", "t_ready", "t_out", "dve_steps", "qk_ready", "qk_out", "v_ready", "v_out", "s_ready",
                 "bias_ready", "p_ready", "o_ready", "o_out", "y_ready", "y_out", "scattered"))
            block = c.enter_context(nc.Block())
            SC = float(D) ** -0.5
            HALF = BLK // 2
            T_P = [sum(1 + k // HALF for k in range(qb)) for qb in range(BLK + 1)]
            T_USES = T_P[BLK]
            DVE_STEPS = 2 * BLK

            @block.sync
            def _(sp):
                sp.dma_start(xn_b[:], XNT[:, 0:T]).then_inc(slice_in, 16)
                with sp.Fori(0, BATCH - 1) as b:
                    sp.wait_ge(v_ready, b * 2 + 2)
                    sp.dma_start(xn_b[:], XNT[:, bass.ds(b * T + T, T)]).then_inc(slice_in, 16)

            @block.gpsimd
            def _(pool):
                scatter_rows(pool, 1, scattered)
                pool.wait_ge(scattered, 16 * 2 * NBLK)

            @block.tensor
            def _(pe):
                with pe.Fori(0, BATCH) as b:
                    def turn(n, blocks):
                        pe.wait_ge(t_out, b * T_USES + n + 1)
                        for j, src in enumerate(blocks):
                            m = pe.transpose(ps[:, n % 2, j * P:(j + 1) * P], src, ident[:])
                        m.then_inc(t_ready, 1)

                    for i in range(4):
                        pe.wait_ge(p_ready, b * BLK + 2)
                        pe.matmul(ps[:, 4 + i, :], W["wq1" if i < 2 else "wk1"][:],
                                  XNT[:, bass.ds(b * T + (i % 2) * TILE, TILE)], start=True, stop=True)\
                            .then_inc(qk_ready, 1)
                    pe.wait_ge(slice_in, b * 16 + 16)
                    pe.wait_ge(o_out, b * BLK + 1)
                    pe.wait_ge(y_out, b * BLK + 1)
                    for h in range(2):
                        for j in range(HALF):
                            blk = slice((h * HALF + j) * P, (h * HALF + j + 1) * P)
                            m = pe.matmul(ps[:, 2 + h, j * P:(j + 1) * P], xn_b[:, blk], W["wv1"][:],
                                          start=True, stop=True)
                        m.then_inc(v_ready, 1)
                    pe.wait_ge(qk_out, b * 4 + 4)

                    def scores(qb):
                        bank = 4 + 2 * (qb % 2)
                        if qb >= 2:
                            pe.wait_ge(p_ready, b * BLK + qb + 1)
                        n_keys = (qb + 1) * P
                        for kt in range(1 + qb // 4):
                            w = min(TILE, n_keys - kt * TILE)
                            last = (kt == qb // 4)
                            m = pe.matmul(ps[:, bank + kt, 0:w], q_t[:, qb * P:(qb + 1) * P],
                                          k_t[:, kt * TILE:kt * TILE + w], start=True, stop=not last)
                            if last:
                                m = pe.matmul(ps[:, bank + kt, w - P:w], identb[:], mask_q[:],
                                              start=False, stop=True)
                        m.then_inc(s_ready, 1)

                    def project(qb):
                        pe.wait_ge(o_out, b * BLK + qb + 2)
                        pe.wait_ge(y_out, b * BLK + qb + 1)
                        pe.matmul(ps[:, 3, 0:D], o_t[:], W["wo1"][:], start=True, stop=True).then_inc(y_ready, 1)

                    scores(0)
                    scores(1)
                    pe.wait_ge(v_out, b * 2 + 2)
                    for qb in range(BLK):
                        pe.wait_ge(p_ready, b * BLK + qb + 3)
                        for h in range(1 + qb // HALF):
                            turn(T_P[qb] + h, [p_sb[:, qb % 2, kb * P:(kb + 1) * P]
                                               for kb in range(h * HALF, min((h + 1) * HALF, qb + 1))])
                        if qb + 2 < BLK:
                            scores(qb + 2)
                        pe.wait_ge(t_out, b * T_USES + T_P[qb + 1] + 2)
                        pe.wait_ge(o_out, b * BLK + qb + 1)
                        for kb in range(qb + 1):
                            m = pe.matmul(ps[:, 2, 0:P], v[:, kb, :], p_t[:, qb % 2, kb, :],
                                          start=(kb == 0), stop=(kb == qb))
                        m.then_inc(o_ready, 1)
                        if qb > 0:
                            project(qb - 1)
                    project(BLK - 1)

            @block.scalar
            def _(act):
                act.sem_inc(t_out, 2)
                act.sem_inc(o_out, 1)
                act.sem_inc(p_ready, 2)
                with act.Fori(0, BATCH) as b:
                    for i in range(4):
                        act.wait_ge(qk_ready, b * 4 + i + 1)
                        dst = q_t if i < 2 else k_t
                        act.activation(dst[:, i % 2 * TILE:(i % 2 + 1) * TILE], ps[:, 4 + i, :], ACT.Copy)\
                            .then_inc(qk_out, 1)

                    def exponentials(qb):
                        w = (qb + 1) * P
                        act.wait_ge(bias_ready, b * BLK + qb + 1)
                        src = ps[:, 4 + 2 * (qb % 2):6 + 2 * (qb % 2), :].rearrange("p k c -> p (k c)")[:, 0:w]
                        act.activation(p_sb[:, qb % 2, 0:w], src, ACT.Exp, bias=bias[:, qb:qb + 1], scale=SC,
                                       accum_out=den[:, qb:qb + 1]).then_inc(p_ready, 1)

                    exponentials(0)
                    for qb in range(BLK):
                        if qb + 1 < BLK:
                            exponentials(qb + 1)
                        for h in range(1 + qb // HALF):
                            n = min((h + 1) * HALF, qb + 1) - h * HALF
                            use = T_P[qb] + h
                            act.wait_ge(t_ready, b * T_USES + use + 1)
                            act.activation(p_t[:, qb % 2, h * HALF:h * HALF + n, :],
                                           ps[:, use % 2, 0:n * P].rearrange("p (k q) -> p k q", k=n), ACT.Copy)\
                                .then_inc(t_out, 1)
                        act.wait_ge(o_ready, b * BLK + qb + 1)
                        if qb > 0:
                            act.wait_ge(y_ready, b * BLK + qb)
                        act.activation(o_t[:], ps[:, 2, 0:P], ACT.Copy).then_inc(o_out, 1)

            @block.vector
            def _(dve):
                dve.sem_inc(y_out, 1)
                with dve.Fori(0, BATCH) as b:
                    cnt = Count(dve, dve_steps, b * DVE_STEPS)
                    for h in range(2):
                        dve.wait_ge(v_ready, b * 2 + h + 1)
                        dve.tensor_copy(v[:, h * HALF:(h + 1) * HALF, :],
                                        ps[:, 2 + h, :].rearrange("p (j d) -> p j d", j=HALF)).then_inc(v_out, 1)

                    def maximum(qb):
                        w = (qb + 1) * P
                        dve.wait_ge(s_ready, b * BLK + qb + 1)
                        src = ps[:, 4 + 2 * (qb % 2):6 + 2 * (qb % 2), :].rearrange("p k c -> p (k c)")[:, 0:w]
                        cnt.mark(dve.tensor_reduce(top[:, qb:qb + 1], src, AX.X, ALU.max))
                        cnt.settle()
                        dve.tensor_scalar(bias[:, qb:qb + 1], top[:, qb:qb + 1], -SC, None, ALU.mult)\
                            .then_inc(bias_ready, 1)

                    def finish(qb):
                        dve.wait_ge(y_ready, b * BLK + qb + 1)
                        rows = X[:, bass.ds(b * BLK + qb, 1), :].squeeze(1)
                        dve.scalar_tensor_tensor(rows, ps[:, 3, 0:D], rden[:, qb:qb + 1], rows, ALU.mult, ALU.add)\
                            .then_inc(y_out, 1)

                    maximum(0)
                    maximum(1)
                    for qb in range(BLK):
                        dve.wait_ge(p_ready, b * BLK + qb + 3)
                        cnt.mark(dve.reciprocal(rden[:, qb:qb + 1], den[:, qb:qb + 1]))
                        cnt.settle()
                        if qb + 2 < BLK:
                            maximum(qb + 2)
                        if qb > 0:
                            finish(qb - 1)
                    finish(BLK - 1)
                    assert cnt.n == DVE_STEPS

        with phase() as c:
            u1 = sb("u1", [P, 2, F1], F32, c)
            u2 = sb("u2", [P, 2, FF1, D], F32, c)
            vec1 = sb("vec1", [P, 2, PER1], F32, c)
            b2 = sb("b2", [P, 2, D], F32, c)
            xs = sb("xs1", [P, 2, QT, D], F32, c)
            xt = sb("xt1", [P, 2, TILE], F32, c)
            hid = sb("hid", [P, 2, FF1, TILE], F32, c)
            y = sb("y1", [P, 2, QT, D], F32, c)
            rows_in, vecs_in, down_in, y_stored = ([sem(f"{n}{i}_e", c) for i in range(2)]
                                                   for n in ("rows_in", "vecs_in", "down_in", "y_stored"))
            (t_ready, xt_ready, h_ready, gelu_ready, y_ready, y_out) = (
                sem(f"{n}_e", c) for n in ("t_ready", "xt_ready", "h_ready", "gelu_ready", "y_ready", "y_out"))
            sp_steps = sem("sp_steps_e", c)
            block = c.enter_context(nc.Block())

            @block.sync
            def _(sp):
                one = lambda ap, e: ap[bass.ds(e, 1)].squeeze(0)
                early = lambda e, slot, rows: ((xs[:, slot], rows), (u1[:, slot], one(f1_w1, e)))
                middle = lambda e, slot, rows: ((vec1[:, slot], vecs[:, bass.ds(e * PER1 + FIRST1, PER1)]),)
                late = lambda e, slot, rows: (
                    (u2[:, slot], one(f1_w2, e).rearrange("(f p) g -> p f g", p=P)),
                    (b2[:, slot], one(f1_b2, e).partition_broadcast(P)))
                used = (lambda s: (h_ready, s * FF1 + FF1), lambda s: (gelu_ready, s * FF1 + 2 * FF1))
                tile_traffic(sp, 1, ((early, rows_in), (middle, vecs_in), (late, down_in)), used, y_out, y, y_stored,
                             sp_steps)

            @block.tensor
            def _(pe):
                def turn(s, slot):
                    pe.wait_ge(rows_in[slot], (s - slot) * 16 + 32)
                    pe.wait_ge(xt_ready, s + 1)
                    for j in range(QT):
                        m = pe.transpose(ps[:, 7, j * P:(j + 1) * P], xs[:, slot, j, :], ident[:])
                    m.then_inc(t_ready, 1)

                def up(s, slot):
                    pe.wait_ge(xt_ready, s + 2)
                    for f in range(FF1):
                        pe.wait_ge(gelu_ready, s * FF1 + f + 1)
                        pe.matmul(ps[:, f, :], u1[:, slot, f * P:(f + 1) * P], xt[:, slot, :],
                                  start=True, stop=True).then_inc(h_ready, 1)

                def down(s, slot):
                    pe.wait_ge(down_in[slot], (s - slot) * 16 + 32)
                    pe.wait_ge(gelu_ready, s * FF1 + 2 * FF1)
                    pe.wait_ge(y_out, s + 1)
                    for j in range(QT):
                        for f in range(FF1):
                            m = pe.matmul(ps[:, 6, j * P:(j + 1) * P], hid[:, slot, f, j * P:(j + 1) * P],
                                          u2[:, slot, f, :], start=(f == 0), stop=(f == FF1 - 1))
                    m.then_inc(y_ready, 1)

                pipeline(pe, TILES, up, down, first=turn)

            @block.scalar
            def _(act):
                def take_rows(s, slot):
                    act.wait_ge(t_ready, s + 1)
                    act.activation(xt[:, slot, :], ps[:, 7, :], ACT.Identity, scale=vec("ln_g"), bias=vec("ln_b"))\
                        .then_inc(xt_ready, 1)

                def hidden(s, slot):
                    act.wait_ge(vecs_in[slot], (s - slot) * 8 + 16)
                    for f in range(FF1):
                        act.wait_ge(h_ready, s * FF1 + f + 1)
                        act.activation(hid[:, slot, f, :], ps[:, f, :], ACT.Gelu, bias=vec1[:, slot, f:f + 1])\
                            .then_inc(gelu_ready, 1)

                act.sem_inc(xt_ready, 1)
                act.sem_inc(gelu_ready, FF1)
                pipeline(act, TILES, hidden, lambda s, slot: None, first=take_rows)

            @block.vector
            def _(dve):
                def result(s, slot):
                    dve.wait_ge(y_ready, s + 1)
                    dve.wait_ge(y_stored[slot], (s - slot) * 8 + 16)
                    dve.tensor_tensor(y[:, slot], ps[:, 6, :].rearrange("p (j d) -> p j d", j=QT),
                                      b2[:, slot].unsqueeze(1).to_broadcast([P, QT, D]), ALU.add).then_inc(y_out, 1)

                dve.sem_inc(y_out, 1)
                pipeline(dve, TILES, lambda s, slot: None, result)

        with phase() as c:
            abel = sb("abel", [P, N], F32, c)
            moe = sb("moe", [P, 2, QT, D], F32, c)
            moe_t = sb("moe_t", [P, 2, TILE], F32, c)
            non = sb("non", [P, 2, TILE], F32, c)
            g_sb = sb("g_sb", [P, 2, TILE], F32, c)
            mixed = sb("mixed", [P, 2, TILE], F32, c)
            mix = sb("mix", [P, 2, D], F32, c)
            out_sb = sb("out_sb", [P, 2, QT, D], F32, c)
            gathered, stored = ([sem(f"{n}{i}_f", c) for i in range(2)] for n in ("gathered", "stored"))
            (rows_picked, mix_set, a_ready, abel_ready, abel_kept, moe_steps, moe_ready, moe_turned, moe_out, n_ready,
             non_ready, z_ready, g_ready, mix_steps, mixed_ready, t_ready, out_ready) = (sem(f"{n}_f", c) for n in (
                 "rows_picked", "mix_set", "a_ready", "abel_ready", "abel_kept", "moe_steps", "moe_ready",
                 "moe_turned", "moe_out", "n_ready", "non_ready", "z_ready", "g_ready", "mix_steps", "mixed_ready",
                 "t_ready", "out_ready"))
            block = c.enter_context(nc.Block())
            out_rows = out.rearrange("b (k p) d -> p (b k) d", p=P)
            MOE_STEPS, MIX_STEPS = 2 * QT, 3

            @block.sync
            def _(sp):
                def store(t, slot):
                    sp.wait_ge(out_ready, t + 3)
                    sp.dma_start(out_rows[:, tile_blocks(t), :], out_sb[:, slot]).then_inc(stored[slot], 16)

                for slot in range(2):
                    sp.sem_inc(stored[slot], 16)
                with sp.Fori(0, NTILE // 2) as i:
                    for slot in range(2):
                        store(i * 2 + slot, slot)
                for slot in range(2):
                    sp.wait_ge(stored[slot], 16 * NTILE // 2 + 16)

            @block.gpsimd
            def _(pool):
                gather_rows(pool, 1, picked, gathered, rows_picked)

            @block.tensor
            def _(pe):
                with pe.Fori(0, NTILE // 2) as i:
                    for slot in range(2):
                        t = i * 2 + slot
                        pe.wait_ge(abel_ready, t + 1)
                        pe.matmul(ps[:, slot, :], W["abw"][:], XMT[:, bass.ds(t * TILE, TILE)],
                                  start=True, stop=True).then_inc(a_ready, 1)
                pe.wait_ge(abel_ready, NTILE + 2)
                pe.wait_ge(mix_set, 2)

                def rotated(t, slot):
                    pe.wait_ge(moe_ready, t + 1)
                    pe.wait_ge(moe_out, t + 1)
                    for j in range(QT):
                        m = pe.transpose(ps[:, 0, j * P:(j + 1) * P], moe[:, slot, j, :], ident[:])
                    m.then_inc(moe_turned, 1)
                    pe.wait_ge(moe_out, t + 2)
                    pe.wait_ge(non_ready, t + 1)
                    pe.matmul(ps[:, 2, :], rot[:], moe_t[:, slot, :], start=True, stop=True).then_inc(n_ready, 1)

                def gate(t, slot):
                    pe.wait_ge(g_ready, t + 1)
                    pe.matmul(ps[:, 4 + slot, :], mix[:, 0, :], abel[:, bass.ds(t * TILE, TILE)],
                              start=True, stop=False)
                    pe.wait_ge(non_ready, t + 2)
                    pe.matmul(ps[:, 4 + slot, :], mix[:, 1, :], non[:, slot, :], start=False, stop=True)\
                        .then_inc(z_ready, 1)

                def back(t, slot):
                    pe.wait_ge(mixed_ready, t + 1)
                    pe.wait_ge(out_ready, t + 1)
                    for j in range(QT):
                        m = pe.transpose(ps[:, 6 + slot, j * P:(j + 1) * P], mixed[:, slot, j * P:(j + 1) * P],
                                         ident[:])
                    m.then_inc(t_ready, 1)

                pipeline(pe, NTILE, rotated, gate, behind=back)

            @block.scalar
            def _(act):
                act.sem_inc(abel_ready, 2)
                act.sem_inc(moe_out, 1)
                act.sem_inc(g_ready, 2)
                with act.Fori(0, NTILE // 2) as i:
                    for slot in range(2):
                        t = i * 2 + slot
                        act.wait_ge(a_ready, t + 1)
                        act.sem_inc(abel_kept, 1)
                        act.activation(abel[:, bass.ds(t * TILE, TILE)], ps[:, slot, :], ACT.Gelu,
                                       bias=vec("abel_b")).then_inc(abel_ready, 1)

                def take_moe(t, slot):
                    act.wait_ge(moe_turned, t + 1)
                    act.activation(moe_t[:, slot], ps[:, 0, :], ACT.Copy).then_inc(moe_out, 1)

                def gate(t, slot):
                    act.wait_ge(z_ready, t + 1)
                    act.activation(g_sb[:, slot], ps[:, 4 + slot, :], ACT.Sigmoid, bias=mixb[:]).then_inc(g_ready, 1)

                pipeline(act, NTILE, take_moe, gate)

            @block.vector
            def _(dve):
                dve.sem_inc(non_ready, 1)
                dve.sem_inc(out_ready, 2)
                for k in range(2):
                    dve.tensor_copy(mix[:, k, :], vec(("mix_a", "mix_b")[k]).to_broadcast([P, D])).then_inc(mix_set, 1)
                dve.wait_ge(abel_ready, NTILE + 2)

                def sum_of_experts(t, slot):
                    cnt = Count(dve, moe_steps, t * MOE_STEPS)
                    dve.wait_ge(rows_picked, t + 1)
                    for k in range(2):
                        for j in range(QT):
                            n = bass.ds(t * QT + j, 1)
                            rows, w = picked[:, k, n, :].squeeze(1), share[:, k, n]
                            if k == 0:
                                cnt.mark(dve.tensor_scalar(moe[:, slot, j, :], rows, w, None, ALU.mult))
                            else:
                                cnt.mark(dve.scalar_tensor_tensor(moe[:, slot, j, :], rows, w, moe[:, slot, j, :],
                                                                  ALU.mult, ALU.add))
                        cnt.settle()
                    dve.sem_inc(moe_ready, 1)
                    dve.wait_ge(n_ready, t + 1)
                    dve.tensor_copy(non[:, slot], ps[:, 2, :]).then_inc(non_ready, 1)

                def mix_branches(t, slot):
                    cnt = Count(dve, mix_steps, t * MIX_STEPS)
                    ab = abel[:, bass.ds(t * TILE, TILE)]
                    dve.wait_ge(non_ready, t + 2)
                    cnt.mark(dve.tensor_tensor(mixed[:, slot], non[:, slot], ab, ALU.subtract))
                    cnt.settle()
                    dve.wait_ge(g_ready, t + 3)
                    cnt.mark(dve.tensor_tensor(mixed[:, slot], mixed[:, slot], g_sb[:, slot], ALU.mult))
                    cnt.settle()
                    cnt.mark(dve.tensor_tensor(mixed[:, slot], mixed[:, slot], ab, ALU.add))
                    cnt.settle()
                    dve.sem_inc(mixed_ready, 1)

                def output(t, slot):
                    dve.wait_ge(t_ready, t + 1)
                    dve.wait_ge(stored[slot], (t - slot) * 8 + 16)
                    dve.tensor_tensor(out_sb[:, slot], ps[:, 6 + slot, :].rearrange("p (j d) -> p j d", d=D),
                                      X[:, tile_blocks(t), :], ALU.add).then_inc(out_ready, 1)

                pipeline(dve, NTILE, sum_of_experts, mix_branches, behind=output)


_INS = ['L0_attn_x', 'L0_attn_Wq', 'L0_attn_Wk', 'L0_attn_Wv', 'L0_attn_Wo', 'L0_ffn_gate_w', 'L0_ffn_gate_b',
        'L0_ffn_w1', 'L0_ffn_b1', 'L0_ffn_w2', 'L0_ffn_b2', 'L0_ffn_wg', 'L0_ffn_bg', 'L0_ffn_w3', 'L0_ffn_b3',
        'L1_attn_Wq', 'L1_attn_Wk', 'L1_attn_Wv', 'L1_attn_Wo', 'L1_ffn_ln_g', 'L1_ffn_ln_b', 'L1_ffn_abel_w',
        'L1_ffn_abel_b', 'L1_ffn_gate_w_moe', 'L1_ffn_gate_b_moe', 'L1_ffn_w1', 'L1_ffn_b1', 'L1_ffn_w2',
        'L1_ffn_b2', 'L1_ffn_gens', 'L1_ffn_mix_w', 'L1_ffn_mix_b']
_OUTS = [((4, 1024, 128), 'float32')]


def kernel(**inputs):
    import numpy as _np
    import concourse.bacc as _bacc
    from concourse import mybir as _mybir
    from concourse.bass_utils import run_bass_kernel_spmd as _run

    nc = _bacc.Bacc("TRN2", target_bir_lowering=False, num_devices=1)
    arrays, args = {}, []
    for name in _INS:
        a = _np.ascontiguousarray(inputs[name])
        arrays[f"in_{name}_dram"] = a
        args.append(nc.dram_tensor(f"in_{name}_dram", a.shape, _mybir.dt.from_np(a.dtype), kind="ExternalInput").ap())
    for i, (shape, dtype) in enumerate(_OUTS):
        dt = _mybir.dt.from_np(_np.dtype(dtype))
        args.append(nc.dram_tensor(f"out_{i}_dram", shape, dt, kind="ExternalOutput").ap())
    two_layers(nc, *args)
    r = _run(nc, [arrays], core_ids=[0])
    got = tuple(r.results[0][f"out_{i}_dram"] for i in range(len(_OUTS)))
    return got[0]
```

```python
from contextlib import ExitStack, contextmanager

import concourse.bass as bass
from concourse import mybir

F32 = mybir.dt.float32
BF16 = mybir.dt.bfloat16
F32R = mybir.dt.float32r
U32 = mybir.dt.uint32
ALU = mybir.AluOpType
ACT = mybir.ActivationFunctionType
AX = mybir.AxisListType

P = 128
NEG = -1.0e30
EPS = 1e-5
TILE = 512
SQUARINGS = 7
DEGREE = 8


class Count:

    def __init__(self, eng, sem, start=0):
        self.eng, self.sem, self.start, self.n = eng, sem, start, 0

    def mark(self, ins):
        self.n += 1
        ins.then_inc(self.sem, 1)

    def settle(self):
        self.eng.wait_ge(self.sem, self.start + self.n)


def moments_of(dve, cnt, src, stats, moments, blocks, stats_written):
    for j in range(blocks):
        cnt.mark(dve.bn_stats(stats[:, j, :], src(j)))
    cnt.settle()
    dve.sem_inc(stats_written, 1)
    for j in range(blocks):
        cnt.mark(dve.bn_aggr(moments[:, j, :], stats[:, j, :]))
    cnt.settle()


def deviation(act, moments, dev, eps):
    return act.activation(dev[:], moments[:, :, 1], ACT.Sqrt, bias=eps[:, 0:1])


def scale_rows(dve, cnt, src, dst, moments, dev, rstd, blocks):
    cnt.mark(dve.reciprocal(rstd[:], dev[:]))
    cnt.settle()
    for j in range(blocks):
        cnt.mark(dve.tensor_scalar(dst(j), src(j), moments[:, j, 0:1], rstd[:, j:j + 1],
                                   ALU.subtract, ALU.mult))


def top2_choices(dve, cnt, logits, lower, hot, score, best, rank, order, n, n_exp):
    wide = [P, n, n_exp]
    bc = lambda ap: ap.unsqueeze(2).to_broadcast(wide)
    ranks = order.unsqueeze(1).to_broadcast(wide)
    for k in range(2):
        src = logits if k == 0 else lower
        cnt.mark(dve.tensor_reduce(best[:, k, :], src, AX.X, ALU.max))
        cnt.settle()
        cnt.mark(dve.tensor_tensor(score, src, bc(best[:, k, :]), ALU.is_equal))
        cnt.settle()
        cnt.mark(dve.tensor_tensor(score, score, ranks, ALU.mult))
        cnt.settle()
        cnt.mark(dve.tensor_reduce(rank, score, AX.X, ALU.max))
        cnt.settle()
        cnt.mark(dve.tensor_tensor(hot[:, k], score, bc(rank), ALU.is_equal))
        cnt.settle()
        if k == 0:
            cnt.mark(dve.scalar_tensor_tensor(lower, hot[:, 0], -3.0e38, logits, ALU.mult, ALU.add))
            cnt.settle()
    cnt.mark(dve.tensor_tensor(rank, best[:, 1, :], best[:, 0, :], ALU.subtract))


def two_layers(nc, x, a0_wq, a0_wk, a0_wv, a0_wo, f0_gw, f0_gb, f0_w1, f0_b1, f0_w2, f0_b2, f0_wg, f0_bg,
               f0_w3, f0_b3, a1_wq, a1_wk, a1_wv, a1_wo, ln_g, ln_b, abel_w, abel_b, f1_gw, f1_gb,
               f1_w1, f1_b1, f1_w2, f1_b2, gens, mix_w, mix_b, out):
    BATCH, T, D = x.shape
    N_EXP, _, F0 = f0_w1.shape
    F1 = f1_w1.shape[2]
    HD = 8
    HEADS = D // HD
    GH = 4
    GROUPS = HEADS // GH
    N = BATCH * T
    NBLK, BLK = N // P, T // P
    NTILE = N // TILE
    QT = TILE // P
    NROT = gens.shape[0]
    assert D == P and HD * 9 + 24 == 96 and GH * HD == 32 and T == 2 * TILE

    dram = lambda name, shape, dt: nc.dram_tensor(name, shape, dt, kind="Internal").ap()
    qk_parts = dram("qk_parts", [2, BATCH * 3 * HD * HEADS * T], BF16)
    v_padded = dram("v_padded", [NBLK, P, HEADS * 32], F32)
    TILES = (2 * N + N_EXP * (TILE - 1)) // TILE
    x_slots = [dram(f"x_slots{i}", [TILES * TILE, D], F32) for i in range(2)]
    y_slots = [dram(f"y_slots{i}", [TILES * TILE, D], F32) for i in range(2)]

    ctx = ExitStack()
    with ctx:
        sb = lambda name, shape, dt, c=ctx: c.enter_context(nc.sbuf_tensor(name, shape, dt))
        sem = lambda name, c=None: nc.alloc_semaphore(name=name)
        ps = ctx.enter_context(nc.psum_tensor("ps", [P, 8, TILE], F32))

        X = sb("X", [P, NBLK, D], F32)
        XN = sb("XN", [P, NBLK, D], F32)
        ATT = sb("ATT", [P, NBLK, D], F32)
        ident = sb("ident", [P, P], F32)
        identb = sb("identb", [P, P], BF16)
        mask_q = sb("mask_q", [P, P], BF16)
        mask_k = sb("mask_k", [P, P], BF16)
        order = sb("order", [P, N_EXP], F32)
        logits = sb("logits", [P, NBLK, N_EXP], F32)
        share = sb("share", [P, 2, NBLK], F32)
        slot_of = sb("slot_of", [P, 2, NBLK], U32)
        tile_expert = sb("tile_expert", [P, TILES], U32)
        before = sb("before", [P, P], F32)
        ones = sb("ones", [P, P], F32)
        zeros = sb("zeros", [P, D], F32)
        steps_of = sb("steps_of", [P, NTILE], F32)
        tile_index = sb("tile_index", [P, TILES], F32)
        W_names = ["wq0", "wk0", "wv0", "wo0", "wq1", "wk1", "wv1", "wo1", "abw"]
        W_src = [a0_wq, a0_wk, a0_wv, a0_wo, a1_wq, a1_wk, a1_wv, a1_wo, abel_w]
        W = {n: sb(n, [P, D], F32) for n in W_names}
        gw = [sb(f"gw{i}", [P, N_EXP], F32) for i in range(2)]
        gb = [sb(f"gb{i}", [P, N_EXP], F32) for i in range(2)]
        FF0, FF1 = F0 // P, F1 // P
        PER0, PER1 = 3 * FF0 + 1, FF1 + 1
        FIRST1 = N_EXP * PER0
        OTHERS = {n: FIRST1 + N_EXP * PER1 + i for i, n in enumerate(("ln_g", "ln_b", "abel_b", "mix_a", "mix_b"))}
        NVEC = max(OTHERS.values()) + 1
        vecs = sb("vecs", [P, NVEC], F32)

        def vec(name):
            return vecs[:, OTHERS[name]:OTHERS[name] + 1]

        mixb = sb("mixb", [P, 1], F32)
        rot = sb("rot", [P, D], F32)
        E = sb("E", [P, 2, NROT, D], F32)
        two_ident = sb("two_ident", [P, P], F32)
        eps = sb("eps", [P, 1], F32)
        x_in = sem("x_in")
        zeroed = sem("zeroed")

        x_blocks = x.rearrange("b (j p) d -> b p j d", p=P)

        ROW_PARTS = 3 * HD * HEADS * T

        def parts_of(qk, start):
            row = qk_parts[qk, bass.ds(start, ROW_PARTS)]
            return row.rearrange("(c d h t) -> c d h t", c=3, d=HD, h=HEADS)

        @contextmanager
        def phase():
            known = nc.snapshot_sems()
            with ExitStack() as c:
                yield c
            nc.clear_and_free_semaphores(nc.allocated_since(known))
            nc.all_engine_barrier()

        def tile_blocks(t):
            return bass.ds(t * QT, QT)

        def steps(eng, count, step):
            step(0, 0, False, True)
            turns = (count - 2) // 2
            with eng.Fori(0, turns) as i:
                for j in (1, 2):
                    step(i * 2 + j, j % 2, True, True)
            for s in range(2 * turns + 1, count):
                step(s, s % 2, True, s + 1 < count)

        def pipeline(eng, count, ahead=None, now=None, behind=None, first=None, last=None):
            def step(s, slot, has_last, has_next):
                for work, at, there in ((first, s + 1, has_next), (behind, s - 1, has_last),
                                        (ahead, s + 1, has_next), (now, s, True), (last, s + 1, has_next)):
                    if work and there:
                        work(at, slot if work is now else 1 - slot)

            for work in (first, ahead, last):
                if work:
                    work(0, 0)
            steps(eng, count, step)
            if behind:
                behind(count - 1, (count - 1) % 2)

        with phase() as c:
            vec_rows = sb("vec_rows", [NVEC, P], F32, c)
            A = sb("A", [P, 2, NROT, D], F32, c)
            small_in, pool_steps, gens_in, pe_round, dve_round = (
                sem(n, c) for n in ("small_in", "pool_steps", "gens_in", "pe_round", "dve_round"))
            block = c.enter_context(nc.Block())

            small = [(W[n][:], s) for n, s in zip(W_names, W_src)]
            small += [(gw[0][:], f0_gw), (gw[1][:], f1_gw)]
            small += [(gb[0][:], f0_gb.partition_broadcast(P)), (gb[1][:], f1_gb.partition_broadcast(P))]
            small += [(mixb[:], mix_b.partition_broadcast(P))]
            for at, per, srcs in ((0, PER0, (f0_b1, f0_b2, f0_bg, f0_b3)), (FIRST1, PER1, (f1_b1, f1_b2))):
                for src in srcs:
                    for f in range(src.shape[1] // P):
                        small.append((vec_rows[bass.DynSlice(at, N_EXP, per), :], src[:, f * P:(f + 1) * P]))
                        at += 1
            for name, src in (("ln_g", ln_g), ("ln_b", ln_b), ("abel_b", abel_b)):
                small.append((vec_rows[OTHERS[name]:OTHERS[name] + 1, :], src.unsqueeze(0)))
            small.append((vec_rows[OTHERS["mix_a"]:OTHERS["mix_a"] + 2, :], mix_w.rearrange("(a p) o -> a (p o)", p=P)))

            @block.sync
            def _(sp):
                for b in range(BATCH):
                    sp.dma_start(X[:, b * BLK:(b + 1) * BLK, :], x_blocks[b]).then_inc(x_in, 16)
                for dst, src in small[0::2]:
                    sp.dma_start(dst, src).then_inc(small_in, 16)
                sp.wait_ge(small_in, 16 * len(small))
                sp.wait_ge(x_in, 16 * BATCH)

            @block.scalar
            def _(act):
                act.dma_start(E[:, 0], gens.rearrange("g p d -> p g d")).then_inc(gens_in, 16)
                for dst, src in small[1::2]:
                    act.dma_start(dst, src).then_inc(small_in, 16)

            @block.gpsimd
            def _(pool):
                cnt = Count(pool, pool_steps)
                cnt.mark(pool.memset(ident[:], 1.0))
                cnt.mark(pool.memset(two_ident[:], 2.0))
                cnt.mark(pool.memset(mask_q[:], 0.0))
                cnt.mark(pool.memset(mask_k[:], 0.0))
                cnt.mark(pool.memset(eps[:], EPS))
                cnt.mark(pool.memset(ones[:], 1.0))
                cnt.mark(pool.memset(before[:], 1.0))
                cnt.mark(pool.memset(zeros[:], 0.0))
                for e in range(N_EXP):
                    cnt.mark(pool.memset(order[:, e:e + 1], float(N_EXP - e)))
                cnt.settle()
                cnt.mark(pool.affine_select(ident[:], ident[:], [[-1, P]], ALU.is_equal, 0.0, 0, 1))
                cnt.mark(pool.affine_select(two_ident[:], two_ident[:], [[-1, P]], ALU.is_equal, 0.0, 0, 1))
                cnt.mark(pool.affine_select(mask_q[:], mask_q[:], [[-1, P]], ALU.is_ge, NEG, 0, 1))
                cnt.mark(pool.affine_select(mask_k[:], mask_k[:], [[1, P]], ALU.is_ge, NEG, 0, -1))
                cnt.settle()
                cnt.mark(pool.tensor_copy(identb[:], ident[:]))
                cnt.mark(pool.affine_select(before[:], before[:], [[1, P]], ALU.is_gt, 0.0, 0, -1))
                for k in range(NTILE):
                    cnt.mark(pool.memset(steps_of[:, k:k + 1], float(k * TILE)))
                for k in range(TILES):
                    cnt.mark(pool.memset(tile_index[:, k:k + 1], float(k)))
                cnt.settle()

            POOL_READY = 8 + N_EXP + 4

            @block.tensor
            def _(pe):
                pe.wait_ge(pool_steps, POOL_READY)
                pe.wait_ge(dve_round, 1)
                for i in range(NROT):
                    m = pe.transpose(ps[:, 0, i * D:(i + 1) * D], A[:, 0, i, :], ident[:])
                m.then_inc(pe_round, 1)
                for k in range(DEGREE - 1):
                    pe.wait_ge(dve_round, 2 + k)
                    for i in range(NROT):
                        m = pe.matmul(ps[:, 0, i * D:(i + 1) * D], A[:, 1, i, :], E[:, 0, i, :],
                                      start=True, stop=True)
                    m.then_inc(pe_round, 1)
                pe.wait_ge(dve_round, DEGREE + 1)
                for i in range(NROT):
                    m = pe.transpose(ps[:, 1, i * D:(i + 1) * D], E[:, 0, i, :], ident[:])
                m.then_inc(pe_round, 1)
                pe.wait_ge(small_in, 16 * len(small))
                pe.transpose(ps[:, 2, 0:NVEC], vec_rows[:], ident[0:NVEC, 0:NVEC]).then_inc(pe_round, 1)

            @block.vector
            def _(dve):
                pair = lambda k: ps[:, k, 0:NROT * D].rearrange("p (g d) -> p g d", g=NROT)
                idents = ident[:].unsqueeze(1).to_broadcast([P, NROT, D])
                cnt = Count(dve, dve_round)
                rounds = 0

                def pe_done():
                    dve.wait_ge(pe_round, rounds)

                dve.wait_ge(gens_in, 16)
                cnt.mark(dve.tensor_scalar(A[:, 0], E[:, 0], 2.0 ** -SQUARINGS, None, ALU.mult))
                dve.wait_ge(pool_steps, POOL_READY)
                cnt.settle()
                rounds += 1
                pe_done()
                dve.tensor_copy(A[:, 1], pair(0))
                cnt.mark(dve.scalar_tensor_tensor(E[:, 0], A[:, 0], 1.0 / DEGREE, idents, ALU.mult, ALU.add))
                for k in range(DEGREE - 1, 0, -1):
                    rounds += 1
                    pe_done()
                    if k > 1:
                        cnt.mark(dve.scalar_tensor_tensor(E[:, 0], pair(0), 1.0 / k, idents, ALU.mult, ALU.add))
                    else:
                        cnt.mark(dve.tensor_copy(E[:, 0], pair(0)))
                rounds += 1
                pe_done()
                cnt.mark(dve.tensor_copy(E[:, 1], pair(1)))
                cnt.settle()
                rounds += 1
                pe_done()
                dve.tensor_copy(vecs[:], ps[:, 2, 0:NVEC])

        with phase() as c:
            xn = sb("xn", [P, 2, QT, D], F32, c)
            xnt = sb("xnt", [P, 2, TILE], F32, c)
            qkf = sb("qkf", [P, 2, 2, TILE], F32, c)
            rest = sb("rest", [P, 2, 2, TILE], F32, c)
            parts = sb("parts", [P, 2, 3, 2, TILE], BF16, c)
            vpad = sb("vpad", [P, 2, QT, HEADS, 32], F32, c)
            stats = sb("stats", [P, QT, 6], F32, c)
            moments = sb("moments", [P, QT, 2], F32, c)
            rstd = sb("rstd", [P, QT], F32, c)
            dev = sb("dev", [P, QT], F32, c)
            parts_stored, v_stored, rows_kept = ([sem(f"{n}{i}", c) for i in range(2)]
                                                 for n in ("parts_stored", "v_stored", "rows_kept"))
            (dve_steps, stats_written, moments_ready, dev_ready, xn_ready, turned, xnt_out, qk_ready, qk_out, v_ready,
             v_out, g_ready, g_out, rest_ready, middle_ready, parts_ready, vpad_set) = (sem(n, c) for n in (
                 "dve_steps", "stats_written", "moments_ready", "dev_ready", "xn_ready", "turned", "xnt_out",
                 "qk_ready", "qk_out", "v_ready", "v_out", "g_ready", "g_out", "rest_ready", "middle_ready",
                 "parts_ready", "vpad_set"))
            block = c.enter_context(nc.Block())
            DVE_STEPS = 3 * QT + 1

            @block.sync
            def _(sp):
                def keep(t, slot):
                    sp.wait_ge(xn_ready, t + 1)
                    sp.dma_start(XN[:, tile_blocks(t), :], xn[:, slot]).then_inc(rows_kept[slot], 16)

                def store(t, slot):
                    sp.wait_ge(v_out, t + 2)
                    sp.dma_start(v_padded[tile_blocks(t)].rearrange("j p c -> p j c"),
                                 vpad[:, slot].rearrange("p j h c -> p j (h c)")).then_inc(v_stored[slot], 16)
                    sp.wait_ge(parts_ready, t + 1)
                    for qk in range(2):
                        dst = parts_of(qk, (t - slot) * (ROW_PARTS // 2))
                        for part in range(3):
                            sp.dma_start(dst[part, :, :, slot * TILE:(slot + 1) * TILE].rearrange("d h t -> h d t"),
                                         parts[:, slot, part, qk, :]).then_inc(parts_stored[slot], 16)

                for slot in range(2):
                    sp.sem_inc(parts_stored[slot], 96)
                    sp.sem_inc(v_stored[slot], 16)
                    sp.sem_inc(rows_kept[slot], 16)
                pipeline(sp, NTILE, first=keep, now=store)
                for slot in range(2):
                    sp.wait_ge(parts_stored[slot], 96 * NTILE // 2 + 96)
                    sp.wait_ge(v_stored[slot], 16 * NTILE // 2 + 16)
                    sp.wait_ge(rows_kept[slot], 16 * NTILE // 2 + 16)

            @block.gpsimd
            def _(pool):
                pool.memset(vpad[:], 0.0).then_inc(vpad_set, 1)
                pool.wait_ge(vpad_set, 1)
                pool.memset(vpad[:, :, :, :, HD:HD + 1], 1.0).then_inc(vpad_set, 1)

            @block.tensor
            def _(pe):
                def turn(t, slot):
                    pe.wait_ge(xn_ready, t + 1)
                    pe.wait_ge(xnt_out, t + 1)
                    for j in range(QT):
                        m = pe.transpose(ps[:, 0, j * P:(j + 1) * P], xn[:, slot, j, :], ident[:])
                    m.then_inc(turned, 1)

                def products(t, slot):
                    pe.wait_ge(xnt_out, t + 2)
                    for qk, w in enumerate((W["wq0"], W["wk0"])):
                        pe.wait_ge(qk_out, t * 2 + qk + 1)
                        pe.matmul(ps[:, 2 + qk, :], w[:], xnt[:, slot], start=True, stop=True).then_inc(qk_ready, 1)
                    for bank, w, width, ready, out_of in ((4, gw[0], N_EXP, g_ready, g_out),
                                                          (1, W["wv0"], D, v_ready, v_out)):
                        pe.wait_ge(out_of, t + 1)
                        for j in range(QT):
                            m = pe.matmul(ps[:, bank, j * width:(j + 1) * width], xnt[:, slot, j * P:(j + 1) * P],
                                          w[:], start=True, stop=True)
                        m.then_inc(ready, 1)

                pipeline(pe, NTILE, now=products, last=turn)

            @block.scalar
            def _(act):
                def root(t, slot):
                    act.wait_ge(moments_ready, t + 1)
                    deviation(act, moments, dev, eps).then_inc(dev_ready, 1)

                def take_rows(t, slot):
                    act.wait_ge(turned, t + 1)
                    act.activation(xnt[:, slot], ps[:, 0, :], ACT.Copy).then_inc(xnt_out, 1)

                def take_products(t, slot):
                    act.wait_ge(parts_stored[slot], (t - slot) * 48 + 96)
                    for qk in range(2):
                        act.wait_ge(qk_ready, t * 2 + qk + 1)
                        for dst in (qkf[:, slot, qk], parts[:, slot, 0, qk]):
                            m = act.activation(dst, ps[:, 2 + qk, :], ACT.Copy, scale=float(HD) ** -0.25)
                        m.then_inc(qk_out, 1)
                    act.wait_ge(v_ready, t + 1)
                    act.wait_ge(v_stored[slot], (t - slot) * 8 + 16)
                    act.wait_ge(vpad_set, 2)
                    act.activation(vpad[:, slot, :, :, 0:HD],
                                   ps[:, 1, :].rearrange("p (j h d) -> p j h d", j=QT, h=HEADS), ACT.Copy)\
                        .then_inc(v_out, 1)

                def middle_part(t, slot):
                    act.wait_ge(rest_ready, t + 1)
                    act.activation(parts[:, slot, 1], rest[:, slot], ACT.Copy).then_inc(middle_ready, 1)

                act.sem_inc(xnt_out, 1)
                act.sem_inc(qk_out, 2)
                act.sem_inc(v_out, 1)
                pipeline(act, NTILE, first=root, behind=middle_part, now=take_products, last=take_rows)

            @block.vector
            def _(dve):
                def normalize(t, slot):
                    cnt = Count(dve, dve_steps, t * DVE_STEPS)
                    rows = lambda j: X[:, bass.ds(t * QT + j, 1), :].squeeze(1)
                    moments_of(dve, cnt, rows, stats, moments, QT, stats_written)
                    dve.sem_inc(moments_ready, 1)
                    dve.wait_ge(dev_ready, t + 1)
                    dve.wait_ge(rows_kept[slot], (t - slot) * 8 + 16)
                    scale_rows(dve, cnt, rows, lambda j: xn[:, slot, j, :], moments, dev, rstd, QT)
                    cnt.settle()
                    dve.sem_inc(xn_ready, 1)

                def take_rest(t, slot):
                    dve.wait_ge(qk_out, t * 2 + 4)
                    dve.tensor_tensor(rest[:, slot], qkf[:, slot], parts[:, slot, 0], ALU.subtract).then_inc(rest_ready, 1)
                    dve.wait_ge(g_ready, t + 1)
                    dve.tensor_tensor(
                        logits[:, tile_blocks(t), :], ps[:, 4, 0:QT * N_EXP].rearrange("p (j e) -> p j e", j=QT),
                        gb[0][:].unsqueeze(1).to_broadcast([P, QT, N_EXP]), ALU.add).then_inc(g_out, 1)

                def low_part(t, slot):
                    dve.wait_ge(middle_ready, t + 1)
                    dve.tensor_tensor(parts[:, slot, 2], rest[:, slot], parts[:, slot, 1], ALU.subtract)\
                        .then_inc(parts_ready, 1)

                dve.sem_inc(g_out, 1)
                pipeline(dve, NTILE, first=normalize, behind=low_part, now=take_rest)

        def squarings(first, end):
            pairs = [ps[:, 1 + k, 0:NROT * D] for k in range(2)]

            def multiply(pe, k, e_ready, e_out):
                if k > first:
                    pe.wait_ge(e_out, k - first)
                if k < SQUARINGS:
                    for out, a, b in ((pairs[0], 1, 0), (pairs[1], 0, 1)):
                        for i in range(NROT):
                            dst = out[:, i * D:(i + 1) * D]
                            pe.matmul(dst, two_ident[:], E[:, b, i, :], start=True, stop=False)
                            if k == SQUARINGS - 1:
                                pe.matmul(dst, ident[:], ident[:], start=False, stop=False)
                            m = pe.matmul(dst, E[:, a, i, :], E[:, b, i, :], start=False, stop=True)
                else:
                    i = k - SQUARINGS + 1
                    pe.matmul(pairs[0][:, 0:D], E[:, 1, 0, :], E[:, 0, i, :], start=True, stop=True)
                    m = pe.matmul(pairs[1][:, 0:D], E[:, 0, i, :], E[:, 1, 0, :], start=True, stop=True)
                m.then_inc(e_ready, 1)

            def take(act, k, e_ready, e_out):
                act.wait_ge(e_ready, k - first + 1)
                if k < SQUARINGS:
                    for j in range(2):
                        m = act.activation(E[:, j], pairs[j].rearrange("p (g d) -> p g d", g=NROT), ACT.Copy)
                elif k < SQUARINGS + NROT - 2:
                    for j in range(2):
                        m = act.activation(E[:, j, 0, :], pairs[j][:, 0:D], ACT.Copy)
                else:
                    m = act.activation(rot[:], pairs[0][:, 0:D], ACT.Copy)
                m.then_inc(e_out, 1)

            return range(first, end), multiply, take

        def route(layer, early, rounds, multiply, take, sync=None, gpsimd=None):
            with phase() as c:
                one = lambda n, shape, dt=F32: sb(f"{n}{layer}", shape, dt, c)
                grid = [P, NBLK, N_EXP]
                lower, score, member, pos = (one(n, grid) for n in ("lower", "score", "member", "pos"))
                hot = one("hot", [P, 2, NBLK, N_EXP])
                best, rank = one("best", [P, 2, NBLK]), one("rank", [P, NBLK])
                upto = one("upto", [P, N_EXP, NBLK])
                over = one("over", [P, N_EXP, NTILE])
                used, ends, starts = (one(n, [P, N_EXP]) for n in ("used", "ends", "starts"))
                slot_f = one("slot_f", [P, 2, NBLK])
                passed, owner = one("passed", [P, TILES, N_EXP]), one("owner", [P, TILES])
                dve_steps, gap_ready, exp_ready, member_ready, counted = (
                    sem(f"{n}{layer}", c) for n in ("dve_steps_r", "gap_ready", "exp_ready", "member_ready",
                                                    "counted"))
                e_ready, e_out = sem(f"e_ready{layer}", c), sem(f"e_out{layer}", c)
                block = c.enter_context(nc.Block())
                if sync:
                    block.sync(sync)
                if gpsimd:
                    block.gpsimd(gpsimd)
                CELLS = NBLK * N_EXP

                @block.scalar
                def _(act):
                    for k in rounds:
                        if k - rounds[0] == early:
                            act.wait_ge(gap_ready, 1)
                            act.activation(rank[:], rank[:], ACT.Exp).then_inc(exp_ready, 1)
                        take(act, k, e_ready, e_out)

                @block.tensor
                def _(pe):
                    for k in rounds:
                        if k - rounds[0] == early:
                            pe.wait_ge(member_ready, 1)
                            rows = member[:].rearrange("p n e -> p (n e)")
                            pe.matmul(ps[:, 0, 0:CELLS], before[:], rows, start=True, stop=True)
                            pe.matmul(ps[:, 0, CELLS:2 * CELLS], ones[:], rows, start=True, stop=True)\
                                .then_inc(counted, 1)
                        multiply(pe, k, e_ready, e_out)

                @block.vector
                def _(dve):
                    cnt = Count(dve, dve_steps)

                    def step(ins):
                        cnt.mark(ins)
                        cnt.settle()

                    def spread(ap, axis, shape):
                        return ap.unsqueeze(axis).to_broadcast(shape)

                    top2_choices(dve, cnt, logits[:], lower[:], hot[:], score[:], best[:], rank[:], order[:],
                                 NBLK, N_EXP)
                    cnt.settle()
                    dve.sem_inc(gap_ready, 1)
                    dve.tensor_tensor(member[:], hot[:, 0], hot[:, 1], ALU.add).then_inc(member_ready, 1)
                    dve.wait_ge(exp_ready, 1)
                    step(dve.tensor_scalar(best[:, 0, :], rank[:], 1.0, None, ALU.add))
                    step(dve.reciprocal(share[:, 0, :], best[:, 0, :]))
                    cnt.mark(dve.tensor_tensor(share[:, 1, :], share[:, 0, :], rank[:], ALU.mult))

                    dve.wait_ge(counted, 1)
                    within = ps[:, 0, 0:CELLS].rearrange("p (n e) -> p n e", n=NBLK)
                    total = ps[:, 0, CELLS:2 * CELLS].rearrange("p (n e) -> p n e", n=NBLK)
                    for e in range(N_EXP):
                        cnt.mark(dve.tensor_tensor_scan(upto[:, e, :], ones[:, 0:NBLK], total[:, :, e], 0.0,
                                                        ALU.mult, ALU.add))
                    cnt.settle()
                    cnt.mark(dve.tensor_tensor(pos[:], upto[:].rearrange("p e n -> p n e"), total, ALU.subtract))
                    shape = [P, N_EXP, NTILE]
                    step(dve.tensor_tensor(over[:], spread(upto[:, :, NBLK - 1], 2, shape),
                                           spread(steps_of[:], 1, shape), ALU.is_gt))
                    cnt.mark(dve.tensor_tensor(pos[:], pos[:], within, ALU.add))
                    step(dve.tensor_reduce(used[:], over[:], AX.X, ALU.add))
                    step(dve.tensor_tensor_scan(ends[:], ones[:, 0:N_EXP], used[:], 0.0, ALU.mult, ALU.add))
                    step(dve.tensor_tensor(starts[:], ends[:], used[:], ALU.subtract))
                    step(dve.scalar_tensor_tensor(pos[:], spread(starts[:], 1, grid), float(TILE), pos[:],
                                                  ALU.mult, ALU.add))
                    for k in range(2):
                        step(dve.tensor_tensor(score[:], hot[:, k], pos[:], ALU.mult))
                        step(dve.tensor_reduce(slot_f[:, k, :], score[:], AX.X, ALU.add))
                    cnt.mark(dve.tensor_copy(slot_of[:], slot_f[:]))
                    shape = [P, TILES, N_EXP]
                    step(dve.tensor_tensor(passed[:], spread(ends[:], 1, shape), spread(tile_index[:], 2, shape),
                                           ALU.is_le))
                    step(dve.tensor_reduce(owner[:], passed[:], AX.X, ALU.add))
                    step(dve.tensor_scalar(tile_expert[:], owner[:], float(N_EXP - 1), None, ALU.min))

        CLEARS = BATCH
        CLEAR_ROWS = TILES * TILE // CLEARS
        assert CLEAR_ROWS % P == 0

        def clear_slots(pool, layer, piece):
            rows = x_slots[layer][bass.ds(piece * CLEAR_ROWS, CLEAR_ROWS), :]
            pool.dma_start(rows.rearrange("(p r) d -> p r d", p=P),
                           zeros[:].unsqueeze(1).to_broadcast([P, CLEAR_ROWS // P, D])).then_inc(zeroed, 16)

        def scatter_rows(pool, layer, scattered, choices=(0, 1), blocks=range(NBLK)):
            pool.wait_ge(zeroed, 16 * CLEARS * (layer + 1))
            for k in choices:
                for n in blocks:
                    pool.indirect_dma_start(
                        x_slots[layer], bass.IndirectOffsetOnAxis(ap=slot_of[:, k, n:n + 1], axis=0),
                        XN[:, n, :], None, bounds_check=TILES * TILE - 1).then_inc(scattered, 16)

        def gather_rows(pool, layer, dst, gathered, picked):
            per = 2 * TILE // P
            for t in range(NTILE + 1):
                if t < NTILE:
                    for k in range(2):
                        for n in range(t * TILE // P, (t + 1) * TILE // P):
                            pool.indirect_dma_start(
                                dst[:, k, n, :], None, y_slots[layer],
                                bass.IndirectOffsetOnAxis(ap=slot_of[:, k, n:n + 1], axis=0),
                                bounds_check=TILES * TILE - 1).then_inc(gathered[t % 2], 16)
                if t > 0:
                    pool.wait_ge(gathered[(t - 1) % 2], ((t - 1) // 2 + 1) * 16 * per)
                    pool.sem_inc(picked, 1)

        with phase() as c:
            NU = BATCH * GROUPS
            UNIT_LOADS = 16 * 7
            qs = [sb(f"qs{g}", [P, GH, T], BF16, c) for g in range(GROUPS)]
            ks = [sb(f"ks{g}", [P, GH, T], BF16, c) for g in range(GROUPS)]
            vs = [sb(f"vs{g}", [P, BLK, GH * 32], F32, c) for g in range(GROUPS)]
            probs = sb("probs", [P, 2, GH, TILE], F32, c)
            o_sb = sb("o_sb", [P, TILE], F32, c)
            maxima = sb("maxima", [P, 2, GH, BLK + BLK // 2], F32, c)
            shift = sb("shift", [P, 3, GH, BLK], BF16, c)
            shift_rest = sb("shift_rest", [P, GH, BLK], F32, c)
            shift_t = sb("shift_t", [3 * GH * BLK, P], BF16, c)
            sums = sb("sums", [P, 2, 4, GH], F32, c)
            unit_in = [sem(f"unit_in{g}", c) for g in range(GROUPS)]
            rows_set, rows_steps = sem("rows_set", c), sem("rows_steps", c)

            def load(sp, b, g):
                heads = slice(g * GH, (g + 1) * GH)
                q_src = parts_of(0, b * ROW_PARTS)[:, :, heads].rearrange("c d h t -> c d (h t)")
                k_src = parts_of(1, b * ROW_PARTS)[:, :, heads].rearrange("c d h t -> (c d) (h t)")
                for i in range(3):
                    rows = slice(24 * i, 24 * (i + 1))
                    sp.dma_start(qs[g][rows].rearrange("r h t -> r (h t)"),
                                 q_src[i].unsqueeze(0).to_broadcast([3, HD, GH * T])).then_inc(unit_in[g], 16)
                    sp.dma_start(ks[g][rows].rearrange("r h t -> r (h t)"), k_src).then_inc(unit_in[g], 16)
                v_src = v_padded[bass.ds(b * BLK, BLK)].rearrange("j p c -> p j c")
                sp.dma_start(vs[g][:], v_src[:, :, g * P:(g + 1) * P]).then_inc(unit_in[g], 16)

            def first_loads(sp, groups):
                for g in groups:
                    sp.wait_ge(rows_set, g + 1)
                    load(sp, 0, g)

            TWO_ONES = 0x3F803F80

            def set_rows(pool, groups):
                cnt = Count(pool, rows_steps, 3 * groups[0])
                for g in groups:
                    cnt.mark(pool.memset(qs[g][64:P].bitcast(U32), 0))
                    cnt.mark(pool.memset(ks[g][64:P].bitcast(U32), 0))
                    cnt.settle()
                    cnt.mark(pool.memset(ks[g][96:99].bitcast(U32), TWO_ONES))
                    cnt.settle()
                    pool.sem_inc(rows_set, 1)

            route(0, 1, *squarings(0, 4), sync=lambda sp: first_loads(sp, (0, 1)),
                  gpsimd=lambda pool: set_rows(pool, (0, 1)))

            (rows_clear, score_ready, exp_done, max_ready, bank_free, pv_done, o_out, o_turned,
             shift_ready, shift_turned, shift_out, shift_in, dve_steps) = (
                sem(n, c) for n in (
                    "rows_clear", "score_ready", "exp_done", "max_ready", "bank_free",
                    "pv_done", "o_out", "o_turned", "shift_ready", "shift_turned", "shift_out",
                    "shift_in", "dve_steps_b"))
            rows_used, scattered = sem("rows_used", c), sem("scattered", c)
            block = c.enter_context(nc.Block())

            CHUNKS = [(h, qb, kt, min(TILE, (qb + 1) * P - kt * TILE))
                      for h in range(GH) for qb in range(BLK) for kt in range(1 + (qb * P) // TILE)]
            NC = len(CHUNKS)
            HALFC = NC // 2
            STEPS = [(qt, kb) for qt in range(2) for kb in range(4 * (qt + 1))]
            NS = len(STEPS)
            LAST_RETURN_STEP, RETURN_STEP, SHIFT_STEP = 1, 5, 7
            work = [4 - max(0, kb - 4 * qt) for qt, kb in STEPS]
            cuts = []
            for first in (0, NS // 2):
                total = sum(work[first:first + NS // 2])
                edges = [HALFC * sum(work[first:first + i]) // total for i in range(NS // 2 + 1)]
                cuts += [[lo + i * (hi - lo) // 4 for i in range(5)] for lo, hi in zip(edges, edges[1:])]
            DVE_STEPS = 6

            BANKS = (0, 1, 7)
            FIRST_USES = NC + 1 + HALFC
            USES = NC + 3
            assert USES % 3 == 0

            class Uses:
                def __init__(self, n):
                    self.n, self.local = n, FIRST_USES % 3

                def take(self):
                    n, bank = self.n, BANKS[(self.n if isinstance(self.n, int) else self.local) % 3]
                    self.n, self.local = self.n + 1, self.local + 1
                    return n, bank

            def uses_of(b, g, has_last=True, missing=0):
                return Uses(b * (GROUPS * USES) + g * USES + FIRST_USES + (not has_last) - missing)
            def after(b, g, k):
                return b + (g + k) // GROUPS, (g + k) % GROUPS

            ends = {g: {"has_next": g + 1 < GROUPS, "has_after": g + 2 < GROUPS,
                        "missing": HALFC * (g + 1 == GROUPS)} for g in range(1, GROUPS)}

            def before_unit(b, g):
                return (b, g - 1) if g else (b - 1, GROUPS - 1)

            def ahead_of(s, b, g):
                return (*after(b, g, 1), HALFC) if s < NS // 2 else (*after(b, g, 2), 0)

            @block.sync
            def _(sp):
                def store_shift(b, g):
                    sp.wait_ge(shift_out, b * GROUPS + g + 1)
                    sp.dma_start(qs[g][96:99].rearrange("r h t -> r (h t)"), shift_t[:]).then_inc(shift_in, 16)

                first_loads(sp, (2, 3))
                store_shift(0, 0)
                with sp.Fori(0, BATCH - 1) as b:
                    for g in range(GROUPS):
                        store_shift(*after(b, g, 1))
                        sp.wait_ge(pv_done, b * (GROUPS * NS) + (g + 1) * NS + 2)
                        load(sp, b + 1, g)
                for g in range(GROUPS - 1):
                    store_shift(BATCH - 1, g + 1)
                sp.wait_ge(shift_in, 16 * NU)

            @block.gpsimd
            def _(pool):
                pool.sem_inc(rows_clear, 2)
                set_rows(pool, (2, 3))
                pool.sem_inc(rows_clear, 2)
                pool.wait_ge(shift_in, 16)
                for piece in range(CLEARS):
                    clear_slots(pool, 0, piece)
                scatter_rows(pool, 0, scattered, (0,))

                def clear_shifts(b, g):
                    pool.wait_ge(pv_done, b * (GROUPS * NS) + (g + 1) * NS + 2)
                    pool.sem_inc(rows_used, 1)
                    pool.memset(qs[g][96:99].bitcast(U32), 0).then_inc(rows_clear, 1)

                clear_shifts(0, 0)
                scatter_rows(pool, 0, scattered, (1,), range(NBLK // 2))
                clear_shifts(0, 1)
                scatter_rows(pool, 0, scattered, (1,), range(NBLK // 2, NBLK))
                clear_shifts(0, 2)
                clear_shifts(0, 3)
                clear_slots(pool, 1, 0)
                clear_slots(pool, 1, BATCH - 1)
                with pool.Fori(1, BATCH - 1) as b:
                    clear_slots(pool, 1, b)
                    for g in range(GROUPS):
                        clear_shifts(b, g)
                pool.wait_ge(scattered, 16 * 2 * NBLK)

            @block.tensor
            def _(pe):
                def loaded(b, g):
                    pe.wait_ge(unit_in[g], b * UNIT_LOADS + UNIT_LOADS)
                    pe.wait_ge(rows_clear, b * GROUPS + g + 1)

                def first_pass(uses, b, g, lo, hi):
                    for i in range(lo, hi):
                        h, qb, kt, w = CHUNKS[i]
                        n, bank = uses.take()
                        pe.wait_ge(bank_free, n + 1)
                        diagonal = qb * P // TILE == kt
                        dst = ps[:, bank, :]
                        m = pe.matmul(dst[:, 0:w], qs[g][:, h, qb * P:(qb + 1) * P],
                                      ks[g][:, h, kt * TILE:kt * TILE + w], start=True, stop=not diagonal)
                        if diagonal:
                            m = pe.matmul(dst[:, w - P:w], identb[:], mask_q[:], start=False, stop=True)
                        m.then_inc(max_ready, 1)

                def turn_shift(uses, b, g):
                    n, bank = uses.take()
                    pe.wait_ge(shift_ready, b * GROUPS + g + 1)
                    pe.wait_ge(bank_free, n + 1)
                    pe.transpose(ps[0:3 * GH * BLK, bank, :].bitcast(BF16)[:, 0:P],
                                 shift[:].rearrange("p c h q -> p (c h q)"), identb[:]).then_inc(shift_turned, 1)

                def turn_output(uses, b, g, qt):
                    n, bank = uses.take()
                    pe.wait_ge(o_out, b * (2 * GROUPS) + 2 * g + qt + 2)
                    pe.wait_ge(bank_free, n + 1)
                    for j in range(4):
                        m = pe.transpose(ps[:, bank, j * P:(j + 1) * P], o_sb[:, j * P:(j + 1) * P], ident[:])
                    m.then_inc(o_turned, 1)

                def scores(b, g, s, pair):
                    qt, kb = STEPS[s]
                    k = 2 * s + pair
                    skip = max(0, kb - 4 * qt) * P
                    pe.wait_ge(exp_done, b * (2 * GROUPS * NS) + 2 * g * NS + k + 1)
                    for i in range(2):
                        h = 2 * pair + i
                        dst = ps[:, 2 + 2 * (k % 2) + i, :]
                        m = pe.matmul(dst[:, 0:TILE - skip], ks[g][:, h, kb * P:(kb + 1) * P],
                                      qs[g][:, h, qt * TILE + skip:(qt + 1) * TILE],
                                      start=True, stop=kb < 4 * qt)
                        if kb >= 4 * qt:
                            m = pe.matmul(dst[:, 0:P], identb[:], mask_k[:], start=False, stop=True)
                    m.then_inc(score_ready, 1)

                def values(b, g, s, pair):
                    qt, kb = STEPS[s]
                    skip = max(0, kb - 4 * qt) * P
                    pe.wait_ge(exp_done, b * (2 * GROUPS * NS) + 2 * g * NS + 2 * s + 3 + pair)
                    if kb == 0 and pair == 0:
                        pe.wait_ge(o_out, b * (2 * GROUPS) + 2 * g + qt + 1)
                    for h in range(2 * pair, 2 * pair + 2):
                        m = pe.matmul(ps[32 * h:32 * (h + 1), 6, skip:TILE], vs[g][:, kb, 32 * h:32 * (h + 1)],
                                      probs[:, s % 2, h, 0:TILE - skip], start=(kb == 0),
                                      stop=(kb == 4 * qt + 3))
                    if pair:
                        m.then_inc(pv_done, 1)

                def unit(b, g, has_last=True, has_next=True, has_after=True, missing=0):
                    u = b * GROUPS + g
                    uses = uses_of(b, g, has_last, missing)
                    bl, gl = before_unit(b, g)
                    pe.wait_ge(shift_in, u * 16 + 16)
                    for s in range(NS):
                        edges = cuts[s]
                        ahead = has_next if s < NS // 2 else has_after
                        bn, gn, off = ahead_of(s, b, g)
                        if s == NS // 2 and ahead:
                            loaded(bn, gn)

                        def first_pass_part(i):
                            if ahead:
                                first_pass(uses, bn, gn, off + edges[i], off + edges[i + 1])

                        for pair in range(2):
                            scores(b, g, s, pair)
                            first_pass_part(2 * pair)
                            if s > 0:
                                values(b, g, s - 1, pair)
                            elif has_last:
                                values(bl, gl, NS - 1, pair)
                            first_pass_part(2 * pair + 1)
                        if s == LAST_RETURN_STEP and has_last:
                            turn_output(uses, bl, gl, 1)
                        if s == RETURN_STEP:
                            turn_output(uses, b, g, 0)
                        if s == SHIFT_STEP and has_next:
                            turn_shift(uses, *after(b, g, 1))
                    return uses

                pe.sem_inc(pv_done, 2)
                pe.sem_inc(o_turned, 1)
                uses = Uses(1)
                loaded(0, 0)
                first_pass(uses, 0, 0, 0, NC)
                turn_shift(uses, 0, 0)
                loaded(0, 1)
                first_pass(uses, 0, 1, 0, HALFC)
                unit(0, 0, has_last=False)
                with pe.Fori(0, BATCH - 1) as b:
                    for g in range(GROUPS):
                        unit(*after(b, g, 1))
                for g in range(1, GROUPS):
                    uses = unit(BATCH - 1, g, **ends[g])
                for pair in range(2):
                    values(BATCH - 1, GROUPS - 1, NS - 1, pair)
                turn_output(uses, BATCH - 1, GROUPS - 1, 1)

            @block.scalar
            def _(act):
                def take_output(b, g, qt):
                    u = b * GROUPS + g
                    act.wait_ge(pv_done, u * NS + (NS if qt else NS // 3) + 2)
                    act.wait_ge(o_turned, u * 2 + qt + 1)
                    act.activation(o_sb[:], ps[:, 6, :], ACT.Copy).then_inc(o_out, 1)

                def unit(b, g, has_last=True):
                    u = b * GROUPS + g
                    for s, (qt, kb) in enumerate(STEPS):
                        w = TILE - max(0, kb - 4 * qt) * P
                        act.wait_ge(pv_done, u * NS + s + 1)
                        for pair in range(2):
                            k = 2 * s + pair
                            act.wait_ge(score_ready, u * (2 * NS) + k + 1)
                            act.activation(probs[:, s % 2, 2 * pair:2 * pair + 2, 0:w],
                                           ps[:, 2 + 2 * (k % 2):4 + 2 * (k % 2), 0:w], ACT.Exp)\
                                .then_inc(exp_done, 1)
                        if s == 0 and has_last:
                            take_output(*before_unit(b, g), 1)
                        if s == NS // 3:
                            take_output(b, g, 0)

                act.sem_inc(exp_done, 2)
                act.sem_inc(o_out, 1)
                unit(0, 0, has_last=False)
                with act.Fori(0, BATCH - 1) as b:
                    for g in range(GROUPS):
                        unit(*after(b, g, 1))
                for g in range(1, GROUPS):
                    unit(BATCH - 1, g)
                take_output(BATCH - 1, GROUPS - 1, 1)

            @block.vector
            def _(dve):
                def reduce(uses, b, g, lo, hi):
                    for i in range(lo, hi):
                        h, qb, kt, w = CHUNKS[i]
                        bank = uses.take()[1]
                        dve.wait_ge(max_ready, b * (GROUPS * NC) + g * NC + i + 1)
                        col = qb if kt == 0 else BLK + qb - 4
                        dve.tensor_reduce(maxima[:, g % 2, h, col:col + 1], ps[:, bank, 0:w], AX.X, ALU.max)\
                            .then_inc(bank_free, 1)

                def take_output(uses, cnt, b, g, qt):
                    bank = uses.take()[1]
                    dve.wait_ge(o_turned, b * (2 * GROUPS) + 2 * g + qt + 2)
                    o = ps[:, bank, :].rearrange("p (q h c) -> p q h c", q=4, h=GH)
                    cnt.mark(dve.reciprocal(sums[:, qt], o[:, :, :, HD]))
                    cnt.settle()
                    blk = b * BLK + 4 * qt
                    dst = ATT[:, bass.ds(blk, 4), g * 32:(g + 1) * 32].rearrange("p q (h d) -> p q h d", h=GH)
                    dve.tensor_tensor(dst, o[:, :, :, 0:HD], sums[:, qt].unsqueeze(3).to_broadcast([P, 4, GH, HD]),
                                      ALU.mult).then_inc(bank_free, 1)

                def make_shift(uses, cnt, b, g):
                    m = maxima[:, g % 2]
                    dve.wait_ge(bank_free, uses.n + len(BANKS))
                    cnt.mark(dve.tensor_tensor(m[:, :, 4:BLK], m[:, :, 4:BLK], m[:, :, BLK:], ALU.max))
                    cnt.settle()
                    cnt.mark(dve.tensor_scalar(shift[:, 0], m[:, :, 0:BLK], -1.0, None, ALU.mult))
                    cnt.settle()
                    cnt.mark(dve.scalar_tensor_tensor(shift_rest[:], m[:, :, 0:BLK], -1.0, shift[:, 0],
                                                      ALU.mult, ALU.subtract))
                    cnt.settle()
                    cnt.mark(dve.tensor_copy(shift[:, 1], shift_rest[:]))
                    cnt.settle()
                    dve.tensor_tensor(shift[:, 2], shift_rest[:], shift[:, 1], ALU.subtract).then_inc(shift_ready, 1)

                def take_shift(uses, b, g, first=False):
                    u = b * GROUPS + g
                    bank = uses.take()[1]
                    dve.wait_ge(shift_turned, u + 1)
                    if not first:
                        dve.wait_ge(shift_in, u * 16)
                    dve.tensor_copy(shift_t[:], ps[0:3 * GH * BLK, bank, :].bitcast(BF16)[:, 0:P]).then_inc(shift_out, 1)
                    dve.wait_ge(shift_out, u + 1)
                    dve.sem_inc(bank_free, 1)

                def unit(b, g, has_last=True, has_next=True, has_after=True, missing=0):
                    uses = uses_of(b, g, has_last, missing)
                    cnt = Count(dve, dve_steps, b * (GROUPS * DVE_STEPS) + (g + 1) * DVE_STEPS)
                    if not has_last:
                        dve.sem_inc(dve_steps, 1)
                        cnt.n += 1
                    for s in range(NS):
                        edges = cuts[s]
                        bn, gn, off = ahead_of(s, b, g)
                        if has_next if s < NS // 2 else has_after:
                            reduce(uses, bn, gn, off + edges[0], off + edges[4])
                        if s == LAST_RETURN_STEP and has_last:
                            take_output(uses, cnt, *before_unit(b, g), 1)
                        if s == RETURN_STEP:
                            take_output(uses, cnt, b, g, 0)
                            if has_next:
                                make_shift(uses, cnt, *after(b, g, 1))
                        if s == SHIFT_STEP and has_next:
                            take_shift(uses, *after(b, g, 1))
                    assert cnt.n == (DVE_STEPS if has_next else 2)
                    return uses, cnt

                dve.sem_inc(bank_free, len(BANKS) + 1)
                dve.sem_inc(dve_steps, DVE_STEPS - 4)
                uses = Uses(1)
                reduce(uses, 0, 0, 0, NC)
                make_shift(uses, Count(dve, dve_steps, DVE_STEPS - 4), 0, 0)
                take_shift(uses, 0, 0, first=True)
                reduce(uses, 0, 1, 0, HALFC)
                unit(0, 0, has_last=False)
                with dve.Fori(0, BATCH - 1) as b:
                    for g in range(GROUPS):
                        unit(*after(b, g, 1))
                for g in range(1, GROUPS):
                    uses, cnt = unit(BATCH - 1, g, **ends[g])
                take_output(uses, cnt, BATCH - 1, GROUPS - 1, 1)


        def tile_traffic(sp, layer, loads, used, y_out, y_sb, y_stored, sp_steps):
            early, middle, late = loads
            turns = (TILES - 2) // 2

            def wait(sem, count):
                sp.wait_ge(sem, count)
                sp.sem_inc(sp_steps, 1)

            def load(group, s, slot, wait=lambda: None):
                e = sp.value_load(tile_expert[0:1, bass.ds(s, 1)], min_val=0, max_val=N_EXP - 1)
                wait()
                rows = x_slots[layer][bass.ds(s * TILE, TILE), :].rearrange("(j p) d -> p j d", p=P)
                tensors, loaded = group
                for dst, src in tensors(e, slot, rows):
                    sp.dma_start(dst, src).then_inc(loaded[slot], 16)

            def store(s, slot):
                wait(y_out, s + 2)
                sp.dma_start(y_slots[layer][bass.ds(s * TILE, TILE), :].rearrange("(j p) d -> p j d", p=P),
                             y_sb[:, slot]).then_inc(y_stored[slot], 16)

            def step(s, slot, has_last=True, more=True):
                if more:
                    load(early, s + 2, slot, lambda: wait(*used[0](s)))
                if has_last:
                    store(s - 1, 1 - slot)
                    if more or s + 1 < TILES:
                        load(late, s + 1, 1 - slot)
                if more:
                    load(middle, s + 2, slot, lambda: wait(*used[1](s)))

            for slot in range(2):
                sp.sem_inc(y_stored[slot], 16)
                for group in loads:
                    load(group, slot, slot)
            step(0, 0, has_last=False)
            with sp.Fori(0, turns) as i:
                for j in (1, 2):
                    step(i * 2 + j, j % 2)
            for s in range(2 * turns + 1, TILES):
                step(s, s % 2, more=False)
            store(TILES - 1, (TILES - 1) % 2)
            for slot in range(2):
                sp.wait_ge(y_stored[slot], 16 * ((TILES + 1 - slot) // 2) + 16)

        def split_matmul(pe, out, a, b, start, stop):
            for n, (i, j) in enumerate(((0, 0), (0, 1), (1, 0))):
                m = pe.matmul(out, a[:, i], b[:, j], start=start and n == 0, stop=stop and n == 2)
            return m

        def split_weights(pool, s, slot, loaded, count, w, parts, steps, seen):
            pool.wait_ge(loaded[slot], (s - slot) * (count // 2) + count)
            pool.sem_inc(seen, 1)
            pool.tensor_copy(parts[:, slot, 0], w[:, slot]).then_inc(steps, 1)
            pool.wait_ge(steps, s * 2 + 1)
            pool.tensor_tensor(parts[:, slot, 1], w[:, slot], parts[:, slot, 0].bitcast(F32), ALU.subtract)\
                .then_inc(steps, 1)

        def in_pairs(eng, work):
            with eng.Fori(0, TILES // 2) as i:
                for slot in range(2):
                    work(i * 2 + slot, slot)
            for s in range(TILES // 2 * 2, TILES):
                work(s, s % 2)

        with phase() as c:
            w12 = sb("w12", [P, 2, 2, F0], F32, c)
            wg = sb("wg", [P, 2, FF0, F0], F32, c)
            w3 = sb("w3", [P, 2, FF0, D], F32, c)
            vec0 = sb("vec0", [P, 2, PER0], F32, c)
            b3 = sb("b3", [P, 2, D], F32, c)
            xs = sb("xs", [P, 2, QT, D], F32, c)
            xt = sb("xt", [P, 2, TILE], F32, c)
            w12_parts = sb("w12_parts", [P, 2, 2, 2, F0], F32R, c)
            wg_parts = sb("wg_parts", [P, 2, 2, FF0, F0], F32R, c)
            xt_parts = sb("xt_parts", [P, 2, 2, TILE], F32R, c)
            z_parts = sb("z_parts", [P, 2, 2, FF0, TILE], F32R, c)
            x1 = sb("x1", [P, 2, FF0, TILE], F32, c)
            z = sb("z", [P, 2, FF0, TILE], F32, c)
            act_out = sb("act_out", [P, 2, FF0, TILE], F32, c)
            y = sb("y", [P, 2, QT, D], F32, c)
            rows_in, gate_in, down_in = ([sem(f"{n}{i}_c", c) for i in range(2)]
                                         for n in ("rows_in", "gate_in", "down_in"))
            y_stored = [sem(f"y_stored{i}", c) for i in range(2)]
            (t_ready, xt_ready, x12_ready, x1_ready, z_ready, g_ready, silu_ready, y_ready, y_out) = (
                sem(f"{n}_c", c) for n in ("t_ready", "xt_ready", "x12_ready", "x1_ready", "z_ready", "g_ready",
                                           "silu_ready", "y_ready", "y_out"))
            sp_steps, w12_split, wg_split, xt_split, z_steps, seen = (
                sem(f"{n}_c", c) for n in ("sp_steps", "w12_split", "wg_split", "xt_split", "z_steps", "seen"))
            block = c.enter_context(nc.Block())

            @block.sync
            def _(sp):
                one = lambda ap, e: ap[bass.ds(e, 1)].squeeze(0)
                early = lambda e, slot, rows: (
                    (xs[:, slot], rows), (w12[:, slot, 0], one(f0_w1, e)), (w12[:, slot, 1], one(f0_w2, e)))
                middle = lambda e, slot, rows: (
                    (vec0[:, slot], vecs[:, bass.ds(e * PER0, PER0)]),
                    (wg[:, slot], one(f0_wg, e).rearrange("(f p) g -> p f g", p=P)))
                late = lambda e, slot, rows: (
                    (w3[:, slot], one(f0_w3, e).rearrange("(f p) g -> p f g", p=P)),
                    (b3[:, slot], one(f0_b3, e).partition_broadcast(P)))
                used = (lambda s: (x12_ready, s * FF0 + FF0), lambda s: (silu_ready, s * FF0 + 2 * FF0))
                tile_traffic(sp, 0, ((early, rows_in), (middle, gate_in), (late, down_in)), used, y_out, y, y_stored,
                             sp_steps)

            @block.gpsimd
            def _(pool):
                def split(s, slot):
                    split_weights(pool, s, slot, rows_in, 48, w12, w12_parts, w12_split, seen)
                    split_weights(pool, s, slot, gate_in, 32, wg, wg_parts, wg_split, seen)

                in_pairs(pool, split)

            @block.tensor
            def _(pe):
                def turn(s, slot):
                    pe.wait_ge(rows_in[slot], (s - slot) * 24 + 48)
                    pe.wait_ge(xt_ready, s + 1)
                    for j in range(QT):
                        m = pe.transpose(ps[:, 7, j * P:(j + 1) * P], xs[:, slot, j, :], ident[:])
                    m.then_inc(t_ready, 1)

                def up(s, slot):
                    pe.wait_ge(w12_split, s * 2 + 2)
                    pe.wait_ge(xt_split, s + 1)
                    for f in range(FF0):
                        pe.wait_ge(z_ready, s * FF0 + f + 1)
                        for k in range(2):
                            m = split_matmul(pe, ps[:, 2 * k + f, :], w12_parts[:, slot, :, k, f * P:(f + 1) * P],
                                             xt_parts[:, slot], True, True)
                        m.then_inc(x12_ready, 1)

                def gated(s, slot):
                    pe.wait_ge(wg_split, s * 2 + 2)
                    pe.wait_ge(z_ready, s * FF0 + 2 * FF0)
                    for go in range(FF0):
                        pe.wait_ge(silu_ready, s * FF0 + go + 1)
                        for f in range(FF0):
                            m = split_matmul(pe, ps[:, 4 + go, :], wg_parts[:, slot, :, f, go * P:(go + 1) * P],
                                             z_parts[:, slot, :, f], f == 0, f == FF0 - 1)
                        m.then_inc(g_ready, 1)

                def down(s, slot):
                    pe.wait_ge(down_in[slot], (s - slot) * 16 + 32)
                    pe.wait_ge(silu_ready, s * FF0 + 2 * FF0)
                    pe.wait_ge(y_out, s + 1)
                    for j in range(QT):
                        for f in range(FF0):
                            m = pe.matmul(ps[:, 6, j * P:(j + 1) * P], act_out[:, slot, f, j * P:(j + 1) * P],
                                          w3[:, slot, f, :], start=(f == 0), stop=(f == FF0 - 1))
                    m.then_inc(y_ready, 1)

                pipeline(pe, TILES, up, gated, behind=down, first=turn)

            @block.scalar
            def _(act):
                def take_rows(s, slot):
                    act.wait_ge(t_ready, s + 1)
                    for dst in (xt[:, slot], xt_parts[:, slot, 0]):
                        m = act.activation(dst, ps[:, 7, :], ACT.Copy)
                    m.then_inc(xt_ready, 1)

                def first(s, slot):
                    act.wait_ge(gate_in[slot], (s - slot) * 16 + 32)
                    for f in range(FF0):
                        act.wait_ge(x12_ready, s * FF0 + f + 1)
                        act.activation(x1[:, slot, f, :], ps[:, f, :], ACT.Identity, bias=vec0[:, slot, f:f + 1])\
                            .then_inc(x1_ready, 1)

                def silu(s, slot):
                    for go in range(FF0):
                        act.wait_ge(g_ready, s * FF0 + go + 1)
                        act.activation(act_out[:, slot, go, :], ps[:, 4 + go, :], ACT.Silu,
                                       bias=vec0[:, slot, 2 * FF0 + go:2 * FF0 + go + 1]).then_inc(silu_ready, 1)

                act.sem_inc(xt_ready, 1)
                act.sem_inc(silu_ready, FF0)
                pipeline(act, TILES, first, silu, first=take_rows)

            @block.vector
            def _(dve):
                def product(s, slot):
                    for f in range(FF0):
                        dve.wait_ge(x1_ready, s * FF0 + f + 1)
                        for dst in (z[:, slot, f], z_parts[:, slot, 0, f]):
                            m = dve.scalar_tensor_tensor(dst, ps[:, 2 + f, :], vec0[:, slot, FF0 + f:FF0 + f + 1],
                                                         x1[:, slot, f, :], ALU.add, ALU.mult)
                        m.then_inc(z_steps, 1)
                        dve.wait_ge(z_steps, s * FF0 + f + 1)
                        dve.tensor_tensor(z_parts[:, slot, 1, f], z[:, slot, f], z_parts[:, slot, 0, f].bitcast(F32),
                                          ALU.subtract).then_inc(z_ready, 1)

                def split(s, slot):
                    dve.wait_ge(xt_ready, s + 2)
                    dve.tensor_tensor(xt_parts[:, slot, 1], xt[:, slot], xt_parts[:, slot, 0].bitcast(F32), ALU.subtract)\
                        .then_inc(xt_split, 1)

                def result(s, slot):
                    dve.wait_ge(y_ready, s + 1)
                    dve.wait_ge(y_stored[slot], (s - slot) * 8 + 16)
                    dve.tensor_tensor(y[:, slot], ps[:, 6, :].rearrange("p (j d) -> p j d", j=QT),
                                      b3[:, slot].unsqueeze(1).to_broadcast([P, QT, D]), ALU.add).then_inc(y_out, 1)

                dve.sem_inc(z_ready, FF0)
                dve.sem_inc(y_out, 1)
                pipeline(dve, TILES, first=split, ahead=product, behind=result)

        XMT = sb("XMT", [P, N], F32)
        picked = sb("picked", [P, 2, NBLK, D], F32)
        between = ctx.enter_context(ExitStack())
        q_all = sb("q_all", [P, N], F32, between)
        k_all = sb("k_all", [P, N], F32, between)
        v_all = sb("v_all", [P, NBLK, D], F32, between)
        with phase() as c:
            att = sb("att", [P, 2, QT, D], F32, c)
            att_t = sb("att_t", [P, TILE], F32, c)
            x1 = sb("x1b", [P, 2, QT, D], F32, c)
            xn = sb("xnb", [P, 2, QT, D], F32, c)
            xm = sb("xmb", [P, 2, QT, D], F32, c)
            xn_t = sb("xn_t", [P, 2, TILE], F32, c)
            xm_t = sb("xm_t", [P, 2, TILE], F32, c)
            wv_t = sb("wv_t", [P, P], F32, c)
            wvo = sb("wvo", [P, D], F32, c)
            stats = sb("stats1", [P, QT, 6], F32, c)
            moments = sb("moments1", [P, QT, 2], F32, c)
            dev = sb("dev1", [P, QT], F32, c)
            rstd = sb("rstd1", [P, QT], F32, c)
            att_in, xm_kept, rows_kept, gathered = (
                [sem(f"{n}{i}_d", c) for i in range(2)] for n in ("att_in", "xm_kept", "rows_kept", "gathered"))
            wvo_ready, wvo_out, qkv_ready, qkv_seen, qkv_out = (
                sem(n, c) for n in ("wvo_ready", "wvo_out", "qkv_ready", "qkv_seen", "qkv_out"))
            (rows_picked, att_turned, att_out, wo_ready, x1_out, sum_steps, norm_steps, stats_written, moments_ready,
             dev_ready, xn_ready, xn_turned, xn_out, xm_ready, xm_turned, xm_out, g_ready, g_out) = (
                sem(f"{n}_d", c) for n in (
                    "rows_picked", "att_turned", "att_out", "wo_ready", "x1_out", "sum_steps", "norm_steps",
                    "stats_written", "moments_ready", "dev_ready", "xn_ready", "xn_turned", "xn_out", "xm_ready",
                    "xm_turned", "xm_out", "g_ready", "g_out"))
            sp_steps = sem("sp_steps_d", c)
            block = c.enter_context(nc.Block())
            SUM_STEPS, NORM_STEPS = 1 + 2 * QT, 2 * (3 * QT + 1) + 1

            @block.sync
            def _(sp):
                def load(t, slot):
                    sp.dma_start(att[:, slot], ATT[:, tile_blocks(t), :]).then_inc(att_in[slot], 16)

                def keep(t, slot):
                    sp.wait_ge(xm_ready, t + 1)
                    sp.dma_start(XN[:, tile_blocks(t), :], xm[:, slot]).then_inc(rows_kept[slot], 16)
                    sp.wait_ge(xm_out, t + 2)
                    sp.sem_inc(sp_steps, 1)
                    sp.dma_start(XMT[:, bass.ds(t * TILE, TILE)], xm_t[:, slot]).then_inc(xm_kept[slot], 16)

                for slot in range(2):
                    for kept in (xm_kept, rows_kept):
                        sp.sem_inc(kept[slot], 16)
                load(0, 0)
                load(1, 1)
                with sp.Fori(0, NTILE // 2 - 1) as i:
                    for slot in range(2):
                        sp.wait_ge(att_turned, i * 2 + slot + 1)
                        load(i * 2 + slot + 2, slot)
                        keep(i * 2 + slot, slot)
                for t in range(NTILE - 2, NTILE):
                    keep(t, t % 2)
                for slot in range(2):
                    for kept in (xm_kept, rows_kept):
                        sp.wait_ge(kept[slot], 16 * NTILE // 2 + 16)

            @block.gpsimd
            def _(pool):
                gather_rows(pool, 0, picked, gathered, rows_picked)

            @block.tensor
            def _(pe):
                def attention_out(t, slot):
                    pe.wait_ge(att_in[slot], (t - slot) * 8 + 16)
                    pe.wait_ge(att_out, t + 1)
                    for j in range(QT):
                        m = pe.transpose(ps[:, 0, j * P:(j + 1) * P], att[:, slot, j, :], ident[:])
                    m.then_inc(att_turned, 1)
                    pe.wait_ge(att_out, t + 2)
                    pe.wait_ge(x1_out, t + 1)
                    for j in range(QT):
                        m = pe.matmul(ps[:, 1, j * P:(j + 1) * P], att_t[:, j * P:(j + 1) * P], W["wo0"][:],
                                      start=True, stop=True)
                    m.then_inc(wo_ready, 1)

                def norms_turned(t, slot):
                    for src, bank, ready, out_of, turned in ((xn, 2, xn_ready, xn_out, xn_turned),
                                                             (xm, 3, xm_ready, xm_out, xm_turned)):
                        pe.wait_ge(ready, t + 1)
                        pe.wait_ge(out_of, t + 1)
                        for j in range(QT):
                            m = pe.transpose(ps[:, bank, j * P:(j + 1) * P], src[:, slot, j, :], ident[:])
                        m.then_inc(turned, 1)
                    pe.wait_ge(xm_out, t + 2)
                    pe.wait_ge(g_out, t + 1)
                    for j in range(QT):
                        m = pe.matmul(ps[:, 4, j * N_EXP:(j + 1) * N_EXP], xm_t[:, slot, j * P:(j + 1) * P],
                                      gw[1][:], start=True, stop=True)
                    m.then_inc(g_ready, 1)
                    pe.wait_ge(xn_out, t + 2)
                    for k, w in enumerate((W["wq1"], W["wk1"])):
                        pe.wait_ge(qkv_out, t * 3 + k + 1)
                        pe.matmul(ps[:, 5 + k, :], w[:], xn_t[:, slot], start=True, stop=True).then_inc(qkv_ready, 1)
                    pe.wait_ge(wvo_out, 2)
                    pe.wait_ge(qkv_out, t * 3 + 3)
                    for j in range(QT):
                        m = pe.matmul(ps[:, 7, j * P:(j + 1) * P], xn_t[:, slot, j * P:(j + 1) * P], wvo[:],
                                      start=True, stop=True)
                    m.then_inc(qkv_ready, 1)

                pe.transpose(ps[:, 7, 0:P], W["wv1"][:], ident[:]).then_inc(wvo_ready, 1)
                pe.wait_ge(wvo_out, 1)
                pe.matmul(ps[:, 7, 0:D], wv_t[:], W["wo1"][:], start=True, stop=True).then_inc(wvo_ready, 1)
                pipeline(pe, NTILE, first=attention_out, behind=norms_turned)

            @block.scalar
            def _(act):
                def take_attention(t, slot):
                    act.wait_ge(att_turned, t + 1)
                    act.activation(att_t[:], ps[:, 0, :], ACT.Copy).then_inc(att_out, 1)

                def roots(t, slot):
                    for norm in range(2):
                        act.wait_ge(moments_ready, t * 2 + norm + 1)
                        deviation(act, moments, dev, eps).then_inc(dev_ready, 1)

                def take_norms(t, slot):
                    act.wait_ge(xn_turned, t + 1)
                    act.activation(xn_t[:, slot], ps[:, 2, :], ACT.Copy).then_inc(xn_out, 1)
                    act.wait_ge(xm_turned, t + 1)
                    act.wait_ge(xm_kept[slot], (t - slot) * 8 + 16)
                    act.activation(xm_t[:, slot], ps[:, 3, :], ACT.Identity, scale=vec("ln_g"), bias=vec("ln_b"))\
                        .then_inc(xm_out, 1)

                def take_qkv(t, slot):
                    cols = bass.ds(t * TILE, TILE)
                    for k, dst in enumerate((q_all[:, cols], k_all[:, cols], v_all[:, tile_blocks(t), :])):
                        act.wait_ge(qkv_ready, t * 3 + k + 1)
                        act.sem_inc(qkv_seen, 1)
                        src = ps[:, 5 + k, :]
                        act.activation(dst, src if k < 2 else src.rearrange("p (j d) -> p j d", j=QT), ACT.Copy)\
                            .then_inc(qkv_out, 1)

                def step(t, slot, has_last, has_next):
                    if has_next:
                        take_attention(t + 1, 1 - slot)
                    if has_last:
                        take_norms(t - 1, 1 - slot)
                    roots(t, slot)
                    if has_last:
                        take_qkv(t - 1, 1 - slot)

                act.sem_inc(qkv_out, 3)
                act.sem_inc(att_out, 1)
                act.sem_inc(xn_out, 1)
                act.sem_inc(xm_out, 1)
                for k, dst in enumerate((wv_t, wvo)):
                    act.wait_ge(wvo_ready, k + 1)
                    act.activation(dst[:], ps[:, 7, 0:P], ACT.Copy).then_inc(wvo_out, 1)
                take_attention(0, 0)
                steps(act, NTILE, step)
                take_norms(NTILE - 1, (NTILE - 1) % 2)
                take_qkv(NTILE - 1, (NTILE - 1) % 2)

            @block.vector
            def _(dve):
                def first_sum(t, slot):
                    cnt = Count(dve, sum_steps, t * SUM_STEPS)
                    dve.wait_ge(wo_ready, t + 1)
                    cnt.mark(dve.tensor_tensor(x1[:, slot], ps[:, 1, :].rearrange("p (j d) -> p j d", j=QT),
                                               X[:, tile_blocks(t), :], ALU.add))
                    cnt.settle()
                    dve.sem_inc(x1_out, 1)
                    dve.wait_ge(rows_picked, t + 1)
                    for k in range(2):
                        for j in range(QT):
                            n = bass.ds(t * QT + j, 1)
                            cnt.mark(dve.scalar_tensor_tensor(
                                x1[:, slot, j, :], picked[:, k, n, :].squeeze(1), share[:, k, n], x1[:, slot, j, :],
                                ALU.mult, ALU.add))
                        cnt.settle()

                def norms(t, slot):
                    cnt = Count(dve, norm_steps, t * NORM_STEPS)
                    moments_of(dve, cnt, lambda j: x1[:, slot, j, :], stats, moments, QT, stats_written)
                    dve.sem_inc(moments_ready, 1)
                    dve.wait_ge(dev_ready, t * 2 + 1)
                    scale_rows(dve, cnt, lambda j: x1[:, slot, j, :], lambda j: xn[:, slot, j, :], moments, dev,
                               rstd, QT)
                    cnt.settle()
                    dve.sem_inc(xn_ready, 1)
                    moments_of(dve, cnt, lambda j: xn[:, slot, j, :], stats, moments, QT, stats_written)
                    dve.sem_inc(moments_ready, 1)
                    cnt.mark(dve.tensor_tensor(X[:, tile_blocks(t), :], x1[:, slot], xn[:, slot], ALU.add))
                    dve.wait_ge(dev_ready, t * 2 + 2)
                    dve.wait_ge(rows_kept[slot], (t - slot) * 8 + 16)
                    scale_rows(dve, cnt, lambda j: xn[:, slot, j, :], lambda j: xm[:, slot, j, :], moments, dev,
                               rstd, QT)
                    cnt.settle()
                    dve.sem_inc(xm_ready, 1)
                    assert cnt.n == NORM_STEPS

                def gate_logits(t, slot):
                    dve.wait_ge(g_ready, t + 1)
                    dve.tensor_tensor(
                        logits[:, tile_blocks(t), :], ps[:, 4, 0:QT * N_EXP].rearrange("p (j e) -> p j e", j=QT),
                        gb[1][:].unsqueeze(1).to_broadcast([P, QT, N_EXP]), ALU.add).then_inc(g_out, 1)

                dve.sem_inc(x1_out, 1)
                dve.sem_inc(g_out, 1)
                pipeline(dve, NTILE, first=first_sum, behind=gate_logits, now=norms)

        route(1, 2, *squarings(4, SQUARINGS + NROT - 1))

        with phase() as c:
            q_row = sb("q_row", [P, 2, T], F32, c)
            p_sb = sb("p_sb", [P, 2, T], F32, c)
            p_t = sb("p_t", [P, 2, BLK, P], F32, c)
            top = sb("top", [P, BLK], F32, c)
            bias = sb("bias", [P, BLK], F32, c)
            den = sb("den", [P, BLK], F32, c)
            rden = sb("rden", [P, BLK], F32, c)
            q_in, q_seen = [sem(f"q_in{i}", c) for i in range(2)], sem("q_seen", c)
            (t_ready, t_out, dve_steps, s_ready, bias_ready, p_ready, y_ready, y_out, scattered) = (
                sem(f"{n}_a", c) for n in ("t_ready", "t_out", "dve_steps", "s_ready", "bias_ready", "p_ready",
                                           "y_ready", "y_out", "scattered"))
            block = c.enter_context(nc.Block())
            SC = float(D) ** -0.5
            HALF = BLK // 2
            T_P = [sum(1 + k // HALF for k in range(qb)) for qb in range(BLK + 1)]
            T_USES = T_P[BLK]
            DVE_STEPS = 2 * BLK

            def rows(eng, work):
                with eng.Fori(0, BATCH // 2) as i:
                    for slot in range(2):
                        work(i * 2 + slot, slot)

            @block.sync
            def _(sp):
                def load(b, slot):
                    sp.dma_start(q_row[:, slot], q_all[:, bass.ds(b * T, T)]).then_inc(q_in[slot], 16)

                load(0, 0)
                load(1, 1)
                with sp.Fori(0, BATCH // 2 - 1) as i:
                    for slot in range(2):
                        sp.wait_ge(s_ready, i * (2 * BLK) + (slot + 1) * BLK)
                        sp.sem_inc(q_seen, 1)
                        load(i * 2 + 2 + slot, slot)

            @block.gpsimd
            def _(pool):
                scatter_rows(pool, 1, scattered)
                pool.wait_ge(scattered, 16 * 2 * NBLK)

            @block.tensor
            def _(pe):
                def row(b, slot):
                    def turn(n, blocks):
                        pe.wait_ge(t_out, b * T_USES + n + 1)
                        for j, src in enumerate(blocks):
                            m = pe.transpose(ps[:, n % 2, j * P:(j + 1) * P], src, ident[:])
                        m.then_inc(t_ready, 1)

                    def scores(qb):
                        bank = 4 + 2 * (qb % 2)
                        pe.wait_ge(p_ready, b * BLK + qb + 1)
                        n_keys = (qb + 1) * P
                        for kt in range(1 + qb // 4):
                            w = min(TILE, n_keys - kt * TILE)
                            last = (kt == qb // 4)
                            m = pe.matmul(ps[:, bank + kt, 0:w], q_row[:, slot, qb * P:(qb + 1) * P],
                                          k_all[:, bass.ds(b * T + kt * TILE, w)], start=True, stop=not last)
                            if last:
                                m = pe.matmul(ps[:, bank + kt, w - P:w], identb[:], mask_q[:],
                                              start=False, stop=True)
                        m.then_inc(s_ready, 1)

                    pe.wait_ge(q_in[slot], (b - slot) * 8 + 16)
                    scores(0)
                    scores(1)
                    for qb in range(BLK):
                        pe.wait_ge(p_ready, b * BLK + qb + 3)
                        for h in range(1 + qb // HALF):
                            turn(T_P[qb] + h, [p_sb[:, qb % 2, kb * P:(kb + 1) * P]
                                               for kb in range(h * HALF, min((h + 1) * HALF, qb + 1))])
                        if qb + 2 < BLK:
                            scores(qb + 2)
                        pe.wait_ge(t_out, b * T_USES + T_P[qb + 1] + 2)
                        pe.wait_ge(y_out, b * BLK + qb + 1)
                        for kb in range(qb + 1):
                            m = pe.matmul(ps[:, 2 + qb % 2, 0:D], p_t[:, qb % 2, kb, :],
                                          v_all[:, bass.ds(b * BLK + kb, 1), :].squeeze(1),
                                          start=(kb == 0), stop=(kb == qb))
                        m.then_inc(y_ready, 1)

                rows(pe, row)

            @block.scalar
            def _(act):
                def row(b, slot):
                    def exponentials(qb):
                        w = (qb + 1) * P
                        act.wait_ge(bias_ready, b * BLK + qb + 1)
                        src = ps[:, 4 + 2 * (qb % 2):6 + 2 * (qb % 2), :].rearrange("p k c -> p (k c)")[:, 0:w]
                        act.activation(p_sb[:, qb % 2, 0:w], src, ACT.Exp, bias=bias[:, qb:qb + 1], scale=SC,
                                       accum_out=den[:, qb:qb + 1]).then_inc(p_ready, 1)

                    exponentials(0)
                    for qb in range(BLK):
                        if qb + 1 < BLK:
                            exponentials(qb + 1)
                        for h in range(1 + qb // HALF):
                            n = min((h + 1) * HALF, qb + 1) - h * HALF
                            use = T_P[qb] + h
                            act.wait_ge(t_ready, b * T_USES + use + 1)
                            act.activation(p_t[:, qb % 2, h * HALF:h * HALF + n, :],
                                           ps[:, use % 2, 0:n * P].rearrange("p (k q) -> p k q", k=n), ACT.Copy)\
                                .then_inc(t_out, 1)

                act.sem_inc(t_out, 2)
                act.sem_inc(p_ready, 2)
                rows(act, row)

            @block.vector
            def _(dve):
                def row(b, slot):
                    cnt = Count(dve, dve_steps, b * DVE_STEPS)

                    def maximum(qb):
                        w = (qb + 1) * P
                        dve.wait_ge(s_ready, b * BLK + qb + 1)
                        src = ps[:, 4 + 2 * (qb % 2):6 + 2 * (qb % 2), :].rearrange("p k c -> p (k c)")[:, 0:w]
                        cnt.mark(dve.tensor_reduce(top[:, qb:qb + 1], src, AX.X, ALU.max))
                        cnt.settle()
                        dve.tensor_scalar(bias[:, qb:qb + 1], top[:, qb:qb + 1], -SC, None, ALU.mult)\
                            .then_inc(bias_ready, 1)

                    def finish(qb):
                        dve.wait_ge(y_ready, b * BLK + qb + 1)
                        own = X[:, bass.ds(b * BLK + qb, 1), :].squeeze(1)
                        dve.scalar_tensor_tensor(own, ps[:, 2 + qb % 2, 0:D], rden[:, qb:qb + 1], own,
                                                 ALU.mult, ALU.add).then_inc(y_out, 1)

                    maximum(0)
                    maximum(1)
                    for qb in range(BLK):
                        dve.wait_ge(p_ready, b * BLK + qb + 3)
                        cnt.mark(dve.reciprocal(rden[:, qb:qb + 1], den[:, qb:qb + 1]))
                        cnt.settle()
                        if qb + 2 < BLK:
                            maximum(qb + 2)
                        if qb > 0:
                            finish(qb - 1)
                    finish(BLK - 1)
                    assert cnt.n == DVE_STEPS

                dve.sem_inc(y_out, 2)
                rows(dve, row)

        between.close()

        with phase() as c:
            u1 = sb("u1", [P, 2, F1], F32, c)
            u2 = sb("u2", [P, 2, FF1, D], F32, c)
            vec1 = sb("vec1", [P, 2, PER1], F32, c)
            b2 = sb("b2", [P, 2, D], F32, c)
            xs = sb("xs1", [P, 2, QT, D], F32, c)
            xt = sb("xt1", [P, 2, TILE], F32, c)
            u1_parts = sb("u1_parts", [P, 2, 2, F1], F32R, c)
            xt_parts = sb("xt_parts1", [P, 2, 2, TILE], F32R, c)
            hid = sb("hid", [P, 2, FF1, TILE], F32, c)
            y = sb("y1", [P, 2, QT, D], F32, c)
            rows_in, vecs_in, down_in, y_stored = ([sem(f"{n}{i}_e", c) for i in range(2)]
                                                   for n in ("rows_in", "vecs_in", "down_in", "y_stored"))
            u1_split, xt_split, seen = sem("u1_split", c), sem("xt_split", c), sem("seen_e", c)
            (t_ready, xt_ready, h_ready, gelu_ready, y_ready, y_out) = (
                sem(f"{n}_e", c) for n in ("t_ready", "xt_ready", "h_ready", "gelu_ready", "y_ready", "y_out"))
            sp_steps = sem("sp_steps_e", c)
            block = c.enter_context(nc.Block())

            @block.sync
            def _(sp):
                one = lambda ap, e: ap[bass.ds(e, 1)].squeeze(0)
                early = lambda e, slot, rows: ((xs[:, slot], rows), (u1[:, slot], one(f1_w1, e)))
                middle = lambda e, slot, rows: ((vec1[:, slot], vecs[:, bass.ds(e * PER1 + FIRST1, PER1)]),)
                late = lambda e, slot, rows: (
                    (u2[:, slot], one(f1_w2, e).rearrange("(f p) g -> p f g", p=P)),
                    (b2[:, slot], one(f1_b2, e).partition_broadcast(P)))
                used = (lambda s: (h_ready, s * FF1 + FF1), lambda s: (gelu_ready, s * FF1 + 2 * FF1))
                tile_traffic(sp, 1, ((early, rows_in), (middle, vecs_in), (late, down_in)), used, y_out, y, y_stored,
                             sp_steps)

            @block.gpsimd
            def _(pool):
                in_pairs(pool, lambda s, slot: split_weights(pool, s, slot, rows_in, 32, u1, u1_parts, u1_split,
                                                          seen))

            @block.tensor
            def _(pe):
                def turn(s, slot):
                    pe.wait_ge(rows_in[slot], (s - slot) * 16 + 32)
                    pe.wait_ge(xt_ready, s + 1)
                    for j in range(QT):
                        m = pe.transpose(ps[:, 7, j * P:(j + 1) * P], xs[:, slot, j, :], ident[:])
                    m.then_inc(t_ready, 1)

                def up(s, slot):
                    pe.wait_ge(u1_split, s * 2 + 2)
                    pe.wait_ge(xt_split, s + 1)
                    for f in range(FF1):
                        pe.wait_ge(gelu_ready, s * FF1 + f + 1)
                        split_matmul(pe, ps[:, f, :], u1_parts[:, slot, :, f * P:(f + 1) * P], xt_parts[:, slot],
                                     True, True).then_inc(h_ready, 1)

                def down(s, slot):
                    pe.wait_ge(down_in[slot], (s - slot) * 16 + 32)
                    pe.wait_ge(gelu_ready, s * FF1 + 2 * FF1)
                    pe.wait_ge(y_out, s + 1)
                    for j in range(QT):
                        for f in range(FF1):
                            m = pe.matmul(ps[:, 6, j * P:(j + 1) * P], hid[:, slot, f, j * P:(j + 1) * P],
                                          u2[:, slot, f, :], start=(f == 0), stop=(f == FF1 - 1))
                    m.then_inc(y_ready, 1)

                pipeline(pe, TILES, first=turn, now=down, last=up)

            @block.scalar
            def _(act):
                def take_rows(s, slot):
                    act.wait_ge(t_ready, s + 1)
                    for dst in (xt[:, slot], xt_parts[:, slot, 0]):
                        m = act.activation(dst, ps[:, 7, :], ACT.Identity, scale=vec("ln_g"), bias=vec("ln_b"))
                    m.then_inc(xt_ready, 1)

                def hidden(s, slot):
                    act.wait_ge(vecs_in[slot], (s - slot) * 8 + 16)
                    for f in range(FF1):
                        act.wait_ge(h_ready, s * FF1 + f + 1)
                        act.activation(hid[:, slot, f, :], ps[:, f, :], ACT.Gelu, bias=vec1[:, slot, f:f + 1])\
                            .then_inc(gelu_ready, 1)

                act.sem_inc(xt_ready, 1)
                act.sem_inc(gelu_ready, FF1)
                pipeline(act, TILES, ahead=hidden, first=take_rows)

            @block.vector
            def _(dve):
                def result(s, slot):
                    dve.wait_ge(y_ready, s + 1)
                    dve.wait_ge(y_stored[slot], (s - slot) * 8 + 16)
                    dve.tensor_tensor(y[:, slot], ps[:, 6, :].rearrange("p (j d) -> p j d", j=QT),
                                      b2[:, slot].unsqueeze(1).to_broadcast([P, QT, D]), ALU.add).then_inc(y_out, 1)

                def split(s, slot):
                    dve.wait_ge(xt_ready, s + 2)
                    dve.tensor_tensor(xt_parts[:, slot, 1], xt[:, slot], xt_parts[:, slot, 0].bitcast(F32), ALU.subtract)\
                        .then_inc(xt_split, 1)

                dve.sem_inc(y_out, 1)
                pipeline(dve, TILES, first=split, now=result)

        with phase() as c:
            abel = sb("abel", [P, N], F32, c)
            moe = sb("moe", [P, 2, QT, D], F32, c)
            moe_t = sb("moe_t", [P, 2, TILE], F32, c)
            non = sb("non", [P, 2, TILE], F32, c)
            g_sb = sb("g_sb", [P, 2, TILE], F32, c)
            mixed = sb("mixed", [P, 2, TILE], F32, c)
            mix = sb("mix", [P, 2, D], F32, c)
            out_sb = sb("out_sb", [P, 2, QT, D], F32, c)
            gathered, stored = ([sem(f"{n}{i}_f", c) for i in range(2)] for n in ("gathered", "stored"))
            (rows_picked, mix_set, a_ready, abel_ready, abel_seen, moe_steps, moe_ready, moe_turned, moe_out, n_ready,
             non_ready, z_ready, g_ready, mix_steps, mixed_ready, t_ready, out_ready) = (sem(f"{n}_f", c) for n in (
                 "rows_picked", "mix_set", "a_ready", "abel_ready", "abel_seen", "moe_steps", "moe_ready",
                 "moe_turned", "moe_out", "n_ready", "non_ready", "z_ready", "g_ready", "mix_steps", "mixed_ready",
                 "t_ready", "out_ready"))
            block = c.enter_context(nc.Block())
            out_rows = out.rearrange("b (k p) d -> p (b k) d", p=P)
            MOE_STEPS, MIX_STEPS = 2 * QT, 3

            @block.sync
            def _(sp):
                def store(t, slot):
                    sp.wait_ge(out_ready, t + 3)
                    sp.dma_start(out_rows[:, tile_blocks(t), :], out_sb[:, slot]).then_inc(stored[slot], 16)

                for slot in range(2):
                    sp.sem_inc(stored[slot], 16)
                with sp.Fori(0, NTILE // 2) as i:
                    for slot in range(2):
                        store(i * 2 + slot, slot)
                for slot in range(2):
                    sp.wait_ge(stored[slot], 16 * NTILE // 2 + 16)

            @block.gpsimd
            def _(pool):
                gather_rows(pool, 1, picked, gathered, rows_picked)

            @block.tensor
            def _(pe):
                with pe.Fori(0, NTILE // 2) as i:
                    for slot in range(2):
                        t = i * 2 + slot
                        pe.wait_ge(abel_ready, t + 1)
                        pe.matmul(ps[:, slot, :], W["abw"][:], XMT[:, bass.ds(t * TILE, TILE)],
                                  start=True, stop=True).then_inc(a_ready, 1)
                pe.wait_ge(abel_ready, NTILE + 2)
                pe.wait_ge(mix_set, 2)

                def turn(t, slot):
                    pe.wait_ge(moe_ready, t + 1)
                    pe.wait_ge(moe_out, t + 1)
                    for j in range(QT):
                        m = pe.transpose(ps[:, 0, j * P:(j + 1) * P], moe[:, slot, j, :], ident[:])
                    m.then_inc(moe_turned, 1)

                def back(t, slot):
                    pe.wait_ge(mixed_ready, t + 1)
                    pe.wait_ge(out_ready, t + 1)
                    for j in range(QT):
                        m = pe.transpose(ps[:, 6 + slot, j * P:(j + 1) * P], mixed[:, slot, j * P:(j + 1) * P],
                                         ident[:])
                    m.then_inc(t_ready, 1)

                def step(t, slot, has_last, has_next):
                    pe.wait_ge(moe_out, t + 2)
                    pe.wait_ge(non_ready, t + 1)
                    pe.matmul(ps[:, 2, :], rot[:], moe_t[:, slot, :], start=True, stop=True).then_inc(n_ready, 1)
                    pe.wait_ge(g_ready, t + 1)
                    pe.matmul(ps[:, 4 + slot, :], mix[:, 0, :], abel[:, bass.ds(t * TILE, TILE)],
                              start=True, stop=False)
                    if has_last:
                        back(t - 1, 1 - slot)
                    pe.wait_ge(non_ready, t + 2)
                    pe.matmul(ps[:, 4 + slot, :], mix[:, 1, :], non[:, slot, :], start=False, stop=True)\
                        .then_inc(z_ready, 1)
                    if has_next:
                        turn(t + 1, 1 - slot)

                turn(0, 0)
                steps(pe, NTILE, step)
                back(NTILE - 1, (NTILE - 1) % 2)

            @block.scalar
            def _(act):
                act.sem_inc(abel_ready, 2)
                act.sem_inc(moe_out, 1)
                act.sem_inc(g_ready, 2)
                with act.Fori(0, NTILE // 2) as i:
                    for slot in range(2):
                        t = i * 2 + slot
                        act.wait_ge(a_ready, t + 1)
                        act.sem_inc(abel_seen, 1)
                        act.activation(abel[:, bass.ds(t * TILE, TILE)], ps[:, slot, :], ACT.Gelu,
                                       bias=vec("abel_b")).then_inc(abel_ready, 1)

                def take_moe(t, slot):
                    act.wait_ge(moe_turned, t + 1)
                    act.activation(moe_t[:, slot], ps[:, 0, :], ACT.Copy).then_inc(moe_out, 1)

                def gate(t, slot):
                    act.wait_ge(z_ready, t + 1)
                    act.activation(g_sb[:, slot], ps[:, 4 + slot, :], ACT.Sigmoid, bias=mixb[:]).then_inc(g_ready, 1)

                pipeline(act, NTILE, now=gate, last=take_moe)

            @block.vector
            def _(dve):
                dve.sem_inc(non_ready, 1)
                dve.sem_inc(out_ready, 2)
                for k in range(2):
                    dve.tensor_copy(mix[:, k, :], vec(("mix_a", "mix_b")[k]).to_broadcast([P, D])).then_inc(mix_set, 1)
                dve.wait_ge(abel_ready, NTILE + 2)

                def sum_of_experts(t, slot):
                    cnt = Count(dve, moe_steps, t * MOE_STEPS)
                    dve.wait_ge(rows_picked, t + 1)
                    for k in range(2):
                        for j in range(QT):
                            n = bass.ds(t * QT + j, 1)
                            rows, w = picked[:, k, n, :].squeeze(1), share[:, k, n]
                            if k == 0:
                                cnt.mark(dve.tensor_scalar(moe[:, slot, j, :], rows, w, None, ALU.mult))
                            else:
                                cnt.mark(dve.scalar_tensor_tensor(moe[:, slot, j, :], rows, w, moe[:, slot, j, :],
                                                                  ALU.mult, ALU.add))
                        cnt.settle()
                    dve.sem_inc(moe_ready, 1)

                def output(t, slot):
                    dve.wait_ge(t_ready, t + 1)
                    dve.wait_ge(stored[slot], (t - slot) * 8 + 16)
                    dve.tensor_tensor(out_sb[:, slot], ps[:, 6 + slot, :].rearrange("p (j d) -> p j d", d=D),
                                      X[:, tile_blocks(t), :], ALU.add).then_inc(out_ready, 1)

                def step(t, slot, has_last, has_next):
                    cnt = Count(dve, mix_steps, t * MIX_STEPS)
                    ab = abel[:, bass.ds(t * TILE, TILE)]
                    dve.wait_ge(n_ready, t + 1)
                    dve.tensor_copy(non[:, slot], ps[:, 2, :]).then_inc(non_ready, 1)
                    if has_next:
                        sum_of_experts(t + 1, 1 - slot)
                    dve.wait_ge(non_ready, t + 2)
                    cnt.mark(dve.tensor_tensor(mixed[:, slot], non[:, slot], ab, ALU.subtract))
                    if has_last:
                        output(t - 1, 1 - slot)
                    cnt.settle()
                    dve.wait_ge(g_ready, t + 3)
                    cnt.mark(dve.tensor_tensor(mixed[:, slot], mixed[:, slot], g_sb[:, slot], ALU.mult))
                    cnt.settle()
                    cnt.mark(dve.tensor_tensor(mixed[:, slot], mixed[:, slot], ab, ALU.add))
                    cnt.settle()
                    dve.sem_inc(mixed_ready, 1)

                sum_of_experts(0, 0)
                steps(dve, NTILE, step)
                output(NTILE - 1, (NTILE - 1) % 2)


_INS = ['L0_attn_x', 'L0_attn_Wq', 'L0_attn_Wk', 'L0_attn_Wv', 'L0_attn_Wo', 'L0_ffn_gate_w', 'L0_ffn_gate_b',
        'L0_ffn_w1', 'L0_ffn_b1', 'L0_ffn_w2', 'L0_ffn_b2', 'L0_ffn_wg', 'L0_ffn_bg', 'L0_ffn_w3', 'L0_ffn_b3',
        'L1_attn_Wq', 'L1_attn_Wk', 'L1_attn_Wv', 'L1_attn_Wo', 'L1_ffn_ln_g', 'L1_ffn_ln_b', 'L1_ffn_abel_w',
        'L1_ffn_abel_b', 'L1_ffn_gate_w_moe', 'L1_ffn_gate_b_moe', 'L1_ffn_w1', 'L1_ffn_b1', 'L1_ffn_w2',
        'L1_ffn_b2', 'L1_ffn_gens', 'L1_ffn_mix_w', 'L1_ffn_mix_b']
_OUTS = [((4, 1024, 128), 'float32')]


def kernel(**inputs):
    import numpy as _np
    import concourse.bacc as _bacc
    from concourse import mybir as _mybir
    from concourse.bass_utils import run_bass_kernel_spmd as _run

    nc = _bacc.Bacc("TRN2", target_bir_lowering=False, num_devices=1)
    arrays, args = {}, []
    for name in _INS:
        a = _np.ascontiguousarray(inputs[name])
        arrays[f"in_{name}_dram"] = a
        args.append(nc.dram_tensor(f"in_{name}_dram", a.shape, _mybir.dt.from_np(a.dtype), kind="ExternalInput").ap())
    for i, (shape, dtype) in enumerate(_OUTS):
        dt = _mybir.dt.from_np(_np.dtype(dtype))
        args.append(nc.dram_tensor(f"out_{i}_dram", shape, dt, kind="ExternalOutput").ap())
    two_layers(nc, *args)
    r = _run(nc, [arrays], core_ids=[0])
    got = tuple(r.results[0][f"out_{i}_dram"] for i in range(len(_OUTS)))
    return got[0]
```
